# Optimizing a Trainium2 kernel written in Bass

```python
import numpy as np
import jax
import jax.numpy as jnp

def _softmax(x, axis=-1):
    return jax.nn.softmax(x, axis=axis)

def _gelu(x):
    return jax.nn.gelu(x, approximate=True)

def _silu(x):
    return jax.nn.silu(x)

def _sigmoid(x):
    return jax.nn.sigmoid(x)

def _layernorm(x, axis=-1, eps=1e-05):
    m = jnp.mean(x, axis=axis, keepdims=True)
    v = jnp.var(x, axis=axis, keepdims=True)
    return (x - m) / jnp.sqrt(v + eps)

def _scatter_add(tgt, idx, src, axis=0):
    return tgt.at[idx].add(src)

def _segment_sum(src, seg, n):
    return jax.ops.segment_sum(src, seg, n)
kernel_name = 'mk_gps_d1_gnn_r8_c70a28'

def setup_inputs(seed: int=0):
    np.random.seed(seed)
    _w = jnp.asarray

    def _rec_inputs():
        import jax
        import jax.numpy as jnp
        _gk = jax.random.key(seed)
        x = -0.0001126 + 1 * jax.random.normal(jax.random.fold_in(_gk, 1), (3750, 256), jnp.float32)
        src = jax.random.randint(jax.random.fold_in(_gk, 2), (60000,), 0, 3750, jnp.int32)
        dst = jax.random.randint(jax.random.fold_in(_gk, 3), (60000,), 0, 3750, jnp.int32)
        _o = jnp.argsort(dst, stable=True)
        src = src[_o]
        dst = dst[_o]
        edge_type_8 = jax.random.randint(jax.random.fold_in(_gk, 12), (60000,), 0, 8, jnp.int32)
        return (x, src, dst, edge_type_8)
    x, src, dst, edge_type_8 = _rec_inputs()

    def _L0_gnn_setup():
        import jax, jax.numpy as jnp
        import numpy as np
        N_NODES = 3750
        N_EDGES = 60000
        IN_FEAT = 256
        OUT_FEAT = 256
        N_RELS = 8
        N_HEADS = 4
        HEAD_DIM = OUT_FEAT // N_HEADS
        LEAKY_SLOPE = 0.2
        key = jax.random.key(seed)
        ks = jax.random.split(key, 8)
        inputs = jax.random.normal(ks[0], (N_NODES, IN_FEAT), dtype=jnp.float32)
        conv_weights = jax.random.normal(ks[1], (N_RELS, N_HEADS, IN_FEAT, HEAD_DIM), dtype=jnp.float32) * (1.0 / np.sqrt(IN_FEAT))
        attn_l = jax.random.normal(ks[2], (N_RELS, N_HEADS, HEAD_DIM), dtype=jnp.float32) * 0.1
        attn_r = jax.random.normal(ks[3], (N_RELS, N_HEADS, HEAD_DIM), dtype=jnp.float32) * 0.1
        h_bias = jax.random.normal(ks[4], (OUT_FEAT,), dtype=jnp.float32) * 0.02
        edge_src = jax.random.randint(ks[5], (N_EDGES,), 0, N_NODES, dtype=jnp.int32)
        edge_dst = jax.random.randint(ks[6], (N_EDGES,), 0, N_NODES, dtype=jnp.int32)
        edge_type = jax.random.randint(ks[7], (N_EDGES,), 0, N_RELS, dtype=jnp.int32)
        return {'inputs': inputs, 'conv_weights': conv_weights, 'attn_l': attn_l, 'attn_r': attn_r, 'h_bias': h_bias, 'edge_src': edge_src, 'edge_dst': edge_dst, 'edge_type': edge_type}
    _L0_gnn_all = _L0_gnn_setup()
    _L0_gnn_in = {k: v for k, v in _L0_gnn_all.items() if k in ('conv_weights', 'attn_l', 'attn_r', 'h_bias')}
    del _L0_gnn_all

    def _L0_mix_setup():
        import jax, jax.numpy as jnp
        import numpy as np
        NHEAD = 8
        ATT_EPS = 1e-06
        LN_EPS = 1e-05

        def _layernorm(x, g, b):
            mu = jnp.mean(x, axis=-1, keepdims=True)
            var = jnp.mean(jnp.square(x - mu), axis=-1, keepdims=True)
            return (x - mu) * jax.lax.rsqrt(var + LN_EPS) * g + b
        key = jax.random.key(seed)
        ks = jax.random.split(key, 7)
        N, L, C = (4, 2048, 256)
        s = 1.0 / np.sqrt(C)
        return {'x': jax.random.normal(ks[0], (N, L, C), jnp.float32), 'Wq': jax.random.normal(ks[1], (C, C), jnp.float32) * s, 'Wk': jax.random.normal(ks[2], (C, C), jnp.float32) * s, 'Wv': jax.random.normal(ks[3], (C, C), jnp.float32) * s, 'Wm': jax.random.normal(ks[4], (C, C), jnp.float32) * s, 'W1': jax.random.normal(ks[5], (2 * C, 2 * C), jnp.float32) * (1.0 / np.sqrt(2 * C)), 'W2': jax.random.normal(ks[6], (2 * C, C), jnp.float32) * (1.0 / np.sqrt(2 * C)), 'g1': jnp.ones((C,), jnp.float32), 'b1': jnp.zeros((C,), jnp.float32), 'g2': jnp.ones((C,), jnp.float32), 'b2': jnp.zeros((C,), jnp.float32)}
    _L0_mix_all = _L0_mix_setup()
    _L0_mix_in = {k: v for k, v in _L0_mix_all.items() if k in ('Wq', 'Wk', 'Wv', 'Wm', 'W1', 'W2', 'g1', 'b1', 'g2', 'b2')}
    del _L0_mix_all

    def _L0_ffn_setup():
        import jax, jax.numpy as jnp
        import numpy as np
        NUM_EXPERTS = 8
        TOP_K = 2
        B, S, D = (8, 1024, 256)

        def _moe(tokens, router_w, w1, b1, w2, b2):
            N = tokens.shape[0]
            E = router_w.shape[0]
            logits = tokens.astype(jnp.float32) @ router_w.astype(jnp.float32).T
            probs = jax.nn.softmax(logits, axis=-1)
            rw, re = jax.lax.top_k(probs, TOP_K)
            if TOP_K > 1:
                rw = rw / jnp.maximum(rw.sum(-1, keepdims=True), 1e-12)
            rw = rw.astype(tokens.dtype)
            combine = jnp.zeros((N, E), tokens.dtype).at[jnp.arange(N)[:, None], re].set(rw)
            out = tokens
            for e in range(E):
                h = jax.nn.gelu(tokens @ w1[e] + b1[e], approximate=False)
                y = h @ w2[e] + b2[e]
                out = out + combine[:, e:e + 1] * y
            return out
        key = jax.random.key(seed)
        ks = jax.random.split(key, 4)
        scale = 1.0 / np.sqrt(D).astype(np.float32)
        return {'input_embeddings': jax.random.normal(ks[0], (B, S, D), jnp.float32), 'router_w': jax.random.normal(ks[1], (NUM_EXPERTS, D), jnp.float32) * scale, 'w1': jax.random.normal(ks[2], (NUM_EXPERTS, D, D), jnp.float32) * scale, 'b1': jnp.zeros((NUM_EXPERTS, D), jnp.float32), 'w2': jax.random.normal(ks[3], (NUM_EXPERTS, D, D), jnp.float32) * scale, 'b2': jnp.zeros((NUM_EXPERTS, D), jnp.float32)}
    _L0_ffn_all = _L0_ffn_setup()
    _L0_ffn_in = {k: v for k, v in _L0_ffn_all.items() if k in ('router_w', 'w1', 'b1', 'w2', 'b2')}
    del _L0_ffn_all
    return {'x': x, 'src': src, 'dst': dst, 'edge_type_8': edge_type_8, 'L0_gnn_conv_weights': _L0_gnn_in['conv_weights'], 'L0_gnn_attn_l': _L0_gnn_in['attn_l'], 'L0_gnn_attn_r': _L0_gnn_in['attn_r'], 'L0_gnn_h_bias': _L0_gnn_in['h_bias'], 'L0_mix_Wq': _L0_mix_in['Wq'], 'L0_mix_Wk': _L0_mix_in['Wk'], 'L0_mix_Wv': _L0_mix_in['Wv'], 'L0_mix_Wm': _L0_mix_in['Wm'], 'L0_mix_W1': _L0_mix_in['W1'], 'L0_mix_W2': _L0_mix_in['W2'], 'L0_mix_g1': _L0_mix_in['g1'], 'L0_mix_b1': _L0_mix_in['b1'], 'L0_mix_g2': _L0_mix_in['g2'], 'L0_mix_b2': _L0_mix_in['b2'], 'L0_ffn_router_w': _L0_ffn_in['router_w'], 'L0_ffn_w1': _L0_ffn_in['w1'], 'L0_ffn_b1': _L0_ffn_in['b1'], 'L0_ffn_w2': _L0_ffn_in['w2'], 'L0_ffn_b2': _L0_ffn_in['b2']}

def reference(x, src, dst, edge_type_8, L0_gnn_conv_weights, L0_gnn_attn_l, L0_gnn_attn_r, L0_gnn_h_bias, L0_mix_Wq, L0_mix_Wk, L0_mix_Wv, L0_mix_Wm, L0_mix_W1, L0_mix_W2, L0_mix_g1, L0_mix_b1, L0_mix_g2, L0_mix_b2, L0_ffn_router_w, L0_ffn_w1, L0_ffn_b1, L0_ffn_w2, L0_ffn_b2):
    import jax
    import jax.numpy as jnp

    def _L0_gnn_ref(inputs, conv_weights, attn_l, attn_r, h_bias, edge_src, edge_dst, edge_type):
        import jax, jax.numpy as jnp
        import numpy as np
        N_NODES = 3750
        N_EDGES = 60000
        IN_FEAT = 256
        OUT_FEAT = 256
        N_RELS = 8
        N_HEADS = 4
        HEAD_DIM = OUT_FEAT // N_HEADS
        LEAKY_SLOPE = 0.2
        feat_all = jnp.einsum('ni,rhid->rnhd', inputs, conv_weights)
        feat_src_e = feat_all[edge_type, edge_src]
        feat_dst_e = feat_all[edge_type, edge_dst]
        el = jnp.sum(feat_src_e * attn_l[edge_type], axis=-1)
        er = jnp.sum(feat_dst_e * attn_r[edge_type], axis=-1)
        e = jax.nn.leaky_relu(el + er, negative_slope=LEAKY_SLOPE)
        m = jax.ops.segment_max(e, edge_dst, num_segments=N_NODES)
        ex = jnp.exp(e - m[edge_dst])
        denom = jax.ops.segment_sum(ex, edge_dst, num_segments=N_NODES)
        alpha = ex / denom[edge_dst]
        h = jax.ops.segment_sum(alpha[..., None] * feat_src_e, edge_dst, num_segments=N_NODES)
        h = h.reshape(N_NODES, OUT_FEAT) + h_bias
        return h

    def _L0_mix_ref(x, Wq, Wk, Wv, Wm, W1, W2, g1, b1, g2, b2):
        import jax, jax.numpy as jnp
        import numpy as np
        NHEAD = 8
        ATT_EPS = 1e-06
        LN_EPS = 1e-05

        def _layernorm(x, g, b):
            mu = jnp.mean(x, axis=-1, keepdims=True)
            var = jnp.mean(jnp.square(x - mu), axis=-1, keepdims=True)
            return (x - mu) * jax.lax.rsqrt(var + LN_EPS) * g + b
        N, L, C = x.shape
        H = NHEAD
        D = C // H
        q = (x @ Wq).reshape(N, L, H, D)
        k = (x @ Wk).reshape(N, L, H, D)
        v = (x @ Wv).reshape(N, L, H, D)
        Q = jax.nn.elu(q) + 1.0
        K = jax.nn.elu(k) + 1.0
        v = v / L
        KV = jnp.einsum('nshd,nshv->nhdv', K, v)
        Z = 1.0 / (jnp.einsum('nlhd,nhd->nlh', Q, K.sum(axis=1)) + ATT_EPS)
        msg = jnp.einsum('nlhd,nhdv,nlh->nlhv', Q, KV, Z) * L
        msg = msg.reshape(N, L, C) @ Wm
        msg = _layernorm(msg, g1, b1)
        h = jnp.concatenate([x, msg], axis=-1) @ W1
        h = jax.nn.relu(h) @ W2
        msg = _layernorm(h, g2, b2)
        return x + msg

    def _L0_ffn_ref(input_embeddings, router_w, w1, b1, w2, b2):
        import jax, jax.numpy as jnp
        import numpy as np
        NUM_EXPERTS = 8
        TOP_K = 2
        B, S, D = (8, 1024, 256)

        def _moe(tokens, router_w, w1, b1, w2, b2):
            N = tokens.shape[0]
            E = router_w.shape[0]
            logits = tokens.astype(jnp.float32) @ router_w.astype(jnp.float32).T
            probs = jax.nn.softmax(logits, axis=-1)
            rw, re = jax.lax.top_k(probs, TOP_K)
            if TOP_K > 1:
                rw = rw / jnp.maximum(rw.sum(-1, keepdims=True), 1e-12)
            rw = rw.astype(tokens.dtype)
            combine = jnp.zeros((N, E), tokens.dtype).at[jnp.arange(N)[:, None], re].set(rw)
            out = tokens
            for e in range(E):
                h = jax.nn.gelu(tokens @ w1[e] + b1[e], approximate=False)
                y = h @ w2[e] + b2[e]
                out = out + combine[:, e:e + 1] * y
            return out
        b, s, d = input_embeddings.shape
        tokens = input_embeddings.reshape(b * s, d)
        return _moe(tokens, router_w, w1, b1, w2, b2).reshape(b, s, d)
    xn = _layernorm(x, axis=-1)
    x = x + _L0_gnn_ref(xn, L0_gnn_conv_weights, L0_gnn_attn_l, L0_gnn_attn_r, L0_gnn_h_bias, src, dst, edge_type_8) + _L0_mix_ref(xn[None], L0_mix_Wq, L0_mix_Wk, L0_mix_Wv, L0_mix_Wm, L0_mix_W1, L0_mix_W2, L0_mix_g1, L0_mix_b1, L0_mix_g2, L0_mix_b2)[0]
    x = x + _L0_ffn_ref(_layernorm(x, axis=-1)[None], L0_ffn_router_w, L0_ffn_w1, L0_ffn_b1, L0_ffn_w2, L0_ffn_b2)[0]
    return x

_drawn_inputs = setup_inputs


def setup_inputs(seed=0):
    import zlib

    import numpy as np

    out = dict(_drawn_inputs(seed))
    spreads = {'L0_mix_g1': (1.0, 0.2),
     'L0_mix_b1': (0.0, 0.1),
     'L0_mix_g2': (1.0, 0.2),
     'L0_mix_b2': (0.0, 0.1),
     'L0_ffn_b1': (0.0, 0.519),
     'L0_ffn_b2': (0.0, 0.355)}
    factors = {'L0_gnn_h_bias': 4.295}
    for name, (base, spread) in spreads.items():
        noise = np.random.default_rng([zlib.crc32(name.encode()), seed]).standard_normal(out[name].shape)
        drawn = base * np.exp(spread * noise) if base else spread * noise
        out[name] = jnp.asarray(drawn.astype(out[name].dtype))
    for name, factor in factors.items():
        out[name] = (out[name] * factor).astype(out[name].dtype)
    return out
```

```python
from contextlib import ExitStack

import concourse.bass as bass
from concourse import mybir

ALU = mybir.AluOpType
ACT = mybir.ActivationFunctionType
AX = mybir.AxisListType.X
F32 = mybir.dt.float32
I32 = mybir.dt.int32
ds = bass.ds

N, D, R, H, E = 3750, 256, 8, 4, 60000
HD = D // H
RF = R * D
TN = 125
NT = N // TN
SJ = 3
SN = SJ * TN
NS = N // SN
GE, GJ = 512, 4
NG = -(-E // GE)
EP = NG * GE
EC = EP // 128
NSTEP = NG + NT - 1
NX = 8
KC = D // 128
AH = 32
LN_EPS, ATT_EPS = 1e-5, 1e-6
BIG = 1e38
W = D + H
U = 3
GC = 4
assert N % SN == 0 and EC % (2 * GC) == 0 and NSTEP % U == 0


class Link:

    def __init__(self, eng, sem):
        self.eng, self.sem, self.base, self.count = eng, sem, 0, 0

    def __call__(self, ins):
        ins.then_inc(self.sem, 1)
        self.count += 1
        return ins

    def wait(self):
        hold(self.eng, self.sem, self.base + self.count)

    def loop(self, trip, per):
        self.per, self.outer = per, self.count
        self.base, self.count = trip * per + self.count, 0

    def close(self, trips):
        assert self.count == self.per, (self.count, self.per)
        self.base, self.count = 0, self.outer + trips * self.per


def hold(eng, sem, value):
    eng.wait_ge(sem, value)
    if not isinstance(value, int):
        eng.nop(nofuse=True)


def build(nc, x, dst_ext, src_pad, type_pad, conv, attn_l, attn_r, h_bias, Wq, Wk, Wv, Wm, W1, W2,
          g1, b1, g2, b2, router, mw1, mb1, mw2, mb2, out, feat_t, l_t, r_t, rec_t):
    with ExitStack() as ctx:
        def sb(name, shape, dt=F32):
            return ctx.enter_context(nc.sbuf_tensor(name, shape, dt))

        def sem(name):
            return ctx.enter_context(nc.semaphore(name))

        psum = ctx.enter_context(nc.psum_tensor("psum", [128, 8, 512], F32))
        bank = [psum[:, i, :] for i in range(8)]

        node_sum = sb("node_sum", [TN, NT, D])
        arena_n = sb("arena_n", [128, NT * W])
        xnT = arena_n[:, 0:KC * N].rearrange("p (c n) -> p c n", c=KC)
        edge_sum = arena_n[0:TN, :].rearrange("p (t w) -> p t w", w=W)
        arena_w = sb("arena_w", [128, KC * RF])
        conv_w = arena_w[:, :].rearrange("p (c w) -> p c w", c=KC)
        mw1_s = arena_w[:, :].rearrange("p (e c w) -> p e c w", e=NX, c=KC)
        arena_f = sb("arena_f", [128, 2 * RF])
        attn_b = arena_f[:, 0:RF]
        prod = arena_f[:, RF:2 * RF]
        feat_s = arena_f[0:TN, :].rearrange("p (u w) -> p u w", u=2)
        ring = arena_f[:, 0:U * GJ * W].rearrange("p (u j w) -> p u j w", u=U, j=GJ)
        mw2_s = sb("mw2_s", [128, NX, KC, D])
        wqm = sb("wqm", [128, 2, KC, D])
        wkv = sb("wkv", [128, KC, 2 * D])
        w1_s = sb("w1_s", [128, 4, 2 * D])
        w2_s = sb("w2_s", [128, 4, D])
        w_lr = sb("w_lr", [128, KC, 2 * R * H])
        rw_s = sb("rw_s", [NX, D])
        rwT = sb("rwT", [128, KC, NX])
        colv = sb("colv", [128, 2 * KC])
        hb_b2 = sb("hb_b2", [TN, 2, D])
        g2_b = sb("g2_b", [TN, D])
        mb1_s = sb("mb1_s", [128, NX, KC])
        mb2_s = sb("mb2_s", [NX, D])
        ident = sb("ident", [128, 128])
        mask = sb("mask", [128, 128])
        zeros = sb("zeros", [128, 132])
        stats = sb("stats", [TN, NT, 6])
        mv = sb("mv", [TN, NT, 2])
        rstd = sb("rstd", [TN, NT, 1])
        xs = sb("xs", [TN, 2, D])
        xt = sb("xt", [128, 2, KC, TN])
        src_a = sb("src_a", [128, EC], I32)
        typ_a = sb("typ_a", [128, EC], I32)
        idx_r = sb("idx_r", [128, EC], I32)
        rec = sb("rec", [128, EC, 2 + H])
        rec_idx = rec[:, :, 0].bitcast(I32)
        new_run = sb("new_run", [128, EC])
        end_run = sb("end_run", [128, EC])
        run_max = sb("run_max", [128, EC, H])
        dst3 = run_max[:, :, :].rearrange("p k h -> p (k h)")[:, 0:3 * EC].rearrange("p (m k) -> p m k", m=3).bitcast(I32)
        idx_st = sb("idx_st", [128, 2, 2, GC], I32)
        lr_ring = sb("lr_ring", [128, 2, 2, GC, H])
        tailf = sb("tailf", [128, 2, H])
        rowf = sb("rowf", [H, 2, 128])
        carry = sb("carry", [H, 130])
        cin = sb("cin", [128, H])
        qt = sb("qt", [128, 3, KC, SN])
        arena_q = qt[:, :, :, :].rearrange("p a c n -> p (a c n)")
        mk, ek, kt = (arena_q[0:TN, n * 2 * D:(n + 1) * 2 * D].rearrange("p (u d) -> p u d", u=2) for n in range(3))
        vt = arena_q[0:TN, 6 * D:6 * D + 4 * 129].rearrange("p (u c n) -> p u c n", u=2, c=KC)
        onehot = arena_q[:, 0:U * GJ * TN].rearrange("p (u j n) -> p u j n", u=U, j=GJ)
        kv_m = sb("kv_m", [128, KC, 128])
        ks_m = sb("ks_m", [128, KC, 128])
        msgT = sb("msgT", [128, KC, SN])
        ms = sb("ms", [TN, SJ, D])
        arena_h = sb("arena_h", [128, 3 * KC * SN])
        hT = arena_h[:, 0:2 * KC * SN].rearrange("p (c n) -> p c n", c=2 * KC)
        msT = arena_h[:, 2 * KC * SN:].rearrange("p (c n) -> p c n", c=KC)
        lr_s = arena_h[0:TN, 0:NT * 2 * R * H].rearrange("p (t w) -> p t w", t=NT)
        st2 = sb("st2", [TN, SJ, 6])
        mv2 = sb("mv2", [TN, SJ, 2])
        sd2 = sb("sd2", [TN, SJ, 1])
        last_i = sb("last_i", [NG, 1], I32)
        last_f = sb("last_f", [NG, 2])
        thr = sb("thr", [NG, NT - 1])
        path_cmp = sb("path_cmp", [NG, 2, NSTEP])
        ones = sb("ones", [128, 128])
        path_f = sb("path_f", [128, 3, NSTEP])
        path_i = sb("path_i", [1, 2, NSTEP + 1], I32)
        rec_b = sb("rec_b", [128, U, GJ, 2 + H])
        dst_rel = sb("dst_rel", [128, U, GJ])
        iota_n = sb("iota_n", [128, 128])
        eps_t = sb("eps_t", [128, 1])
        tmp_t = sb("tmp_t", [TN, 2, NT])
        lg_s = sb("lg_s", [TN, 4, SJ, NX])
        rt = sb("rt", [TN, 4, SJ])
        top = sb("top", [TN, SJ, 8])
        top_i = sb("top_i", [TN, SJ, 8], mybir.dt.uint32)
        top_f = sb("top_f", [TN, SJ, 8])
        combT = sb("combT", [NX, SN])

        s = {k: sem("s_" + k) for k in (
            "x wts conv attn edges last moe1 consts dve act pool stats std xs tp lr_x xt lr lr_ev lr_out "
            "wlr f_xt f_kv f_pe01 f_pe f_act f_dve f_out stored kvm mk ek kt vt kv_ready q q_mn q_ex q_t nd msg m ms_var "
            "ms_sd ms tpm msT h1 h_act h2 h2_var h2_sd h2_done idx gath0 gath1 gath_use a_tail a_tp a_row a_tpb "
            "a_sub a_ex rec_out path_c path_p path_r rec_in0 rec_in1 rec_in2 row_in0 row_in1 row_in2 slot oh "
            "agg_ev rw_tp rw_ev x2_var x2_sd x2n x2tp x2T lg lg_x lg_ex cmb cmb_tp cmT bias bias_ev up hid down acc outd").split()}
        rec_in = [s["rec_in0"], s["rec_in1"], s["rec_in2"]]
        row_in = [s["row_in0"], s["row_in1"], s["row_in2"]]
        gath = [s["gath0"], s["gath1"]]

        x_v = x.rearrange("(t p) d -> p t d", p=TN)
        out_v = out.rearrange("(t p) d -> p t d", p=TN)
        feat_v = feat_t.rearrange("(t p) w -> p t w", p=TN)
        feat_rows = feat_t.rearrange("n (r d) -> (n r) d", r=R)
        l_rows = l_t.rearrange("n (r h) -> (n r) h", h=H)
        r_rows = r_t.rearrange("n (r h) -> (n r) h", h=H)
        rec_g = rec_t.rearrange("(g q j) w -> g q (j w)", g=NG, j=GJ)
        logits = rec[:, :, 2:2 + H]
        y_at = [[bank[4][0:TN, 0:D], bank[4][0:TN, D:2 * D], bank[5][0:TN, 0:D]],
                [bank[6][0:TN, 0:D], bank[6][0:TN, D:2 * D], bank[7][0:TN, 0:D]]]
        bias_at = [bank[6][0:TN, 0:D], bank[6][0:TN, D:2 * D], bank[5][0:TN, D:2 * D]]
        WTS = 16 * 15

        def bcast(v, parts):
            return v.rearrange("(a n) -> a n", a=1).broadcast_to([parts, v.shape[0]])

        block = ctx.enter_context(nc.Block())

        @block.sync
        def _(sp):
            for c in range(KC):
                sp.dma_start(conv_w[:, c, :].rearrange("p (g d) -> p g d", d=HD),
                             conv.rearrange("r h i d -> i (r h) d")[c * 128:(c + 1) * 128]).then_inc(s["conv"], 16)
            sp.dma_start(attn_b, bcast(attn_l.rearrange("r h d -> (r h d)"), 128)).then_inc(s["attn"], 16)
            sp.dma_start(node_sum[:, :, :], x_v).then_inc(s["x"], 16)
            for m in range(3):
                sp.dma_start(dst3[:, m, :], dst_ext[m:m + EP].rearrange("(p k) -> p k", p=128)).then_inc(s["edges"], 16)
            sp.dma_start(src_a[:, :], src_pad.rearrange("(p k) -> p k", p=128)).then_inc(s["edges"], 16)
            sp.dma_start(typ_a[:, :], type_pad.rearrange("(p k) -> p k", p=128)).then_inc(s["edges"], 16)
            for n, w in ((0, Wq), (1, Wm)):
                sp.dma_start(wqm[:, n], w.rearrange("(c p) n -> p c n", p=128)).then_inc(s["wts"], 16)
            for n, w in ((0, Wk), (1, Wv)):
                sp.dma_start(wkv[:, :, n * D:(n + 1) * D], w.rearrange("(c p) n -> p c n", p=128)).then_inc(s["wts"], 16)
            sp.dma_start(w1_s[:, :, :], W1.rearrange("(c p) n -> p c n", p=128)).then_inc(s["wts"], 16)
            sp.dma_start(w2_s[:, :, :], W2.rearrange("(c p) n -> p c n", p=128)).then_inc(s["wts"], 16)
            sp.dma_start(rw_s[:, :], router).then_inc(s["wts"], 16)
            sp.dma_start(hb_b2[:, 0, :], bcast(h_bias, TN)).then_inc(s["wts"], 16)
            sp.dma_start(hb_b2[:, 1, :], bcast(b2, TN)).then_inc(s["wts"], 16)
            sp.dma_start(g2_b[:, :], bcast(g2, TN)).then_inc(s["wts"], 16)
            with nc.allow_non_contiguous_dma(reason="vectors laid out by feature on the partitions"):
                sp.dma_start(last_i[:, :], dst_ext[1:1 + EP].rearrange("(g k) -> g k", g=NG)[:, GE - 1:GE]).then_inc(s["last"], 16)
                for n, v in ((0, g1), (1, b1)):
                    sp.dma_start(colv[:, n * KC:(n + 1) * KC], v.rearrange("(c p) -> p c", p=128)).then_inc(s["wts"], 16)
                sp.dma_start(mb1_s[:, :, :].rearrange("p e c -> p (e c)"),
                             mb1.rearrange("e (c p) -> p (e c)", p=128)).then_inc(s["wts"], 16)
            sp.dma_start(mb2_s[:, :], mb2).then_inc(s["wts"], 16)
            sp.dma_start(mw2_s[:, :, :, :].rearrange("p e c n -> p (e c) n"),
                         mw2.rearrange("e (c p) n -> p (e c) n", p=128)).then_inc(s["wts"], 16)
            sp.wait_ge(s["wlr"], 1)
            sp.dma_start(attn_b, bcast(attn_r.rearrange("r h d -> (r h d)"), 128)).then_inc(s["attn"], 16)
            sp.wait_ge(s["lr_ev"], 1)
            sp.dma_start(l_t.rearrange("(t p) w -> p t w", p=TN), lr_s[:, :, 0:R * H]).then_inc(s["lr_out"], 16)
            sp.dma_start(r_t.rearrange("(t p) w -> p t w", p=TN), lr_s[:, :, R * H:2 * R * H]).then_inc(s["lr_out"], 16)
            sp.sem_inc(s["stored"], 2)
            with sp.Fori(0, NT // 2) as i:
                for u in range(2):
                    t = 2 * i + u
                    hold(sp, s["f_act"], t + 2)
                    hold(sp, s["f_dve"], t + 2)
                    sp.dma_start(feat_v[:, ds(t, 1), :].rearrange("p t w -> p (t w)"), feat_s[:, u, :]).then_inc(s["f_out"], 16)
                    hold(sp, s["f_out"], 16 * (t + 1))
                    sp.sem_inc(s["stored"], 1)
            sp.wait_ge(s["f_pe"], NT + 2)
            sp.dma_start(mw1_s.rearrange("p e c n -> p (e c) n"), mw1.rearrange("e (c p) n -> p (e c) n", p=128)).then_inc(s["moe1"], 16)
            sp.wait_ge(s["a_ex"], 1)
            sp.dma_start(rec_t.rearrange("(p k) w -> p (k w)", p=128), rec[:, :, :].rearrange("p k w -> p (k w)")).then_inc(s["rec_out"], 16)
            sp.wait_ge(s["rec_out"], 16)
            sp.wait_ge(s["path_r"], 1)
            with sp.Fori(0, NSTEP // U) as i:
                for u in range(U):
                    hold(sp, s["oh"], U * i + u + 1)
                    g = sp.value_load(path_i[0:1, 0, ds(U * i + u, 1)], min_val=0, max_val=NG - 1)
                    sp.dma_start(rec_b[:, u].rearrange("p j w -> p (j w)"), rec_g[ds(g, 1)].rearrange("g q w -> (g q) w")).then_inc(rec_in[u], 16)
            with sp.Fori(0, NS) as k:
                hold(sp, s["acc"], NX * k + NX + 2)
                sp.dma_start(out_v[:, ds(k * SJ, SJ), :], node_sum[:, ds(k * SJ, SJ), :]).then_inc(s["outd"], 16)
            sp.wait_ge(s["outd"], 16 * NS)

        @block.gpsimd
        def _(pool):
            link = Link(pool, s["pool"])
            link(pool.memset(ident[:, :], 0.0))
            link(pool.memset(ones[:, :], 1.0))
            link(pool.memset(zeros[:, :], 0.0))
            link(pool.memset(eps_t[:, :], LN_EPS))
            link(pool.memset(vt[:, :, :, 128:129], 1.0))
            for tile, step, base, mul in ((iota_n[:, :], 1, 0, 0), (thr[:, :], TN, TN, 0), (path_cmp[:, 0, :], 1, 0, 0),
                                          (path_f[:, 0, :], 1, 0, 0), (last_f[:, 0:1], 0, 1, 1)):
                link(pool.iota(tile, pattern=[[step, tile.shape[1]]], base=base, channel_multiplier=mul,
                               allow_small_or_imprecise_dtypes=True))
            link.wait()
            link(pool.affine_select(out=ident[:, :], in_=ident[:, :], compare_op=ALU.not_equal, fill=1.0,
                                    base=0, pattern=[[-1, 128]], channel_multiplier=1))
            link(pool.affine_select(out=mask[:, :], in_=ones[:, :], compare_op=ALU.is_ge, fill=0.0,
                                    base=0, pattern=[[-AH, 128 // AH], [0, AH]], channel_multiplier=1))
            link.wait()
            pool.affine_select(out=mask[:, :], in_=mask[:, :], compare_op=ALU.is_ge, fill=0.0,
                               base=AH - 1, pattern=[[AH, 128 // AH], [0, AH]], channel_multiplier=-1).then_inc(s["consts"], 1)

            pool.wait_ge(s["idx"], 1)
            pool.wait_ge(s["lr_out"], 32)

            def ask(u, col):
                link(pool.tensor_copy(idx_st[:, u, 0, :], rec_idx[:, ds(col, GC)]))
                link(pool.tensor_copy(idx_st[:, u, 1, :], idx_r[:, ds(col, GC)]))
                link.wait()
                for n, rows in ((0, l_rows), (1, r_rows)):
                    for c in range(GC):
                        pool.indirect_dma_start(out=lr_ring[:, u, n, c, :], out_offset=None, in_=rows,
                                                in_offset=bass.IndirectOffsetOnAxis(ap=idx_st[:, u, n, c:c + 1], axis=0),
                                                ).then_inc(gath[u], 16)

            def take(u, col, times):
                hold(pool, gath[u], times * (2 * GC * 16))
                link(pool.tensor_tensor(logits[:, ds(col, GC), :], lr_ring[:, u, 0], lr_ring[:, u, 1], ALU.add))
                link.wait()

            turns = EC // (2 * GC)
            ask(0, 0)
            with pool.Fori(0, turns - 1) as i:
                link.loop(i, 6)
                ask(1, 2 * GC * i + GC)
                take(0, 2 * GC * i, i + 1)
                ask(0, 2 * GC * i + 2 * GC)
                take(1, 2 * GC * i + GC, i + 1)
            link.close(turns - 1)
            ask(1, (2 * turns - 1) * GC)
            take(0, (2 * turns - 2) * GC, turns)
            take(1, (2 * turns - 1) * GC, turns)
            pool.drain().then_inc(s["gath_use"], 1)

            pool.wait_ge(s["f_out"], 16 * NT)
            with pool.Fori(0, NSTEP // U) as i:
                for u in range(U):
                    hold(pool, rec_in[u], 16 * i + 16)
                    hold(pool, s["slot"], U * i + u + 1)
                    for j in range(GJ):
                        pool.indirect_dma_start(out=ring[:, u, j, 0:D], out_offset=None, in_=feat_rows,
                                                in_offset=bass.IndirectOffsetOnAxis(ap=rec_b[:, u, j, 0:1].bitcast(I32), axis=0),
                                                ).then_inc(row_in[u], 16)

        @block.scalar
        def _(act):
            act.wait_ge(s["stats"], 1)
            act.wait_ge(s["consts"], 1)
            act.activation(rstd[:, :, 0], mv[:, :, 1], ACT.Sqrt, bias=eps_t[0:TN, :]).then_inc(s["std"], 1)
            act.sem_inc(s["lr_x"], 2)
            with act.Fori(0, NT // 2) as i:
                for u in range(2):
                    t = 2 * i + u
                    hold(act, s["tp"], t + 3)
                    hold(act, s["lr"], t + 1)
                    v = bank[u][:, 0:256].rearrange("p (c n) -> p c n", c=KC)[:, :, 0:TN]
                    act.activation(xt[:, u], v, ACT.Copy).then_inc(s["xt"], 1)
                    act.activation(xnT[:, :, ds(t * TN, TN)], v, ACT.Copy).then_inc(s["lr_x"], 1)
            act.wait_ge(s["lr_x"], NT + 2)
            act.wait_ge(s["lr"], NT + 2)
            act.sem_inc(s["vt"], 2)
            act.sem_inc(s["f_act"], 1)
            with act.Fori(0, NT // 2) as i:
                for u in range(2):
                    t = 2 * i + u
                    hold(act, s["f_pe"], t + 1)
                    act.activation(xt[:, u], xnT[:, :, ds(t * TN, TN)], ACT.Copy).then_inc(s["f_xt"], 1)
                    hold(act, s["mk"], t + 1)
                    act.activation(ek[:, u, :], mk[:, u, :], ACT.Exp).then_inc(s["ek"], 1)
                    hold(act, s["kt"], t + 3)
                    hold(act, s["kvm"], t + 1)
                    act.activation(vt[:, u, :, 0:128], bank[4 + u][0:TN, D:2 * D].rearrange("p (c n) -> p c n", c=KC),
                                   ACT.Copy).then_inc(s["vt"], 1)
                    hold(act, s["f_pe01"], t + 1)
                    hold(act, s["stored"], t + 1)
                    act.activation(feat_s[:, u, 0:1024].rearrange("p (n w) -> p n w", n=2), psum[0:TN, 0:2, :],
                                   ACT.Copy).then_inc(s["f_act"], 1)
            act.wait_ge(s["lr_out"], 32)
            act.sem_inc(s["h_act"], 1)
            with act.Fori(0, NS) as k:
                hold(act, s["q_mn"], k + 1)
                act.activation(qt[:, 1], qt[:, 0], ACT.Exp).then_inc(s["q_ex"], 1)
                hold(act, s["ms_var"], k + 1)
                act.activation(sd2[:, :, 0], mv2[:, :, 1], ACT.Sqrt, bias=eps_t[0:TN, :]).then_inc(s["ms_sd"], 1)
                hold(act, s["tpm"], k + 1)
                for c in range(KC):
                    act.activation(msT[:, c, :], bank[6 + c][:, 0:SN], ACT.Identity, scale=colv[:, c:c + 1],
                                   bias=colv[:, KC + c:KC + c + 1]).then_inc(s["msT"], 1)
                hold(act, s["h1"], k + 1)
                act.activation(hT[:, :, :], psum[:, 0:4, 0:SN], ACT.Relu).then_inc(s["h_act"], 1)
                hold(act, s["h2_var"], k + 1)
                act.activation(sd2[:, :, 0], mv2[:, :, 1], ACT.Sqrt, bias=eps_t[0:TN, :]).then_inc(s["h2_sd"], 1)
            act.wait_ge(s["a_sub"], 1)
            act.activation(logits, run_max[:, :, :], ACT.Exp).then_inc(s["a_ex"], 1)
            act.sem_inc(s["hid"], 2)
            with act.Fori(0, NS) as k:
                hold(act, s["x2_var"], k + 1)
                act.activation(sd2[:, :, 0], mv2[:, :, 1], ACT.Sqrt, bias=eps_t[0:TN, :]).then_inc(s["x2_sd"], 1)
                hold(act, s["x2tp"], k + 1)
                act.activation(msT[:, :, :], psum[:, 0:2, 0:SN], ACT.Copy).then_inc(s["x2T"], 1)
                hold(act, s["lg_x"], k + 1)
                act.activation(lg_s[:, 1], lg_s[:, 0], ACT.Exp).then_inc(s["lg_ex"], 1)
                for e in range(NX):
                    hold(act, s["up"], NX * k + e + 1)
                    hold(act, s["down"], NX * k + e + 1)
                    h0 = (e % 2) * KC
                    for c in range(KC):
                        ins = act.activation(hT[:, h0 + c, :], bank[h0 + c][:, 0:SN], ACT.Gelu, bias=mb1_s[:, e, c:c + 1])
                    ins.then_inc(s["hid"], 1)

        @block.vector
        def _(dve):
            link = Link(dve, s["dve"])

            def layer_stats():
                link.wait()
                for j in range(SJ):
                    ins = dve.bn_aggr(mv2[:, j, :], st2[:, j, :])
                return ins

            dve.wait_ge(s["edges"], 16 * 5)
            link(dve.scalar_tensor_tensor(out=rec_idx, in0=src_a[:, :], scalar=float(R), in1=typ_a[:, :], op0=ALU.mult, op1=ALU.add))
            link(dve.tensor_copy(rec[:, :, 1], dst3[:, 1, :]))
            link(dve.tensor_scalar(idx_r[:, :], dst3[:, 1, :], float(N - 1), float(R), ALU.min, ALU.mult))
            link(dve.tensor_tensor(new_run[:, :], dst3[:, 0, :], dst3[:, 1, :], ALU.not_equal))
            link(dve.tensor_tensor(end_run[:, :], dst3[:, 1, :], dst3[:, 2, :], ALU.not_equal))
            link.wait()
            link(dve.tensor_scalar(new_run[:, :], new_run[:, :], -BIG, None, ALU.mult))
            link(dve.tensor_scalar(end_run[:, :], end_run[:, :], -BIG, None, ALU.mult))
            dve.tensor_tensor(idx_r[:, :], idx_r[:, :], typ_a[:, :], ALU.add).then_inc(s["idx"], 1)
            dve.wait_ge(s["last"], 16)
            dve.wait_ge(s["consts"], 1)
            link(dve.tensor_copy(last_f[:, 1:2], last_i[:, :]))
            link.wait()
            link(dve.tensor_scalar(thr[:, :], thr[:, :], last_f[:, 1:2], None, ALU.is_le))
            link.wait()
            link(dve.tensor_reduce(last_f[:, 1:2], thr[:, :], AX, ALU.add))
            link.wait()
            link(dve.tensor_tensor(last_f[:, 1:2], last_f[:, 1:2], last_f[:, 0:1], ALU.add))
            link.wait()
            dve.tensor_scalar(path_cmp[:, 1, :], path_cmp[:, 0, :], last_f[:, 1:2], None, ALU.is_ge).then_inc(s["path_c"], 1)
            dve.wait_ge(s["rw_tp"], 1)
            dve.tensor_copy(rwT[:, :, :], bank[7][:, 0:KC * NX].rearrange("p (c n) -> p c n", c=KC)).then_inc(s["rw_ev"], 1)
            dve.wait_ge(s["path_p"], 1)
            link(dve.tensor_copy(path_f[:, 1, :], bank[6][:, 0:NSTEP]))
            link.wait()
            link(dve.tensor_tensor(path_f[:, 2, :], path_f[:, 0, :], path_f[:, 1, :], ALU.subtract))
            link(dve.tensor_copy(path_i[0:1, 0, 0:NSTEP], path_f[0:1, 1, :]))
            link(dve.memset(path_i[0:1, 1, :], 0))
            link.wait()
            link(dve.tensor_copy(path_i[0:1, 1, 1:NSTEP + 1], path_f[0:1, 2, :]))
            link.wait()
            dve.tensor_scalar(path_f[:, 2, :], path_f[:, 2, :], float(TN), None, ALU.mult).then_inc(s["path_r"], 1)

            for side in range(2):
                dve.wait_ge(s["conv"], 16 * KC)
                dve.wait_ge(s["attn"], 16 * (side + 1))
                for c in range(KC):
                    link(dve.tensor_tensor(prod, conv_w[:, c, :], attn_b, ALU.mult))
                    link.wait()
                    ins = dve.tensor_reduce(w_lr[:, c, side * R * H:(side + 1) * R * H],
                                            prod.rearrange("p (g d) -> p g d", d=HD), AX, ALU.add)
                    if c < KC - 1:
                        link(ins)
                        link.wait()
                ins.then_inc(s["wlr"], 1)

            dve.wait_ge(s["x"], 16)
            with dve.Fori(0, NT // 2) as i:
                link.loop(i, 2)
                for u in range(2):
                    link(dve.bn_stats(stats[:, ds(2 * i + u, 1), :].rearrange("p t w -> p (t w)"),
                                      node_sum[:, ds(2 * i + u, 1), :].rearrange("p t w -> p (t w)")))
            link.close(NT // 2)
            link.wait()
            link(dve.tensor_tensor(mv[:, :, 0], stats[:, :, 1], stats[:, :, 4], ALU.add))
            link(dve.tensor_tensor(tmp_t[:, 0, :], stats[:, :, 1], stats[:, :, 4], ALU.subtract))
            link(dve.tensor_tensor(tmp_t[:, 1, :], stats[:, :, 2], stats[:, :, 5], ALU.add))
            link.wait()
            link(dve.tensor_scalar(mv[:, :, 0], mv[:, :, 0], 0.5, None, ALU.mult))
            link(dve.tensor_tensor(tmp_t[:, 0, :], tmp_t[:, 0, :], tmp_t[:, 0, :], ALU.mult))
            link(dve.tensor_scalar(tmp_t[:, 1, :], tmp_t[:, 1, :], 1.0 / D, None, ALU.mult))
            link.wait()
            dve.scalar_tensor_tensor(out=mv[:, :, 1], in0=tmp_t[:, 0, :], scalar=0.25, in1=tmp_t[:, 1, :],
                                     op0=ALU.mult, op1=ALU.add).then_inc(s["stats"], 1)
            dve.wait_ge(s["wts"], WTS)
            link(dve.tensor_tensor(hb_b2[:, 0, :], hb_b2[:, 0, :], hb_b2[:, 1, :], ALU.add))
            dve.wait_ge(s["std"], 1)
            link(dve.reciprocal(rstd[:, :, 0], rstd[:, :, 0]))
            link.wait()
            with dve.Fori(0, NT // 2) as i:
                link.loop(i, 4)
                for u in range(2):
                    t = 2 * i + u
                    row = node_sum[:, ds(t, 1), :].rearrange("p t w -> p (t w)")
                    hold(dve, s["tp"], t + 1)
                    dve.tensor_scalar(xs[:, u, :], row, mv[:, ds(t, 1), 0], rstd[:, ds(t, 1), 0],
                                      ALU.subtract, ALU.mult).then_inc(s["xs"], 1)
                    hold(dve, s["xs"], t + 1)
                    link(dve.tensor_tensor(row, row, xs[:, u, :], ALU.add))
                    link.wait()
                    link(dve.tensor_tensor(row, row, hb_b2[:, 0, :], ALU.add))
            link.close(NT // 2)
            dve.wait_ge(s["lr"], NT + 2)
            dve.tensor_copy(lr_s[:, :, :].rearrange("p t w -> p (t w)"),
                            psum[0:TN, 4:8, :].rearrange("p b w -> p (b w)")[:, 0:NT * 2 * R * H]).then_inc(s["lr_ev"], 1)

            dve.sem_inc(s["kt"], 2)
            dve.sem_inc(s["f_dve"], 1)
            with dve.Fori(0, NT // 2) as i:
                for u in range(2):
                    t = 2 * i + u
                    k_ps = bank[4 + u][0:TN, 0:D]
                    hold(dve, s["f_kv"], t + 1)
                    dve.tensor_scalar(mk[:, u, :], k_ps, 0.0, None, ALU.min).then_inc(s["mk"], 1)
                    hold(dve, s["ek"], t + 1)
                    hold(dve, s["kvm"], t + 1)
                    dve.scalar_tensor_tensor(out=kt[:, u, :], in0=k_ps, scalar=0.0, in1=ek[:, u, :],
                                             op0=ALU.max, op1=ALU.add).then_inc(s["kt"], 1)
                    hold(dve, s["f_pe"], t + 3)
                    hold(dve, s["stored"], t + 1)
                    dve.tensor_copy(feat_s[:, u, 1024:2048].rearrange("p (n w) -> p n w", n=2),
                                    psum[0:TN, 2:4, :]).then_inc(s["f_dve"], 1)
            dve.wait_ge(s["kvm"], NT + 3)
            for c in range(KC):
                link(dve.scalar_tensor_tensor(out=kv_m[:, c, :], in0=bank[6 + c][:, 0:128], scalar=1.0 / N,
                                              in1=mask[:, :], op0=ALU.mult, op1=ALU.mult))
                link(dve.tensor_scalar(ks_m[:, c, :], mask[:, :], bank[6 + c][:, 128:129], None, ALU.mult))
            link.wait()
            dve.sem_inc(s["kv_ready"], 1)

            dve.sem_inc(s["h2_done"], 1)
            with dve.Fori(0, NS) as k:
                link.loop(k, 17)
                hold(dve, s["q"], k + 1)
                q_ps = psum[:, 0:2, 0:SN]
                dve.tensor_scalar(qt[:, 0], q_ps, 0.0, None, ALU.min).then_inc(s["q_mn"], 1)
                hold(dve, s["q_ex"], k + 1)
                dve.scalar_tensor_tensor(out=qt[:, 2], in0=q_ps, scalar=0.0, in1=qt[:, 1],
                                         op0=ALU.max, op1=ALU.add).then_inc(s["q_t"], 1)
                hold(dve, s["nd"], k + 1)
                link(dve.tensor_scalar(msgT[:, :, :], psum[:, 4:6, 0:SN], ATT_EPS, None, ALU.add))
                link.wait()
                link(dve.reciprocal(msgT[:, :, :], msgT[:, :, :]))
                link.wait()
                dve.scalar_tensor_tensor(out=msgT[:, :, :], in0=psum[:, 2:4, 0:SN], scalar=float(N), in1=msgT[:, :, :],
                                         op0=ALU.mult, op1=ALU.mult).then_inc(s["msg"], 1)
                hold(dve, s["m"], k + 1)
                for j in range(SJ):
                    link(dve.bn_stats(st2[:, j, :], bank[j][0:TN, 0:D]))
                layer_stats().then_inc(s["ms_var"], 1)
                hold(dve, s["ms_sd"], k + 1)
                link(dve.reciprocal(sd2[:, :, 0], sd2[:, :, 0]))
                link.wait()
                for j in range(SJ):
                    ins = dve.tensor_scalar(ms[:, j, :], bank[j][0:TN, 0:D], mv2[:, j, 0:1], sd2[:, j, :], ALU.subtract, ALU.mult)
                ins.then_inc(s["ms"], 1)
                hold(dve, s["h2"], k + 1)
                for j in range(SJ):
                    link(dve.bn_stats(st2[:, j, :], bank[4 + j][0:TN, 0:D]))
                layer_stats().then_inc(s["h2_var"], 1)
                hold(dve, s["h2_sd"], k + 1)
                link(dve.reciprocal(sd2[:, :, 0], sd2[:, :, 0]))
                link.wait()
                for j in range(SJ):
                    link(dve.tensor_scalar(ms[:, j, :], bank[4 + j][0:TN, 0:D], mv2[:, j, 0:1], sd2[:, j, :], ALU.subtract, ALU.mult))
                link.wait()
                dve.sem_inc(s["h2_done"], 1)
                for j in range(SJ):
                    link(dve.tensor_tensor(ms[:, j, :], ms[:, j, :], g2_b[:, :], ALU.mult))
                link.wait()
                link(dve.tensor_tensor(node_sum[:, ds(k * SJ, SJ), :], node_sum[:, ds(k * SJ, SJ), :], ms[:, :, :], ALU.add))
            link.close(NS)

            dve.wait_ge(s["gath_use"], 1)
            link(dve.scalar_tensor_tensor(out=logits, in0=logits, scalar=0.2, in1=logits, op0=ALU.mult, op1=ALU.max))
            link.wait()

            def flip(ap, back):
                return ap[:, ::-1] if back else ap

            for back in range(2):
                marks = end_run if back else new_run
                for again in range(2):
                    for h in range(H):
                        src = run_max[:, :, h] if back or again else logits[:, :, h]
                        link(dve.tensor_tensor_scan(flip(run_max[:, :, h], back), flip(marks[:, :], back), flip(src, back),
                                                    cin[:, h:h + 1] if again else -BIG, ALU.add, ALU.max))
                    link.wait()
                    if again:
                        continue
                    edge = 0 if back else EC - 1
                    link(dve.tensor_copy(tailf[:, 0, :], run_max[:, edge, :]))
                    link(dve.tensor_reduce(tailf[:, 1, 0:1], marks[:, :], AX, ALU.min))
                    link.wait()
                    link(dve.tensor_copy(tailf[:, 1, 1:H], tailf[:, 1, 0:1].broadcast_to([128, H - 1])))
                    link(dve.memset(carry[:, :], -BIG))
                    link.wait()
                    dve.sem_inc(s["a_tail"], 1)
                    dve.wait_ge(s["a_tp"], back + 1)
                    link(dve.tensor_copy(rowf[:, :, :], bank[0][0:H, 0:256].rearrange("p (a n) -> p a n", a=2)))
                    link.wait()
                    link(dve.tensor_tensor_scan(flip(carry[:, 1:129], back), flip(rowf[:, 1, :], back), flip(rowf[:, 0, :], back),
                                                -BIG, ALU.add, ALU.max))
                    link.wait()
                    dve.sem_inc(s["a_row"], 1)
                    dve.wait_ge(s["a_tpb"], back + 1)
                    link(dve.tensor_copy(cin[:, :], bank[1][:, 0:H]))
                    link.wait()
            dve.tensor_tensor(run_max[:, :, :], logits, run_max[:, :, :], ALU.subtract).then_inc(s["a_sub"], 1)

            dve.wait_ge(s["h1"], NS)
            dve.memset(arena_n[:, :], 0.0).then_inc(s["dve"], 1)
            link.count += 1
            link.wait()
            dve.sem_inc(s["oh"], U)
            dve.sem_inc(s["agg_ev"], 2)

            def add_step(at, psum_row):
                b = dve.value_load(path_i[0:1, 1, at], min_val=0, max_val=NT - 1)
                row = edge_sum[:, ds(b, 1), :].rearrange("p t w -> p (t w)")
                dve.tensor_tensor(row, row, psum_row[0:TN, 0:W], ALU.add).then_inc(s["agg_ev"], 1)

            with dve.Fori(0, NSTEP // U) as i:
                link.loop(i, 3 * U)
                for u in range(U):
                    st = U * i + u
                    hold(dve, row_in[u], 16 * GJ * i + 16 * GJ)
                    rows = ring[:, u, :, 0:D].rearrange("p j (h d) -> p j h d", h=H)
                    ex = rec_b[:, u, :, 2:2 + H]
                    link(dve.tensor_scalar(dst_rel[:, u, :], rec_b[:, u, :, 1], path_f[:, 2, ds(st, 1)], None, ALU.subtract))
                    link(dve.tensor_copy(ring[:, u, :, D:W], ex))
                    link(dve.tensor_tensor(rows, rows, ex.unsqueeze(3).broadcast_to([128, GJ, H, HD]), ALU.mult))
                    link.wait()
                    dve.tensor_tensor(onehot[:, u], iota_n[:, 0:TN].unsqueeze(1).broadcast_to([128, GJ, TN]),
                                      dst_rel[:, u, :].unsqueeze(2).broadcast_to([128, GJ, TN]), ALU.is_equal).then_inc(s["oh"], 1)
                    hold(dve, s["slot"], st + U)
                    hold(dve, s["agg_ev"], st + 2)
                    add_step(ds(st, 1), bank[(u - 1) % U])
            link.close(NSTEP // U)
            dve.wait_ge(s["slot"], NSTEP + U)
            dve.wait_ge(s["agg_ev"], NSTEP + 2)
            add_step(slice(NSTEP, NSTEP + 1), bank[U - 1])
            dve.wait_ge(s["agg_ev"], NSTEP + 3)

            den = edge_sum[:, :, D:W]
            link(dve.tensor_scalar(den, den, 1e-30, None, ALU.max))
            link.wait()
            link(dve.reciprocal(den, den))
            link.wait()
            dve.sem_inc(s["acc"], 2)
            with dve.Fori(0, NS) as k:
                link.loop(k, 35)
                rows = node_sum[:, ds(k * SJ, SJ), :]
                for j in range(SJ):
                    t = k * SJ + j
                    v = edge_sum[:, ds(t, 1), 0:D].rearrange("p t (h d) -> p (t h) d", h=H)
                    link(dve.tensor_tensor(v, v, edge_sum[:, ds(t, 1), D:W].rearrange("p t h -> p (t h)").unsqueeze(2)
                                           .broadcast_to([TN, H, HD]), ALU.mult))
                link.wait()
                link(dve.tensor_tensor(rows, rows, edge_sum[:, ds(k * SJ, SJ), 0:D], ALU.add))
                link.wait()
                for j in range(SJ):
                    link(dve.bn_stats(st2[:, j, :], node_sum[:, ds(k * SJ + j, 1), :].rearrange("p t w -> p (t w)")))
                layer_stats().then_inc(s["x2_var"], 1)
                hold(dve, s["x2_sd"], k + 1)
                link(dve.reciprocal(sd2[:, :, 0], sd2[:, :, 0]))
                link.wait()
                for j in range(SJ):
                    link(dve.tensor_scalar(ms[:, j, :], node_sum[:, ds(k * SJ + j, 1), :].rearrange("p t w -> p (t w)"),
                                           mv2[:, j, 0:1], sd2[:, j, :], ALU.subtract, ALU.mult))
                link.wait()
                dve.sem_inc(s["x2n"], 1)
                link(dve.tensor_tensor(rows, rows, ms[:, :, :], ALU.add))
                hold(dve, s["lg"], k + 1)
                lg, pr = bank[2][0:TN, 0:SJ * NX].rearrange("p (j n) -> p j n", j=SJ), lg_s[:, 2]

                def wide(ap):
                    return ap.unsqueeze(2).broadcast_to([TN, SJ, NX])

                link(dve.tensor_reduce(rt[:, 0, :], lg, AX, ALU.max))
                link.wait()
                dve.tensor_tensor(lg_s[:, 0], lg, wide(rt[:, 0, :]), ALU.subtract).then_inc(s["lg_x"], 1)
                hold(dve, s["lg_ex"], k + 1)
                link(dve.tensor_reduce(rt[:, 1, :], lg_s[:, 1], AX, ALU.add))
                link.wait()
                link(dve.reciprocal(rt[:, 1, :], rt[:, 1, :]))
                link.wait()
                link(dve.tensor_tensor(pr, lg_s[:, 1], wide(rt[:, 1, :]), ALU.mult))
                link.wait()
                for j in range(SJ):
                    link(dve.max(top[:, j, :], lg_s[:, 2, j, :]))
                link.wait()
                for j in range(SJ):
                    link(dve.max_index(top_i[:, j, :], top[:, j, :], lg_s[:, 2, j, :]))
                link(dve.tensor_tensor(rt[:, 2, :], top[:, :, 0], top[:, :, 1], ALU.add))
                link.wait()
                link(dve.tensor_copy(top_f[:, :, :], top_i[:, :, :]))
                link(dve.tensor_scalar(rt[:, 2, :], rt[:, 2, :], 1e-12, None, ALU.max))
                link.wait()
                link(dve.reciprocal(rt[:, 2, :], rt[:, 2, :]))
                link.wait()
                link(dve.tensor_tensor(rt[:, 3, :], top[:, :, 1], rt[:, 2, :], ALU.mult))
                link(dve.tensor_tensor(rt[:, 2, :], top[:, :, 0], rt[:, 2, :], ALU.mult))
                experts = iota_n[0:TN, 0:NX].unsqueeze(1).broadcast_to([TN, SJ, NX])
                link(dve.tensor_tensor(lg_s[:, 0], experts, wide(top_f[:, :, 0]), ALU.is_equal))
                link(dve.tensor_tensor(lg_s[:, 1], experts, wide(top_f[:, :, 1]), ALU.is_equal))
                link.wait()
                link(dve.tensor_tensor(lg_s[:, 0], lg_s[:, 0], wide(rt[:, 2, :]), ALU.mult))
                link(dve.tensor_tensor(lg_s[:, 1], lg_s[:, 1], wide(rt[:, 3, :]), ALU.mult))
                link.wait()
                dve.tensor_tensor(lg_s[:, 3], lg_s[:, 0], lg_s[:, 1], ALU.add).then_inc(s["cmb"], 1)
                hold(dve, s["cmb_tp"], k + 1)
                dve.tensor_copy(combT[:, :], bank[7][0:NX, 0:SN]).then_inc(s["cmT"], 1)

                def add_rows(j, y, scale):
                    row = node_sum[:, ds(k * SJ + j, 1), :].rearrange("p t w -> p (t w)")
                    return dve.scalar_tensor_tensor(out=row, in0=y, scalar=scale, in1=row, op0=ALU.mult, op1=ALU.add)

                hold(dve, s["bias"], k + 1)
                for j in range(SJ):
                    link(add_rows(j, bias_at[j], 1.0))
                link.wait()
                dve.sem_inc(s["bias_ev"], 1)
                for e in range(NX):
                    hold(dve, s["down"], NX * k + e + 3)
                    for j in range(SJ):
                        ins = add_rows(j, y_at[e % 2][j], lg_s[:, 3, j, e:e + 1])
                    ins.then_inc(s["acc"], 1)
                    hold(dve, s["acc"], NX * k + e + 3)
            link.close(NS)

        @block.tensor
        def _(pe):
            def product(out_ap, pairs, sem_=None, **kw):
                for n, (w, m) in enumerate(pairs):
                    ins = pe.matmul(out_ap, w, m, start=n == 0, stop=n == len(pairs) - 1, skip_group_check=True)
                return ins

            pe.wait_ge(s["wts"], WTS)
            pe.wait_ge(s["consts"], 1)
            for c in range(KC):
                ins = pe.transpose(bank[7][:, c * NX:(c + 1) * NX], rw_s[:, c * 128:(c + 1) * 128], ident[0:NX, 0:NX])
            ins.then_inc(s["rw_tp"], 1)
            pe.wait_ge(s["path_c"], 1)
            product(bank[6][:, 0:NSTEP], [(ones[0:NG, :], path_cmp[:, 1, :])]).then_inc(s["path_p"], 1)

            pe.wait_ge(s["wlr"], 2)
            pe.wait_ge(s["rw_ev"], 1)
            pe.wait_ge(s["path_r"], 1)
            pe.sem_inc(s["tp"], 2)
            pe.sem_inc(s["lr"], 2)
            lr_ps = psum[0:TN, 4:8, :].rearrange("p b w -> p (b w)")
            with pe.Fori(0, NT // 2) as i:
                for u in range(2):
                    t = 2 * i + u
                    hold(pe, s["xs"], t + 1)
                    hold(pe, s["lr_x"], t + 1)
                    for c in range(KC):
                        ins = pe.transpose(bank[u][:, c * 128:c * 128 + TN], xs[:, u, c * 128:(c + 1) * 128], ident[0:TN, 0:TN])
                    ins.then_inc(s["tp"], 1)
                    hold(pe, s["xt"], t + 1)
                    product(lr_ps[:, ds(t * 2 * R * H, 2 * R * H)], [(xt[:, u, c, :], w_lr[:, c, :]) for c in range(KC)]).then_inc(s["lr"], 1)
            pe.wait_ge(s["lr_ev"], 1)
            pe.wait_ge(s["lr_x"], NT + 2)
            for c in range(KC):
                ins = pe.matmul(bank[6 + c][:, 0:129], zeros[0:TN, 0:128], zeros[0:TN, 0:129], start=True, stop=False, skip_group_check=True)
            ins.then_inc(s["kvm"], 1)
            pe.wait_ge(s["kvm"], 1)
            pe.sem_inc(s["kvm"], 1)
            pe.sem_inc(s["f_pe"], 2)
            with pe.Fori(0, NT // 2) as i:
                for u in range(2):
                    t = 2 * i + u
                    hold(pe, s["f_xt"], t + 1)
                    hold(pe, s["vt"], t + 1)
                    hold(pe, s["kt"], t + 1)
                    product(bank[4 + u][0:TN, :], [(xt[:, u, c, :], wkv[:, c, :]) for c in range(KC)]).then_inc(s["f_kv"], 1)
                    hold(pe, s["f_act"], t + 1)
                    for n in range(2):
                        ins = product(bank[n][0:TN, :], [(xt[:, u, c, :], conv_w[:, c, n * 512:(n + 1) * 512]) for c in range(KC)])
                    ins.then_inc(s["f_pe01"], 1)
                    hold(pe, s["f_dve"], t + 1)
                    for n in range(2, 4):
                        ins = product(bank[n][0:TN, :], [(xt[:, u, c, :], conv_w[:, c, n * 512:(n + 1) * 512]) for c in range(KC)])
                    ins.then_inc(s["f_pe"], 1)
                    hold(pe, s["kt"], t + 3)
                    hold(pe, s["vt"], t + 3)
                    for c in range(KC):
                        ins = pe.matmul(bank[6 + c][:, 0:129], kt[:, u, c * 128:(c + 1) * 128], vt[:, u, c, :],
                                        start=False, stop=False, skip_group_check=True)
                    ins.then_inc(s["kvm"], 1)
            for c in range(KC):
                ins = pe.matmul(bank[6 + c][:, 0:129], zeros[0:TN, 0:128], zeros[0:TN, 0:129], start=False, stop=True, skip_group_check=True)
            ins.then_inc(s["kvm"], 1)
            pe.wait_ge(s["f_act"], NT + 1)
            pe.wait_ge(s["f_dve"], NT + 1)
            pe.wait_ge(s["kv_ready"], 1)
            with pe.Fori(0, NS) as k:
                hold(pe, s["h_act"], k + 1)
                for o in range(KC):
                    ins = product(bank[o][:, 0:SN], [(wqm[:, 0, c, o * 128:(o + 1) * 128], xnT[:, c, ds(k * SN, SN)]) for c in range(KC)])
                ins.then_inc(s["q"], 1)
                hold(pe, s["q_t"], k + 1)
                hold(pe, s["h2_done"], k + 1)
                for c in range(KC):
                    product(bank[2 + c][:, 0:SN], [(kv_m[:, c, :], qt[:, 2, c, :])])
                    ins = product(bank[4 + c][:, 0:SN], [(ks_m[:, c, :], qt[:, 2, c, :])])
                ins.then_inc(s["nd"], 1)
                hold(pe, s["msg"], k + 1)
                for j in range(SJ):
                    ins = product(bank[j][0:TN, 0:D], [(msgT[:, c, j * TN:(j + 1) * TN], wqm[:, 1, c, :]) for c in range(KC)])
                ins.then_inc(s["m"], 1)
                hold(pe, s["ms"], k + 1)
                for j in range(SJ):
                    for c in range(KC):
                        ins = pe.transpose(bank[6 + c][:, j * TN:(j + 1) * TN], ms[:, j, c * 128:(c + 1) * 128], ident[0:TN, 0:TN])
                ins.then_inc(s["tpm"], 1)
                hold(pe, s["msT"], KC * k + KC)
                for o in range(2 * KC):
                    cols = slice(o * 128, (o + 1) * 128)
                    ins = product(bank[o][:, 0:SN], [(w1_s[:, c, cols], xnT[:, c, ds(k * SN, SN)]) for c in range(KC)]
                                  + [(w1_s[:, KC + c, cols], msT[:, c, :]) for c in range(KC)])
                ins.then_inc(s["h1"], 1)
                hold(pe, s["h_act"], k + 2)
                for j in range(SJ):
                    ins = product(bank[4 + j][0:TN, 0:D], [(hT[:, c, j * TN:(j + 1) * TN], w2_s[:, c, :]) for c in range(2 * KC)])
                ins.then_inc(s["h2"], 1)
            for back in range(2):
                pe.wait_ge(s["a_tail"], back + 1)
                for n in range(2):
                    ins = pe.transpose(bank[0][0:H, n * 128:(n + 1) * 128], tailf[:, n, :], ident[:, :])
                ins.then_inc(s["a_tp"], 1)
                pe.wait_ge(s["a_row"], back + 1)
                row = carry[:, 2:130] if back else carry[:, 0:128]
                pe.transpose(bank[1][:, 0:H], row, ident[0:H, 0:H]).then_inc(s["a_tpb"], 1)
            pe.wait_ge(s["a_sub"], 1)
            pe.wait_ge(s["h2_done"], NS + 1)
            product(bank[U - 1][0:TN, 0:132], [(zeros[:, 0:TN], zeros[:, 0:132])])
            product(bank[U - 1][0:TN, 132:W], [(zeros[:, 0:TN], zeros[:, 0:W - 132])]).then_inc(s["slot"], 1)
            pe.wait_ge(s["slot"], 1)
            pe.sem_inc(s["slot"], U - 1)
            with pe.Fori(0, NSTEP // U) as i:
                for u in range(U):
                    st = U * i + u
                    hold(pe, s["oh"], st + U + 1)
                    hold(pe, s["agg_ev"], st + 1)
                    product(bank[u][0:TN, 0:W], [(onehot[:, u, j, :], ring[:, u, j, :]) for j in range(GJ)]).then_inc(s["slot"], 1)
            pe.wait_ge(s["agg_ev"], NSTEP + 3)
            pe.wait_ge(s["moe1"], 16)
            pe.sem_inc(s["down"], 2)

            with pe.Fori(0, NS) as k:
                hold(pe, s["x2n"], k + 1)
                hold(pe, s["hid"], NX * k + 1)
                for j in range(SJ):
                    for c in range(KC):
                        ins = pe.transpose(bank[c][:, j * TN:(j + 1) * TN], ms[:, j, c * 128:(c + 1) * 128], ident[0:TN, 0:TN])
                ins.then_inc(s["x2tp"], 1)
                hold(pe, s["x2T"], k + 1)
                hold(pe, s["hid"], NX * k + 2)
                for j in range(SJ):
                    ins = product(bank[2][0:TN, j * NX:(j + 1) * NX], [(msT[:, c, j * TN:(j + 1) * TN], rwT[:, c, :]) for c in range(KC)])
                ins.then_inc(s["lg"], 1)

                def up(e):
                    hold(pe, s["hid"], NX * k + e + 1)
                    for o in range(KC):
                        ins = product(bank[(e % 2) * KC + o][:, 0:SN],
                                      [(mw1_s[:, e, c, o * 128:(o + 1) * 128], msT[:, c, :]) for c in range(KC)])
                    ins.then_inc(s["up"], 1)

                def down(e):
                    hold(pe, s["hid"], NX * k + e + 3)
                    hold(pe, s["acc"], NX * k + e + 1)
                    for j in range(SJ):
                        ins = product(y_at[e % 2][j], [(hT[:, (e % 2) * KC + c, j * TN:(j + 1) * TN], mw2_s[:, e, c, :]) for c in range(KC)])
                    ins.then_inc(s["down"], 1)

                up(0)
                hold(pe, s["cmb"], k + 1)
                up(1)
                hold(pe, s["acc"], NX * k + 2)
                for j in range(SJ):
                    ins = pe.transpose(bank[7][0:NX, j * TN:(j + 1) * TN], lg_s[:, 3, j, :], ident[0:TN, 0:TN])
                ins.then_inc(s["cmb_tp"], 1)
                hold(pe, s["cmT"], k + 1)
                for j in range(SJ):
                    ins = product(bias_at[j], [(combT[:, j * TN:(j + 1) * TN], mb2_s[:, :])])
                ins.then_inc(s["bias"], 1)
                hold(pe, s["bias_ev"], k + 1)
                down(0)
                for e in range(1, NX):
                    if e + 1 < NX:
                        up(e + 1)
                    down(e)


_INS = {"x": "x", "conv": "L0_gnn_conv_weights", "attn_l": "L0_gnn_attn_l", "attn_r": "L0_gnn_attn_r",
        "h_bias": "L0_gnn_h_bias", "Wq": "L0_mix_Wq", "Wk": "L0_mix_Wk", "Wv": "L0_mix_Wv", "Wm": "L0_mix_Wm",
        "W1": "L0_mix_W1", "W2": "L0_mix_W2", "g1": "L0_mix_g1", "b1": "L0_mix_b1", "g2": "L0_mix_g2",
        "b2": "L0_mix_b2", "router": "L0_ffn_router_w", "mw1": "L0_ffn_w1", "mb1": "L0_ffn_b1",
        "mw2": "L0_ffn_w2", "mb2": "L0_ffn_b2"}


def kernel(**inputs):
    import numpy as _np
    import concourse.bacc as _bacc
    from concourse import mybir as _mybir
    from concourse.bass_utils import run_bass_kernel_spmd as _run

    nc = _bacc.Bacc("TRN2", target_bir_lowering=False, num_devices=1)
    arrays = {name: _np.ascontiguousarray(inputs[key]) for name, key in _INS.items()}
    dst, src, typ = (_np.asarray(inputs[k]) for k in ("dst", "src", "edge_type_8"))
    pad = EP - E
    arrays["dst_ext"] = _np.concatenate([_np.full(1, -1, dst.dtype), dst, _np.full(pad, N, dst.dtype), _np.full(1, N + 1, dst.dtype)])
    arrays["src_pad"] = _np.concatenate([src, _np.zeros(pad, src.dtype)])
    arrays["type_pad"] = _np.concatenate([typ, _np.zeros(pad, typ.dtype)])
    args = {k: nc.dram_tensor(f"in_{k}", a.shape, _mybir.dt.from_np(a.dtype), kind="ExternalInput").ap() for k, a in arrays.items()}
    args["out"] = nc.dram_tensor("out_0", (N, D), F32, kind="ExternalOutput").ap()
    for name, shape in (("feat_t", (N, RF)), ("l_t", (N, R * H)), ("r_t", (N, R * H)), ("rec_t", (EP, 2 + H))):
        args[name] = nc.dram_tensor(name, shape, F32).ap()
    build(nc, **args)
    r = _run(nc, [{f"in_{k}": a for k, a in arrays.items()}], core_ids=[0])
    return r.results[0]["out_0"]
```

```python
from contextlib import ExitStack

import concourse.bass as bass
from concourse import mybir

ALU = mybir.AluOpType
ACT = mybir.ActivationFunctionType
AX = mybir.AxisListType.X
F32 = mybir.dt.float32
I32 = mybir.dt.int32
ds = bass.ds

N, D, R, H, E = 3750, 256, 8, 4, 60000
HD = D // H
RF = R * D
TN = 125
NT = N // TN
SJ = 3
SN = SJ * TN
NS = N // SN
GE, GJ = 512, 4
NG = -(-E // GE)
EP = NG * GE
EC = EP // 128
NSTEP = NG + NT - 1
NX = 8
TOP = 2
NM = (TOP * N + NX * 127) // 128
assert NM % 2 == 0 and NM * 128 * D % (128 * 132) == 0
KC = D // 128
AH = 32
LN_EPS, ATT_EPS = 1e-5, 1e-6
BIG = 1e38
W = D + H
U = 3
GC = 8
RQ = NS - 2
EQ = EC // RQ
ZQ = 4
assert N % SN == 0 and EC % (2 * GC) == GC and EC % RQ == 0 and EC % ZQ == 0 and NSTEP % U == 0


class Link:

    def __init__(self, eng, sem):
        self.eng, self.sem, self.base, self.count = eng, sem, 0, 0

    def __call__(self, ins):
        ins.then_inc(self.sem, 1)
        self.count += 1
        return ins

    def wait(self):
        hold(self.eng, self.sem, self.base + self.count)

    def loop(self, trip, per):
        self.per, self.outer = per, self.count
        self.base, self.count = trip * per + self.count, 0

    def close(self, trips):
        assert self.count == self.per, (self.count, self.per)
        self.base, self.count = 0, self.outer + trips * self.per


def hold(eng, sem, value):
    eng.wait_ge(sem, value)
    if not isinstance(value, int):
        eng.nop(nofuse=True)


def build(nc, x, dst_ext, src_pad, type_pad, conv, attn_l, attn_r, h_bias, Wq, Wk, Wv, Wm, W1, W2,
          g1, b1, g2, b2, router, mw1, mb1, mw2, mb2,
          out, feat_t, l_t, r_t, rec_t, dst_t, run_t, xs_t, ys_t):
    with ExitStack() as ctx:
        def sb(name, shape, dt=F32):
            return ctx.enter_context(nc.sbuf_tensor(name, shape, dt))

        def sem(name):
            return ctx.enter_context(nc.semaphore(name))

        psum = ctx.enter_context(nc.psum_tensor("psum", [128, 8, 512], F32))
        bank = [psum[:, i, :] for i in range(8)]

        node_sum = sb("node_sum", [TN, NT, D])
        arena_n = sb("arena_n", [128, NT * W])
        xnT = arena_n[:, 0:KC * N].rearrange("p (c n) -> p c n", c=KC)
        edge_sum = arena_n[0:TN, :].rearrange("p (t w) -> p t w", w=W)
        arena_h = sb("arena_h", [128, 3 * KC * SN])
        arena_w = sb("arena_w", [128, KC * RF])
        conv_w = arena_w[:, :].rearrange("p (c w) -> p c w", c=KC)
        mw1_s = arena_w[:, :].rearrange("p (e c w) -> p e c w", e=NX, c=KC)
        arena_f = sb("arena_f", [128, 2 * RF])
        attn_b = arena_f[:, 0:RF]
        prod = arena_f[:, RF:2 * RF]
        feat_s = arena_f[0:TN, :].rearrange("p (u w) -> p u w", u=2)
        r_part = arena_f[:, 0:EQ * R * H].rearrange("p (k g) -> p k g", g=R * H)
        is_type = arena_w[:, 0:EQ * R].rearrange("p (k r) -> p k r", r=R)
        attn_rb = arena_h[:, 0:RF]
        zero_w = arena_n[:, 0:EC // ZQ * R * H]
        ring = arena_f[:, 0:U * GJ * W].rearrange("p (u j w) -> p u j w", u=U, j=GJ)
        mw2_s = sb("mw2_s", [128, NX, KC, D])
        wqm = sb("wqm", [128, 2, KC, D])
        wkv = sb("wkv", [128, KC, 2 * D])
        w1_s = sb("w1_s", [128, 4, 2 * D])
        w2_s = sb("w2_s", [128, 4, D])
        w_lr = sb("w_lr", [128, KC, 2 * R * H])
        rw_s = sb("rw_s", [NX, D])
        rwT = sb("rwT", [128, KC, NX])
        colv = sb("colv", [128, 2 * KC])
        hb_b2 = sb("hb_b2", [TN, 2, D])
        g2_b = sb("g2_b", [TN, D])
        b1_row = arena_f[:, 0:NX * D].rearrange("p (e n) -> p e n", e=NX)
        b2_row = arena_f[:, NX * D:2 * NX * D].rearrange("p (e n) -> p e n", e=NX)
        ident = sb("ident", [128, 128])
        mask = sb("mask", [128, 128])
        zeros = sb("zeros", [128, 132])
        stats = sb("stats", [TN, NT, 6])
        mv = sb("mv", [TN, NT, 2])
        rstd = sb("rstd", [TN, NT, 1])
        xs = sb("xs", [TN, 2, D])
        xt = sb("xt", [128, 2, KC, TN])
        src_a = sb("src_a", [128, EC], I32)
        typ_a = sb("typ_a", [128, EC], I32)
        dst_f = sb("dst_f", [128, EC])
        first_i = sb("first_i", [128, 1], I32)
        first_w = sb("first_w", [128, TN])
        node_id = sb("node_id", [TN, NT])
        part_of = sb("part_of", [TN, NT])
        part_i = sb("part_i", [TN, NT], I32)
        below = sb("below", [TN, NT])
        first_at = sb("first_at", [TN, NT + 1])
        node_at = sb("node_at", [TN, NT])
        node_at_i = sb("node_at_i", [TN, NT], I32)
        shift = sb("shift", [TN, 2, TN])
        keep = sb("keep", [128, EC])
        r_first = sb("r_first", [128, R * H])
        rec = sb("rec", [128, EC, 2 + H])
        rec_idx = rec[:, :, 0].bitcast(I32)
        new_run = sb("new_run", [128, EC])
        end_run = sb("end_run", [128, EC])
        typ_f = src_a[:, :].bitcast(F32)
        run_max = sb("run_max", [128, EC, H])
        dst3 = run_max[:, :, :].rearrange("p k h -> p (k h)")[:, 0:3 * EC].rearrange("p (m k) -> p m k", m=3).bitcast(I32)
        idx_st = sb("idx_st", [128, 2, GC], I32)
        l_ring = sb("l_ring", [128, 2, GC, H])
        tailf = sb("tailf", [128, 2, H])
        rowf = sb("rowf", [H, 2, 128])
        carry = sb("carry", [H, 130])
        cin = sb("cin", [128, H])
        qt = sb("qt", [128, 3, KC, SN])
        arena_q = qt[:, :, :, :].rearrange("p a c n -> p (a c n)")
        found = arena_q[0:TN, 0:2 * EC].rearrange("p (u k) -> p u k", u=2)
        mk, ek, kt = (arena_q[0:TN, n * 2 * D:(n + 1) * 2 * D].rearrange("p (u d) -> p u d", u=2) for n in range(3))
        vt = arena_q[0:TN, 6 * D:6 * D + 4 * 129].rearrange("p (u c n) -> p u c n", u=2, c=KC)
        onehot = arena_q[:, 0:U * GJ * TN].rearrange("p (u j n) -> p u j n", u=U, j=GJ)
        kv_m = sb("kv_m", [128, KC, 128])
        ks_m = sb("ks_m", [128, KC, 128])
        msgT = sb("msgT", [128, KC, SN])
        ms = sb("ms", [TN, SJ, D])
        hT = arena_h[:, 0:2 * KC * SN].rearrange("p (c n) -> p c n", c=2 * KC)
        msT = arena_h[:, 2 * KC * SN:].rearrange("p (c n) -> p c n", c=KC)
        lr_s = arena_h[0:TN, 0:NT * 2 * R * H].rearrange("p (t w) -> p t w", t=NT)
        st2 = sb("st2", [TN, SJ, 6])
        mv2 = sb("mv2", [TN, SJ, 2])
        sd2 = sb("sd2", [TN, SJ, 1])
        last_i = sb("last_i", [NG, 1], I32)
        last_f = sb("last_f", [NG, 2])
        thr = sb("thr", [NG, NT - 1])
        path_cmp = sb("path_cmp", [NG, 2, NSTEP])
        ones = sb("ones", [128, 128])
        path_f = sb("path_f", [128, 3, NSTEP])
        path_i = sb("path_i", [1, 2, NSTEP + 1], I32)
        rec_b = sb("rec_b", [128, U, GJ, 2 + H])
        dst_rel = sb("dst_rel", [128, U, GJ])
        iota_n = sb("iota_n", [128, 128])
        eps_t = sb("eps_t", [128, 1])
        tmp_t = sb("tmp_t", [TN, 2, NT])
        lg_s = arena_q[0:TN, 0:5 * NT * NX].rearrange("p (a t e) -> p a t e", a=5, t=NT)
        hot = arena_q[0:TN, 5 * NT * NX:7 * NT * NX].rearrange("p (a t e) -> p a t e", a=TOP, t=NT)
        rt = sb("rt", [TN, 6, NT])
        share = sb("share", [TN, TOP, NT])
        row_of = sb("row_of", [TN, TOP, NT], I32)
        tri = sb("tri", [TN, TN])
        ex_t = sb("ex_t", [TN, 4, NX])
        step_x = arena_q[0:1, 7 * NT * NX:7 * NT * NX + NM * NX]
        step_f = sb("step_f", [1, NM])
        step_i = sb("step_i", [1, NM], I32)
        x_in, x_T, h_b, h_g, h_T, y_b = (arena_n[:, n * 2 * D:(n + 1) * 2 * D].rearrange("p (u d) -> p u d", u=2) for n in range(6))
        y_in = arena_n[0:TN, 12 * D:(12 + 4 * TOP) * D].rearrange("p (u a d) -> p u a d", u=4, a=TOP)

        s = {k: sem("s_" + k) for k in (
            "x wts conv attn edges last moe1 consts dve act pool stats std xs tp lr_x xt lr lr_ev lr_out "
            "wlr zeroed run_z dst_out d0 d0_bc part found0 found1 found_ev first_up shifted node_pos scat r_first_in "
            "r_load r_sel f_xt f_kv f_pe01 f_pe f_act f_dve f_out stored kvm mk ek kt vt kv_ready q q_mn "
            "q_ex q_t nd msg m ms_var ms_sd ms tpm msT h1a h1b h_act h2 h2_var h2_sd h2_done idx gath0 gath1 gath_use "
            "a_tail a_tp a_row a_tpb a_sub a_ex rec_out path_c path_p path_r rec_in0 rec_in1 rec_in2 row_in0 row_in1 "
            "row_in2 slot oh agg_ev rw_tp rw_ev x2_var x2_sd x2n x2tp x2T lg lg_x lg_ex picked ranked placed steps "
            "xs_z sent b_rows x_in0 x_in1 xtp xtc up hb hg htp htc down yb y_out0 y_out1 y_in0 y_in1 y_in2 y_in3 acc outd").split()}
        rec_in = [s["rec_in0"], s["rec_in1"], s["rec_in2"]]
        row_in = [s["row_in0"], s["row_in1"], s["row_in2"]]
        gath = [s["gath0"], s["gath1"]]

        x_v = x.rearrange("(t p) d -> p t d", p=TN)
        out_v = out.rearrange("(t p) d -> p t d", p=TN)
        feat_v = feat_t.rearrange("(t p) w -> p t w", p=TN)
        feat_rows = feat_t.rearrange("n (r d) -> (n r) d", r=R)
        l_rows = l_t.rearrange("n (r h) -> (n r) h", h=H)
        run_q = run_t[0:EP, :].rearrange("(p k) w -> p (k w)", p=128)
        found_in = [s["found0"], s["found1"]]
        right = run_max[:, :, :]
        rec_g = rec_t.rearrange("(g q j) w -> g q (j w)", g=NG, j=GJ)
        logits = rec[:, :, 2:2 + H]
        x_rows = xs_t.rearrange("(s p) d -> s p d", p=128)
        y_rows = ys_t.rearrange("(s p) d -> s p d", p=128)
        x_arr, y_left = [s["x_in0"], s["x_in1"]], [s["y_out0"], s["y_out1"]]
        y_arr = [s["y_in0"], s["y_in1"], s["y_in2"], s["y_in3"]]
        WTS = 16 * 13

        def bcast(v, parts):
            return v.rearrange("(a n) -> a n", a=1).broadcast_to([parts, v.shape[0]])

        def expert_steps(eng, stages):
            first = 3
            last = NM - 3
            assert (last - first) % 2 == 0

            def turn(i):
                for lead, f in stages:
                    if 0 <= i + lead < NM:
                        f(i + lead, (i + lead) % 2, (i + lead) // 2)

            for i in range(-2, first):
                turn(i)
            with eng.Fori(0, (last - first) // 2) as m:
                for v in range(first, first + 2):
                    for lead, f in stages:
                        f(2 * m + (v + lead), (v + lead) % 2, m + (v + lead) // 2)
            for i in range(last, NM + 1):
                turn(i)

        def step_expert(eng, st):
            at = slice(st, st + 1) if isinstance(st, int) else ds(st, 1)
            return eng.value_load(step_i[0:1, at], min_val=0, max_val=NX - 1)

        block = ctx.enter_context(nc.Block())

        @block.sync
        def _(sp):
            for m in range(3):
                sp.dma_start(dst3[:, m, :], dst_ext[m:m + EP].rearrange("(p k) -> p k", p=128)).then_inc(s["edges"], 16)
            sp.dma_start(src_a[:, :], src_pad.rearrange("(p k) -> p k", p=128)).then_inc(s["edges"], 16)
            sp.dma_start(typ_a[:, :], type_pad.rearrange("(p k) -> p k", p=128)).then_inc(s["edges"], 16)
            for c in range(KC):
                sp.dma_start(conv_w[:, c, :].rearrange("p (g d) -> p g d", d=HD),
                             conv.rearrange("r h i d -> i (r h) d")[c * 128:(c + 1) * 128]).then_inc(s["conv"], 16)
            sp.dma_start(attn_b, bcast(attn_l.rearrange("r h d -> (r h d)"), 128)).then_inc(s["attn"], 16)
            sp.dma_start(attn_rb, bcast(attn_r.rearrange("r h d -> (r h d)"), 128)).then_inc(s["attn"], 16)
            sp.dma_start(node_sum[:, :, :], x_v).then_inc(s["x"], 16)
            sp.wait_ge(s["d0"], 1)
            sp.dma_start(dst_t.rearrange("(p k) -> p k", p=128), dst_f[:, :]).then_inc(s["dst_out"], 16)
            sp.wait_ge(s["zeroed"], 1)
            for q in range(ZQ):
                w = EC // ZQ * R * H
                sp.dma_start(run_q[:, q * w:(q + 1) * w], zero_w).then_inc(s["run_z"], 16)
            for n, w in ((0, Wq), (1, Wm)):
                sp.dma_start(wqm[:, n], w.rearrange("(c p) n -> p c n", p=128)).then_inc(s["wts"], 16)
            for n, w in ((0, Wk), (1, Wv)):
                sp.dma_start(wkv[:, :, n * D:(n + 1) * D], w.rearrange("(c p) n -> p c n", p=128)).then_inc(s["wts"], 16)
            sp.dma_start(w1_s[:, :, :], W1.rearrange("(c p) n -> p c n", p=128)).then_inc(s["wts"], 16)
            sp.dma_start(w2_s[:, :, :], W2.rearrange("(c p) n -> p c n", p=128)).then_inc(s["wts"], 16)
            sp.dma_start(rw_s[:, :], router).then_inc(s["wts"], 16)
            sp.dma_start(hb_b2[:, 0, :], bcast(h_bias, TN)).then_inc(s["wts"], 16)
            sp.dma_start(hb_b2[:, 1, :], bcast(b2, TN)).then_inc(s["wts"], 16)
            sp.dma_start(g2_b[:, :], bcast(g2, TN)).then_inc(s["wts"], 16)
            with nc.allow_non_contiguous_dma(reason="vectors laid out by feature on the partitions"):
                sp.dma_start(last_i[:, :], dst_ext[1:1 + EP].rearrange("(g k) -> g k", g=NG)[:, GE - 1:GE]).then_inc(s["last"], 16)
                for n, v in ((0, g1), (1, b1)):
                    sp.dma_start(colv[:, n * KC:(n + 1) * KC], v.rearrange("(c p) -> p c", p=128)).then_inc(s["wts"], 16)
            sp.dma_start(mw2_s[:, :, :, :].rearrange("p e c n -> p (e c) n"),
                         mw2.rearrange("e (c p) n -> p (e c) n", p=128)).then_inc(s["wts"], 16)
            sp.wait_ge(s["lr_ev"], 1)
            sp.dma_start(l_t.rearrange("(t p) w -> p t w", p=TN), lr_s[:, :, 0:R * H]).then_inc(s["lr_out"], 16)
            sp.dma_start(r_t.rearrange("(t p) w -> p t w", p=TN), lr_s[:, :, R * H:2 * R * H]).then_inc(s["lr_out"], 16)
            sp.sem_inc(s["stored"], 2)
            with sp.Fori(0, NT // 2) as i:
                for u in range(2):
                    t = 2 * i + u
                    hold(sp, s["f_act"], t + 2)
                    hold(sp, s["f_dve"], t + 2)
                    sp.dma_start(feat_v[:, ds(t, 1), :].rearrange("p t w -> p (t w)"), feat_s[:, u, :]).then_inc(s["f_out"], 16)
                    hold(sp, s["f_out"], 16 * (t + 1))
                    sp.sem_inc(s["stored"], 1)
            for n in range(2):
                half = NM * D // 132 // 2
                sp.dma_start(xs_t.rearrange("(p k) d -> p (k d)", p=128)[:, n * half * 132:(n + 1) * half * 132].rearrange("p (a b) -> p a b", b=132),
                             zeros[:, :].unsqueeze(1).broadcast_to([128, half, 132])).then_inc(s["xs_z"], 16)
            sp.wait_ge(s["f_pe"], NT + 2)
            sp.wait_ge(s["scat"], 16 * NT)
            with sp.Fori(0, RQ) as q:
                hold(sp, s["r_sel"], q + 1)
                sp.dma_start(r_part.rearrange("p k g -> p (k g)"), run_q[:, ds(q * EQ * R * H, EQ * R * H)]).then_inc(s["r_load"], 16)
            sp.wait_ge(s["r_sel"], RQ + 1)
            sp.dma_start(mw1_s.rearrange("p e c n -> p (e c) n"), mw1.rearrange("e (c p) n -> p (e c) n", p=128)).then_inc(s["moe1"], 16)
            sp.wait_ge(s["a_ex"], 1)
            sp.dma_start(rec_t.rearrange("(p k) w -> p (k w)", p=128), rec[:, :, :].rearrange("p k w -> p (k w)")).then_inc(s["rec_out"], 16)
            sp.wait_ge(s["rec_out"], 16)
            sp.wait_ge(s["path_r"], 1)
            with sp.Fori(0, NSTEP // U) as i:
                for u in range(U):
                    hold(sp, s["oh"], U * i + u + 1)
                    g = sp.value_load(path_i[0:1, 0, ds(U * i + u, 1)], min_val=0, max_val=NG - 1)
                    sp.dma_start(rec_b[:, u].rearrange("p j w -> p (j w)"), rec_g[ds(g, 1)].rearrange("g q w -> (g q) w")).then_inc(rec_in[u], 16)
            sp.wait_ge(s["slot"], NSTEP + U)
            sp.dma_start(b1_row.rearrange("p e n -> p (e n)"), bcast(mb1.rearrange("e n -> (e n)"), 128)).then_inc(s["b_rows"], 16)
            sp.dma_start(b2_row.rearrange("p e n -> p (e n)"), bcast(mb2.rearrange("e n -> (e n)"), 128)).then_inc(s["b_rows"], 16)
            with sp.Fori(0, NM // 2) as i:
                for u in range(2):
                    hold(sp, s["yb"], 2 * i + u + 3)
                    sp.dma_start(y_rows[ds(2 * i + u, 1)].rearrange("s p d -> (s p) d"), y_b[:, u]).then_inc(y_left[u], 16)
            with sp.Fori(0, NS) as k:
                hold(sp, s["acc"], SJ * k + SJ)
                sp.dma_start(out_v[:, ds(k * SJ, SJ), :], node_sum[:, ds(k * SJ, SJ), :]).then_inc(s["outd"], 16)
            sp.wait_ge(s["outd"], 16 * NS)

        @block.gpsimd
        def _(pool):
            link = Link(pool, s["pool"])
            link(pool.memset(ident[:, :], 0.0))
            link(pool.memset(ones[:, :], 1.0))
            link(pool.memset(zeros[:, :], 0.0))
            link(pool.memset(eps_t[:, :], LN_EPS))
            link(pool.memset(vt[:, :, :, 128:129], 1.0))
            for tile, step, base, mul in ((iota_n[:, :], 1, 0, 0), (thr[:, :], TN, TN, 0), (path_cmp[:, 0, :], 1, 0, 0),
                                          (path_f[:, 0, :], 1, 0, 0), (last_f[:, 0:1], 0, 1, 1), (node_id[:, :], TN, 0, 1)):
                link(pool.iota(tile, pattern=[[step, tile.shape[1]]], base=base, channel_multiplier=mul,
                               allow_small_or_imprecise_dtypes=True))
            link.wait()
            link(pool.affine_select(out=ident[:, :], in_=ident[:, :], compare_op=ALU.not_equal, fill=1.0,
                                    base=0, pattern=[[-1, 128]], channel_multiplier=1))
            link(pool.affine_select(out=shift[:, 0, :], in_=zeros[0:TN, 0:TN], compare_op=ALU.not_equal, fill=1.0,
                                    base=-1, pattern=[[-1, TN]], channel_multiplier=1))
            link(pool.affine_select(out=shift[:, 1, :], in_=zeros[0:TN, 0:TN], compare_op=ALU.not_equal, fill=1.0,
                                    base=TN - 1, pattern=[[-1, TN]], channel_multiplier=TN))
            link(pool.affine_select(out=tri[:, :], in_=ones[0:TN, 0:TN], compare_op=ALU.is_gt, fill=0.0,
                                    base=0, pattern=[[1, TN]], channel_multiplier=-1))
            link(pool.affine_select(out=mask[:, :], in_=ones[:, :], compare_op=ALU.is_ge, fill=0.0,
                                    base=0, pattern=[[-AH, 128 // AH], [0, AH]], channel_multiplier=1))
            link.wait()
            pool.affine_select(out=mask[:, :], in_=mask[:, :], compare_op=ALU.is_ge, fill=0.0,
                               base=AH - 1, pattern=[[AH, 128 // AH], [0, AH]], channel_multiplier=-1).then_inc(s["consts"], 1)

            pool.wait_ge(s["part"], 1)
            pool.wait_ge(s["dst_out"], 16)
            for t in range(NT):
                if t > 1:
                    pool.wait_ge(s["found_ev"], t - 1)
                pool.indirect_dma_start(out=found[:, t % 2, :], out_offset=None, in_=dst_t.rearrange("(p k) -> p k", p=128),
                                        in_offset=bass.IndirectOffsetOnAxis(ap=part_i[:, t:t + 1], axis=0)).then_inc(found_in[t % 2], 16)
            pool.wait_ge(s["idx"], 1)
            pool.wait_ge(s["lr_out"], 32)

            def ask(u, col):
                link(pool.tensor_copy(idx_st[:, u, :], rec_idx[:, ds(col, GC)]))
                link.wait()
                for c in range(GC):
                    pool.indirect_dma_start(out=l_ring[:, u, c, :], out_offset=None, in_=l_rows,
                                            in_offset=bass.IndirectOffsetOnAxis(ap=idx_st[:, u, c:c + 1], axis=0),
                                            ).then_inc(gath[u], 16)

            def take(u, col, times):
                hold(pool, gath[u], times * (GC * 16))
                link(pool.tensor_copy(logits[:, ds(col, GC), :], l_ring[:, u]))
                link.wait()

            turns = EC // (2 * GC)
            ask(0, 0)
            pool.wait_ge(s["node_pos"], 1)
            pool.wait_ge(s["run_z"], 16 * ZQ)
            for t in range(NT):
                pool.indirect_dma_start(out=run_t, out_offset=bass.IndirectOffsetOnAxis(ap=node_at_i[:, t:t + 1], axis=0),
                                        in_=lr_s[:, t, R * H:2 * R * H], in_offset=None).then_inc(s["scat"], 16)
            pool.indirect_dma_start(out=r_first[:, :], out_offset=None, in_=r_t,
                                    in_offset=bass.IndirectOffsetOnAxis(ap=first_i[:, 0:1], axis=0)).then_inc(s["r_first_in"], 16)
            with pool.Fori(0, turns) as i:
                link.loop(i, 4)
                ask(1, 2 * GC * i + GC)
                take(0, 2 * GC * i, i + 1)
                ask(0, 2 * GC * i + 2 * GC)
                take(1, 2 * GC * i + GC, i + 1)
            link.close(turns)
            take(0, 2 * GC * turns, turns + 1)
            pool.drain().then_inc(s["gath_use"], 1)

            pool.wait_ge(s["f_out"], 16 * NT)
            with pool.Fori(0, NSTEP // U) as i:
                for u in range(U):
                    hold(pool, rec_in[u], 16 * i + 16)
                    hold(pool, s["slot"], U * i + u + 1)
                    for j in range(GJ):
                        pool.indirect_dma_start(out=ring[:, u, j, 0:D], out_offset=None, in_=feat_rows,
                                                in_offset=bass.IndirectOffsetOnAxis(ap=rec_b[:, u, j, 0:1].bitcast(I32), axis=0),
                                                ).then_inc(row_in[u], 16)

            pool.wait_ge(s["placed"], 1)
            pool.wait_ge(s["xs_z"], 32)
            for t in range(NT):
                for a in range(TOP):
                    pool.indirect_dma_start(out=xs_t, out_offset=bass.IndirectOffsetOnAxis(ap=row_of[:, a, t:t + 1], axis=0),
                                            in_=edge_sum[:, t, 0:D], in_offset=None).then_inc(s["sent"], 16)
            pool.wait_ge(s["sent"], 16 * TOP * NT)
            for st in range(2):
                pool.dma_start(x_in[:, st], x_rows[st]).then_inc(x_arr[st], 16)
            with pool.Fori(0, NM // 2 - 1) as i:
                for u in range(2):
                    hold(pool, s["xtp"], 2 * i + u + 1)
                    pool.dma_start(x_in[:, u], x_rows[ds(2 * i + u + 2, 1)].rearrange("s p d -> (s p) d")).then_inc(x_arr[u], 16)
            for u in range(2):
                pool.wait_ge(y_left[u], 16 * NM // 2)
            for t in range(NT):
                if t >= 4:
                    pool.wait_ge(s["acc"], t - 3)
                for a in range(TOP):
                    pool.indirect_dma_start(out=y_in[:, t % 4, a, :], out_offset=None, in_=ys_t,
                                            in_offset=bass.IndirectOffsetOnAxis(ap=row_of[:, a, t:t + 1], axis=0)).then_inc(y_arr[t % 4], 16)

        @block.scalar
        def _(act):
            act.wait_ge(s["stats"], 1)
            act.wait_ge(s["consts"], 1)
            act.activation(rstd[:, :, 0], mv[:, :, 1], ACT.Sqrt, bias=eps_t[0:TN, :]).then_inc(s["std"], 1)
            act.wait_ge(s["run_z"], 16 * ZQ)
            act.sem_inc(s["lr_x"], 2)
            with act.Fori(0, NT // 2) as i:
                for u in range(2):
                    t = 2 * i + u
                    hold(act, s["tp"], t + 3)
                    hold(act, s["lr"], t + 1)
                    v = bank[u][:, 0:256].rearrange("p (c n) -> p c n", c=KC)[:, :, 0:TN]
                    act.activation(xt[:, u], v, ACT.Copy).then_inc(s["xt"], 1)
                    act.activation(xnT[:, :, ds(t * TN, TN)], v, ACT.Copy).then_inc(s["lr_x"], 1)
            act.wait_ge(s["lr_x"], NT + 2)
            act.wait_ge(s["lr"], NT + 2)
            act.sem_inc(s["vt"], 2)
            act.sem_inc(s["f_act"], 1)
            with act.Fori(0, NT // 2) as i:
                for u in range(2):
                    t = 2 * i + u
                    hold(act, s["f_pe"], t + 1)
                    act.activation(xt[:, u], xnT[:, :, ds(t * TN, TN)], ACT.Copy).then_inc(s["f_xt"], 1)
                    hold(act, s["mk"], t + 1)
                    act.activation(ek[:, u, :], mk[:, u, :], ACT.Exp).then_inc(s["ek"], 1)
                    hold(act, s["kt"], t + 3)
                    hold(act, s["kvm"], t + 1)
                    act.activation(vt[:, u, :, 0:128], bank[4 + u][0:TN, D:2 * D].rearrange("p (c n) -> p c n", c=KC),
                                   ACT.Copy).then_inc(s["vt"], 1)
                    hold(act, s["f_pe01"], t + 1)
                    hold(act, s["stored"], t + 1)
                    act.activation(feat_s[:, u, 0:1024].rearrange("p (n w) -> p n w", n=2), psum[0:TN, 0:2, :],
                                   ACT.Copy).then_inc(s["f_act"], 1)
            act.wait_ge(s["lr_out"], 32)
            act.wait_ge(s["scat"], 16 * NT)

            def q_exp(k):
                hold(act, s["q_mn"], k + 1)
                act.activation(qt[:, 1], qt[:, 0], ACT.Exp).then_inc(s["q_ex"], 1)

            def second_half(k):
                hold(act, s["tpm"], k + 1)
                for c in range(KC):
                    act.activation(msT[:, c, :], bank[4 + c][:, 0:SN], ACT.Identity, scale=colv[:, c:c + 1],
                                   bias=colv[:, KC + c:KC + c + 1]).then_inc(s["msT"], 1)
                for n, (b, done) in enumerate(((6, s["h1a"]), (4, s["h1b"]))):
                    hold(act, done, k + 1)
                    act.activation(hT[:, n * KC:(n + 1) * KC, :], psum[:, b:b + KC, 0:SN], ACT.Relu).then_inc(s["h_act"], 1)

            def root(k, var, sd):
                hold(act, s[var], k + 1)
                act.activation(sd2[:, :, 0], mv2[:, :, 1], ACT.Sqrt, bias=eps_t[0:TN, :]).then_inc(s[sd], 1)

            def q_turn(k):
                q_exp(k + 1)
                second_half(k)
                root(k + 1, "ms_var", "ms_sd")
                root(k, "h2_var", "h2_sd")

            q_exp(0)
            root(0, "ms_var", "ms_sd")
            with act.Fori(0, NS - 2) as k:
                q_turn(k)
            q_turn(NS - 2)
            second_half(NS - 1)
            root(NS - 1, "h2_var", "h2_sd")
            act.wait_ge(s["a_sub"], 1)
            act.activation(logits, run_max[:, :, :], ACT.Exp).then_inc(s["a_ex"], 1)
            act.sem_inc(s["x2T"], 1)
            with act.Fori(0, NS) as k:
                hold(act, s["x2_var"], k + 1)
                act.activation(sd2[:, :, 0], mv2[:, :, 1], ACT.Sqrt, bias=eps_t[0:TN, :]).then_inc(s["x2_sd"], 1)
                hold(act, s["x2tp"], k + 2)
                hold(act, s["lg"], k + 1)
                act.activation(msT[:, :, :], psum[:, 0:2, 0:SN], ACT.Copy).then_inc(s["x2T"], 1)
            act.wait_ge(s["lg_x"], 1)
            act.activation(lg_s[:, 1], lg_s[:, 0], ACT.Exp).then_inc(s["lg_ex"], 1)

            for k in ("xtc", "hg", "htc"):
                act.sem_inc(s[k], 2)

            def x_turned(st, u, n):
                hold(act, s["xtp"], st + 1)
                hold(act, s["up"], st + 1)
                act.activation(x_T[:, u], bank[u][:, 0:D], ACT.Copy).then_inc(s["xtc"], 1)

            def gelu(st, u, n):
                hold(act, s["hb"], st + 3)
                hold(act, s["htp"], st + 1)
                act.activation(h_g[:, u], h_b[:, u], ACT.Gelu).then_inc(s["hg"], 1)

            def h_turned(st, u, n):
                hold(act, s["htp"], st + 3)
                hold(act, s["down"], st + 1)
                act.activation(h_T[:, u], bank[4 + u][:, 0:D], ACT.Copy).then_inc(s["htc"], 1)

            expert_steps(act, [(2, x_turned), (1, gelu), (0, h_turned)])

        @block.vector
        def _(dve):
            link = Link(dve, s["dve"])

            def layer_stats():
                link.wait()
                for j in range(SJ):
                    ins = dve.bn_aggr(mv2[:, j, :], st2[:, j, :])
                return ins

            link(dve.memset(arena_n[:, :], 0.0))
            link.wait()
            dve.sem_inc(s["zeroed"], 1)
            dve.wait_ge(s["edges"], 16 * 5)
            link(dve.tensor_copy(dst_f[:, :], dst3[:, 1, :]))
            dve.wait_ge(s["consts"], 1)
            link.wait()
            link(dve.tensor_scalar(first_w[:, :], ones[:, 0:TN], dst_f[:, 0:1], None, ALU.mult))
            link(dve.tensor_scalar(first_i[:, :], dst3[:, 1, 0:1], float(N - 1), None, ALU.min))
            link.wait()
            dve.sem_inc(s["d0"], 1)
            link(dve.scalar_tensor_tensor(out=rec_idx, in0=src_a[:, :], scalar=float(R), in1=typ_a[:, :], op0=ALU.mult, op1=ALU.add))
            link(dve.tensor_copy(rec[:, :, 1], dst3[:, 1, :]))
            link(dve.tensor_tensor(new_run[:, :], dst3[:, 0, :], dst3[:, 1, :], ALU.not_equal))
            link(dve.tensor_tensor(end_run[:, :], dst3[:, 1, :], dst3[:, 2, :], ALU.not_equal))
            link.wait()
            link(dve.tensor_copy(typ_f, typ_a[:, :]))
            link(dve.tensor_scalar(keep[:, :], new_run[:, :], -1.0, 1.0, ALU.mult, ALU.add))
            link.wait()
            link(dve.tensor_scalar(new_run[:, :], new_run[:, :], -BIG, None, ALU.mult))
            dve.tensor_scalar(end_run[:, :], end_run[:, :], -BIG, None, ALU.mult).then_inc(s["idx"], 1)
            dve.wait_ge(s["d0_bc"], 1)
            cmp = arena_q[0:TN, 0:5 * 128].rearrange("p (t n) -> p t n", t=5)
            for t in range(0, NT, 5):
                link(dve.tensor_tensor(cmp, bank[5][0:TN, 0:128].unsqueeze(1).broadcast_to([TN, 5, 128]),
                                       node_id[:, t:t + 5].unsqueeze(2).broadcast_to([TN, 5, 128]), ALU.is_lt))
                link.wait()
                link(dve.tensor_reduce(part_of[:, t:t + 5], cmp, AX, ALU.add))
                link.wait()
            link(dve.tensor_scalar(part_of[:, :], part_of[:, :], -1.0, 0.0, ALU.add, ALU.max))
            link.wait()
            dve.tensor_copy(part_i[:, :], part_of[:, :]).then_inc(s["part"], 1)
            dve.wait_ge(s["last"], 16)
            dve.wait_ge(s["consts"], 1)
            link(dve.tensor_copy(last_f[:, 1:2], last_i[:, :]))
            link.wait()
            link(dve.tensor_scalar(thr[:, :], thr[:, :], last_f[:, 1:2], None, ALU.is_le))
            link.wait()
            link(dve.tensor_reduce(last_f[:, 1:2], thr[:, :], AX, ALU.add))
            link.wait()
            link(dve.tensor_tensor(last_f[:, 1:2], last_f[:, 1:2], last_f[:, 0:1], ALU.add))
            link.wait()
            dve.tensor_scalar(path_cmp[:, 1, :], path_cmp[:, 0, :], last_f[:, 1:2], None, ALU.is_ge).then_inc(s["path_c"], 1)
            dve.wait_ge(s["rw_tp"], 1)
            dve.tensor_copy(rwT[:, :, :], bank[7][:, 0:KC * NX].rearrange("p (c n) -> p c n", c=KC)).then_inc(s["rw_ev"], 1)
            dve.wait_ge(s["path_p"], 1)
            link(dve.tensor_copy(path_f[:, 1, :], bank[6][:, 0:NSTEP]))
            link.wait()
            link(dve.tensor_tensor(path_f[:, 2, :], path_f[:, 0, :], path_f[:, 1, :], ALU.subtract))
            link(dve.tensor_copy(path_i[0:1, 0, 0:NSTEP], path_f[0:1, 1, :]))
            link(dve.memset(path_i[0:1, 1, :], 0))
            link.wait()
            link(dve.tensor_copy(path_i[0:1, 1, 1:NSTEP + 1], path_f[0:1, 2, :]))
            link.wait()
            dve.tensor_scalar(path_f[:, 2, :], path_f[:, 2, :], float(TN), None, ALU.mult).then_inc(s["path_r"], 1)

            for side in range(2):
                dve.wait_ge(s["conv"], 16 * KC)
                dve.wait_ge(s["attn"], 32)
                for c in range(KC):
                    link(dve.tensor_tensor(prod, conv_w[:, c, :], attn_rb if side else attn_b, ALU.mult))
                    link.wait()
                    link(dve.tensor_reduce(w_lr[:, c, side * R * H:(side + 1) * R * H],
                                           prod.rearrange("p (g d) -> p g d", d=HD), AX, ALU.add))
                    link.wait()
            dve.sem_inc(s["wlr"], 1)

            dve.wait_ge(s["x"], 16)
            with dve.Fori(0, NT // 2) as i:
                link.loop(i, 2)
                for u in range(2):
                    link(dve.bn_stats(stats[:, ds(2 * i + u, 1), :].rearrange("p t w -> p (t w)"),
                                      node_sum[:, ds(2 * i + u, 1), :].rearrange("p t w -> p (t w)")))
            link.close(NT // 2)
            link.wait()
            link(dve.tensor_tensor(mv[:, :, 0], stats[:, :, 1], stats[:, :, 4], ALU.add))
            link(dve.tensor_tensor(tmp_t[:, 0, :], stats[:, :, 1], stats[:, :, 4], ALU.subtract))
            link(dve.tensor_tensor(tmp_t[:, 1, :], stats[:, :, 2], stats[:, :, 5], ALU.add))
            link.wait()
            link(dve.tensor_scalar(mv[:, :, 0], mv[:, :, 0], 0.5, None, ALU.mult))
            link(dve.tensor_tensor(tmp_t[:, 0, :], tmp_t[:, 0, :], tmp_t[:, 0, :], ALU.mult))
            link(dve.tensor_scalar(tmp_t[:, 1, :], tmp_t[:, 1, :], 1.0 / D, None, ALU.mult))
            link.wait()
            dve.scalar_tensor_tensor(out=mv[:, :, 1], in0=tmp_t[:, 0, :], scalar=0.25, in1=tmp_t[:, 1, :],
                                     op0=ALU.mult, op1=ALU.add).then_inc(s["stats"], 1)
            dve.wait_ge(s["wts"], WTS)
            link(dve.tensor_tensor(hb_b2[:, 0, :], hb_b2[:, 0, :], hb_b2[:, 1, :], ALU.add))
            dve.wait_ge(s["std"], 1)
            link(dve.reciprocal(rstd[:, :, 0], rstd[:, :, 0]))
            link.wait()
            with dve.Fori(0, NT // 2) as i:
                link.loop(i, 4)
                for u in range(2):
                    t = 2 * i + u
                    row = node_sum[:, ds(t, 1), :].rearrange("p t w -> p (t w)")
                    hold(dve, s["tp"], t + 1)
                    dve.tensor_scalar(xs[:, u, :], row, mv[:, ds(t, 1), 0], rstd[:, ds(t, 1), 0],
                                      ALU.subtract, ALU.mult).then_inc(s["xs"], 1)
                    hold(dve, found_in[u], 16 * i + 16)
                    link(dve.tensor_scalar(found[:, u, :], found[:, u, :], node_id[:, ds(t, 1)], None, ALU.is_lt))
                    link.wait()
                    link(dve.tensor_reduce(below[:, ds(t, 1)], found[:, u, :], AX, ALU.add))
                    link.wait()
                    dve.sem_inc(s["found_ev"], 1)
            link.close(NT // 2)
            link(dve.scalar_tensor_tensor(out=first_at[:, 0:NT], in0=part_of[:, :], scalar=float(EC), in1=below[:, :],
                                          op0=ALU.mult, op1=ALU.add))
            link(dve.memset(first_at[:, NT:NT + 1], float(E)))
            link.wait()
            dve.sem_inc(s["first_up"], 1)
            link(dve.tensor_scalar(node_id[:, :], node_id[:, :], float(EP), None, ALU.add))
            dve.wait_ge(s["shifted"], 1)
            link(dve.tensor_tensor(node_at[:, :], bank[2][0:TN, 0:NT], first_at[:, 0:NT], ALU.is_gt))
            link.wait()
            link(dve.tensor_tensor(first_at[:, 0:NT], first_at[:, 0:NT], node_id[:, :], ALU.subtract))
            link.wait()
            link(dve.tensor_tensor(node_at[:, :], node_at[:, :], first_at[:, 0:NT], ALU.mult))
            link.wait()
            link(dve.tensor_tensor(node_at[:, :], node_at[:, :], node_id[:, :], ALU.add))
            link.wait()
            dve.tensor_copy(node_at_i[:, :], node_at[:, :]).then_inc(s["node_pos"], 1)
            dve.wait_ge(s["lr"], NT + 2)
            dve.tensor_copy(lr_s[:, :, :].rearrange("p t w -> p (t w)"),
                            psum[0:TN, 4:8, :].rearrange("p b w -> p (b w)")[:, 0:NT * 2 * R * H]).then_inc(s["lr_ev"], 1)

            dve.sem_inc(s["kt"], 2)
            dve.sem_inc(s["f_dve"], 1)
            with dve.Fori(0, NT // 2) as i:
                link.loop(i, 6)
                for u in range(2):
                    t = 2 * i + u
                    k_ps = bank[4 + u][0:TN, 0:D]
                    row = node_sum[:, ds(t, 1), :].rearrange("p t w -> p (t w)")
                    hold(dve, s["f_kv"], t + 1)
                    dve.tensor_scalar(mk[:, u, :], k_ps, 0.0, None, ALU.min).then_inc(s["mk"], 1)
                    hold(dve, s["ek"], t + 1)
                    hold(dve, s["kvm"], t + 1)
                    dve.scalar_tensor_tensor(out=kt[:, u, :], in0=k_ps, scalar=0.0, in1=ek[:, u, :],
                                             op0=ALU.max, op1=ALU.add).then_inc(s["kt"], 1)
                    hold(dve, s["f_pe"], t + 3)
                    hold(dve, s["stored"], t + 1)
                    dve.tensor_copy(feat_s[:, u, 1024:2048].rearrange("p (n w) -> p n w", n=2),
                                    psum[0:TN, 2:4, :]).then_inc(s["f_dve"], 1)
                    link(dve.tensor_scalar(xs[:, u, :], row, mv[:, ds(t, 1), 0], rstd[:, ds(t, 1), 0], ALU.subtract, ALU.mult))
                    link.wait()
                    link(dve.tensor_tensor(row, row, xs[:, u, :], ALU.add))
                    link.wait()
                    link(dve.tensor_tensor(row, row, hb_b2[:, 0, :], ALU.add))
            link.close(NT // 2)
            dve.wait_ge(s["kvm"], NT + 3)
            for c in range(KC):
                link(dve.scalar_tensor_tensor(out=kv_m[:, c, :], in0=bank[6 + c][:, 0:128], scalar=1.0 / N,
                                              in1=mask[:, :], op0=ALU.mult, op1=ALU.mult))
                link(dve.tensor_scalar(ks_m[:, c, :], mask[:, :], bank[6 + c][:, 128:129], None, ALU.mult))
            link.wait()
            dve.sem_inc(s["kv_ready"], 1)

            dve.wait_ge(s["r_first_in"], 16)
            dve.sem_inc(s["h2_done"], 1)
            dve.sem_inc(s["r_sel"], 1)
            q_ps = psum[:, 0:2, 0:SN]
            m_at = [bank[2][0:TN, 0:D], bank[2][0:TN, D:2 * D], bank[3][0:TN, 0:D]]
            o_at = [bank[6][0:TN, 0:D], bank[6][0:TN, D:2 * D], bank[7][0:TN, 0:D]]
            norm = arena_h[0:TN, 0:SJ * D].rearrange("p (j d) -> p j d", j=SJ)

            def normalise(to, at):
                link(dve.reciprocal(sd2[:, :, 0], sd2[:, :, 0]))
                link.wait()
                for j in range(SJ):
                    link(dve.tensor_scalar(to[:, j, :], at[j], mv2[:, j, 0:1], sd2[:, j, :], ALU.subtract, ALU.mult))
                link.wait()

            def first_half(k):
                hold(dve, s["q"], k + 1)
                dve.tensor_scalar(qt[:, 0], q_ps, 0.0, None, ALU.min).then_inc(s["q_mn"], 1)
                hold(dve, s["q_ex"], k + 1)
                dve.scalar_tensor_tensor(out=qt[:, 2], in0=q_ps, scalar=0.0, in1=qt[:, 1],
                                         op0=ALU.max, op1=ALU.add).then_inc(s["q_t"], 1)
                hold(dve, s["nd"], k + 1)
                link(dve.tensor_scalar(msgT[:, :, :], q_ps, ATT_EPS, None, ALU.add))
                link.wait()
                link(dve.reciprocal(msgT[:, :, :], msgT[:, :, :]))
                link.wait()
                dve.scalar_tensor_tensor(out=msgT[:, :, :], in0=psum[:, 2:4, 0:SN], scalar=float(N), in1=msgT[:, :, :],
                                         op0=ALU.mult, op1=ALU.mult).then_inc(s["msg"], 1)

            def norm_1(k):
                hold(dve, s["m"], k + 1)
                for j in range(SJ):
                    link(dve.bn_stats(st2[:, j, :], m_at[j]))
                layer_stats().then_inc(s["ms_var"], 1)
                hold(dve, s["ms_sd"], k + 1)
                normalise(ms, m_at)
                dve.sem_inc(s["ms"], 1)

            def norm_2(k):
                hold(dve, s["h2"], k + 1)
                for j in range(SJ):
                    link(dve.bn_stats(st2[:, j, :], o_at[j]))
                layer_stats().then_inc(s["h2_var"], 1)
                hold(dve, s["h2_sd"], k + 1)
                normalise(norm, o_at)
                link(dve.tensor_tensor(norm, norm, g2_b[:, :].unsqueeze(1).broadcast_to([TN, SJ, D]), ALU.mult))
                link.wait()
                rows = node_sum[:, ds(k * SJ, SJ), :] if not isinstance(k, int) else node_sum[:, k * SJ:(k + 1) * SJ, :]
                link(dve.tensor_tensor(rows, rows, norm, ALU.add))
                link.wait()
                dve.sem_inc(s["h2_done"], 1)

            def right_part(q):
                hold(dve, s["r_load"], 16 * q + 16)
                for g in range(R * H):
                    link(dve.tensor_tensor_scan(r_part[:, :, g], keep[:, ds(q * EQ, EQ)], r_part[:, :, g],
                                                r_first[:, g:g + 1], ALU.mult, ALU.add))
                link(dve.tensor_tensor(is_type, typ_f[:, ds(q * EQ, EQ)].unsqueeze(2).broadcast_to([128, EQ, R]),
                                       iota_n[:, 0:R].unsqueeze(1).broadcast_to([128, EQ, R]), ALU.is_equal))
                link.wait()
                link(dve.tensor_copy(r_first[:, :], r_part[:, EQ - 1, :]))
                link.wait()
                part4 = r_part.rearrange("p k (r h) -> p k r h", h=H)
                link(dve.tensor_tensor(part4, part4, is_type.unsqueeze(3).broadcast_to([128, EQ, R, H]), ALU.mult))
                link.wait()
                link(dve.tensor_reduce(right[:, ds(q * EQ, EQ), :], r_part.rearrange("p k (r h) -> p k h r", h=H), AX, ALU.add))
                link.wait()
                dve.sem_inc(s["r_sel"], 1)

            first_half(0)
            norm_1(0)
            with dve.Fori(0, NS - 2) as k:
                link.loop(k, 2 + 7 + 9 + R * H + 4)
                first_half(k + 1)
                right_part(k)
                norm_1(k + 1)
                norm_2(k)
            link.close(NS - 2)
            first_half(NS - 1)
            norm_1(NS - 1)
            norm_2(NS - 2)
            norm_2(NS - 1)

            dve.wait_ge(s["gath_use"], 1)
            link(dve.tensor_tensor(logits, logits, right, ALU.add))
            link.wait()
            link(dve.scalar_tensor_tensor(out=logits, in0=logits, scalar=0.2, in1=logits, op0=ALU.mult, op1=ALU.max))
            link.wait()

            def flip(ap, back):
                return ap[:, ::-1] if back else ap

            for back in range(2):
                marks = end_run if back else new_run
                for again in range(2):
                    for h in range(H):
                        src = run_max[:, :, h] if back or again else logits[:, :, h]
                        link(dve.tensor_tensor_scan(flip(run_max[:, :, h], back), flip(marks[:, :], back), flip(src, back),
                                                    cin[:, h:h + 1] if again else -BIG, ALU.add, ALU.max))
                    link.wait()
                    if again:
                        continue
                    edge = 0 if back else EC - 1
                    link(dve.tensor_copy(tailf[:, 0, :], run_max[:, edge, :]))
                    link(dve.tensor_reduce(tailf[:, 1, 0:1], marks[:, :], AX, ALU.min))
                    link.wait()
                    link(dve.tensor_copy(tailf[:, 1, 1:H], tailf[:, 1, 0:1].broadcast_to([128, H - 1])))
                    link(dve.memset(carry[:, :], -BIG))
                    link.wait()
                    dve.sem_inc(s["a_tail"], 1)
                    dve.wait_ge(s["a_tp"], back + 1)
                    link(dve.tensor_copy(rowf[:, :, :], bank[0][0:H, 0:256].rearrange("p (a n) -> p a n", a=2)))
                    link.wait()
                    link(dve.tensor_tensor_scan(flip(carry[:, 1:129], back), flip(rowf[:, 1, :], back), flip(rowf[:, 0, :], back),
                                                -BIG, ALU.add, ALU.max))
                    link.wait()
                    dve.sem_inc(s["a_row"], 1)
                    dve.wait_ge(s["a_tpb"], back + 1)
                    link(dve.tensor_copy(cin[:, :], bank[1][:, 0:H]))
                    link.wait()
            dve.tensor_tensor(run_max[:, :, :], logits, run_max[:, :, :], ALU.subtract).then_inc(s["a_sub"], 1)

            dve.wait_ge(s["h1b"], NS)
            dve.memset(arena_n[:, :], 0.0).then_inc(s["dve"], 1)
            link.count += 1
            link.wait()
            dve.sem_inc(s["oh"], U)
            dve.sem_inc(s["agg_ev"], 2)

            def add_step(at, psum_row):
                b = dve.value_load(path_i[0:1, 1, at], min_val=0, max_val=NT - 1)
                row = edge_sum[:, ds(b, 1), :].rearrange("p t w -> p (t w)")
                dve.tensor_tensor(row, row, psum_row[0:TN, 0:W], ALU.add).then_inc(s["agg_ev"], 1)

            with dve.Fori(0, NSTEP // U) as i:
                link.loop(i, 3 * U)
                for u in range(U):
                    st = U * i + u
                    hold(dve, row_in[u], 16 * GJ * i + 16 * GJ)
                    rows = ring[:, u, :, 0:D].rearrange("p j (h d) -> p j h d", h=H)
                    ex = rec_b[:, u, :, 2:2 + H]
                    link(dve.tensor_scalar(dst_rel[:, u, :], rec_b[:, u, :, 1], path_f[:, 2, ds(st, 1)], None, ALU.subtract))
                    link(dve.tensor_copy(ring[:, u, :, D:W], ex))
                    link(dve.tensor_tensor(rows, rows, ex.unsqueeze(3).broadcast_to([128, GJ, H, HD]), ALU.mult))
                    link.wait()
                    dve.tensor_tensor(onehot[:, u], iota_n[:, 0:TN].unsqueeze(1).broadcast_to([128, GJ, TN]),
                                      dst_rel[:, u, :].unsqueeze(2).broadcast_to([128, GJ, TN]), ALU.is_equal).then_inc(s["oh"], 1)
                    hold(dve, s["slot"], st + U)
                    hold(dve, s["agg_ev"], st + 2)
                    add_step(ds(st, 1), bank[(u - 1) % U])
            link.close(NSTEP // U)
            dve.wait_ge(s["slot"], NSTEP + U)
            dve.wait_ge(s["agg_ev"], NSTEP + 2)
            add_step(slice(NSTEP, NSTEP + 1), bank[U - 1])
            dve.wait_ge(s["agg_ev"], NSTEP + 3)

            den = edge_sum[:, :, D:W]
            link(dve.tensor_scalar(den, den, 1e-30, None, ALU.max))
            link.wait()
            link(dve.reciprocal(den, den))
            link.wait()
            with dve.Fori(0, NS) as k:
                link.loop(k, 13)
                rows = node_sum[:, ds(k * SJ, SJ), :]
                for j in range(SJ):
                    t = k * SJ + j
                    v = edge_sum[:, ds(t, 1), 0:D].rearrange("p t (h d) -> p (t h) d", h=H)
                    link(dve.tensor_tensor(v, v, edge_sum[:, ds(t, 1), D:W].rearrange("p t h -> p (t h)").unsqueeze(2)
                                           .broadcast_to([TN, H, HD]), ALU.mult))
                link.wait()
                link(dve.tensor_tensor(rows, rows, edge_sum[:, ds(k * SJ, SJ), 0:D], ALU.add))
                link.wait()
                for j in range(SJ):
                    link(dve.bn_stats(st2[:, j, :], node_sum[:, ds(k * SJ + j, 1), :].rearrange("p t w -> p (t w)")))
                layer_stats().then_inc(s["x2_var"], 1)
                hold(dve, s["x2_sd"], k + 1)
                link(dve.reciprocal(sd2[:, :, 0], sd2[:, :, 0]))
                link.wait()
                hold(dve, s["x2tp"], k + 1)
                for j in range(SJ):
                    link(dve.tensor_scalar(ms[:, j, :], node_sum[:, ds(k * SJ + j, 1), :].rearrange("p t w -> p (t w)"),
                                           mv2[:, j, 0:1], sd2[:, j, :], ALU.subtract, ALU.mult))
                link.wait()
                dve.sem_inc(s["x2n"], 1)
                link(dve.tensor_tensor(rows, rows, ms[:, :, :], ALU.add))
                link(dve.tensor_copy(edge_sum[:, ds(k * SJ, SJ), 0:D], ms[:, :, :]))
            link.close(NS)
            dve.wait_ge(s["lg"], NS + 1)
            lg, pr, scr = bank[2][0:TN, 0:NT * NX].rearrange("p (t e) -> p t e", e=NX), lg_s[:, 2], lg_s[:, 3]
            experts = iota_n[0:TN, 0:NX].unsqueeze(1).broadcast_to([TN, NT, NX])

            def wide(ap):
                return ap.unsqueeze(2).broadcast_to([TN, NT, NX])

            def then(ins):
                link(ins)
                link.wait()

            then(dve.tensor_reduce(rt[:, 0, :], lg, AX, ALU.max))
            dve.tensor_tensor(lg_s[:, 0], lg, wide(rt[:, 0, :]), ALU.subtract).then_inc(s["lg_x"], 1)
            dve.wait_ge(s["lg_ex"], 1)
            then(dve.tensor_reduce(rt[:, 1, :], lg_s[:, 1], AX, ALU.add))
            then(dve.reciprocal(rt[:, 1, :], rt[:, 1, :]))
            then(dve.tensor_tensor(pr, lg_s[:, 1], wide(rt[:, 1, :]), ALU.mult))
            for a in range(TOP):
                then(dve.tensor_reduce(rt[:, 2 + a, :], pr, AX, ALU.max))
                then(dve.tensor_tensor(scr, pr, wide(rt[:, 2 + a, :]), ALU.is_lt))
                then(dve.scalar_tensor_tensor(out=scr, in0=scr, scalar=float(NX), in1=experts, op0=ALU.mult, op1=ALU.add))
                then(dve.tensor_reduce(rt[:, 4, :], scr, AX, ALU.min))
                then(dve.tensor_tensor(hot[:, a], experts, wide(rt[:, 4, :]), ALU.is_equal))
                if a == 0:
                    then(dve.scalar_tensor_tensor(out=pr, in0=hot[:, a], scalar=-4.0, in1=pr, op0=ALU.mult, op1=ALU.add))
            dve.tensor_tensor(lg_s[:, 4], hot[:, 0], hot[:, 1], ALU.add).then_inc(s["picked"], 1)
            then(dve.tensor_tensor(rt[:, 4, :], rt[:, 2, :], rt[:, 3, :], ALU.add))
            then(dve.tensor_scalar(rt[:, 4, :], rt[:, 4, :], 1e-12, None, ALU.max))
            then(dve.reciprocal(rt[:, 4, :], rt[:, 4, :]))
            for a in range(TOP):
                link(dve.tensor_tensor(share[:, a, :], rt[:, 2 + a, :], rt[:, 4, :], ALU.mult))
            dve.wait_ge(s["ranked"], 1)
            total, upto = bank[3][0:TN, NT * NX:2 * NT * NX].rearrange("p (t e) -> p t e", e=NX), lg_s[:, 0]
            then(dve.tensor_copy(lg_s[:, 1], total))
            for e in range(NX):
                link(dve.tensor_tensor_scan(upto[:, :, e], ones[0:TN, 0:NT], lg_s[:, 1, :, e], 0.0, ALU.mult, ALU.add))
            link.wait()
            then(dve.tensor_copy(ex_t[:, 0, :], upto[:, NT - 1, :]))
            tens = lg_s[:, 3].rearrange("p t e -> p (t e)").rearrange("p (e t) -> p e t", e=NX)
            then(dve.tensor_scalar(rt[:, 5, :], iota_n[0:TN, 0:NT], 128.0, None, ALU.mult))
            then(dve.tensor_tensor(tens, ex_t[:, 0, :].unsqueeze(2).broadcast_to([TN, NX, NT]),
                                   rt[:, 5, :].unsqueeze(1).broadcast_to([TN, NX, NT]), ALU.is_gt))
            then(dve.tensor_reduce(ex_t[:, 1, :], tens, AX, ALU.add))
            then(dve.tensor_tensor_scan(ex_t[:, 2, :], ones[0:TN, 0:NX], ex_t[:, 1, :], 0.0, ALU.mult, ALU.add))
            then(dve.tensor_tensor(ex_t[:, 3, :], ex_t[:, 2, :], ex_t[:, 1, :], ALU.subtract))
            then(dve.tensor_tensor(upto, upto, lg_s[:, 1], ALU.subtract))
            then(dve.tensor_tensor(upto, upto, bank[3][0:TN, 0:NT * NX].rearrange("p (t e) -> p t e", e=NX), ALU.add))
            then(dve.scalar_tensor_tensor(out=upto, in0=ex_t[:, 3, :].unsqueeze(1).broadcast_to([TN, NT, NX]), scalar=128.0,
                                          in1=upto, op0=ALU.mult, op1=ALU.add))
            for a in range(TOP):
                then(dve.tensor_tensor(hot[:, a], hot[:, a], upto, ALU.mult))
                then(dve.tensor_reduce(rt[:, a, :], hot[:, a], AX, ALU.add))
                link(dve.tensor_copy(row_of[:, a, :], rt[:, a, :]))
            link.wait()
            dve.sem_inc(s["placed"], 1)
            then(dve.tensor_tensor(step_x.rearrange("p (n e) -> p n e", e=NX), path_f[0:1, 0, 0:NM].unsqueeze(2).broadcast_to([1, NM, NX]),
                                   ex_t[0:1, 2, :].unsqueeze(1).broadcast_to([1, NM, NX]), ALU.is_ge))
            then(dve.tensor_reduce(step_f[:, :], step_x.rearrange("p (n e) -> p n e", e=NX), AX, ALU.add))
            then(dve.tensor_scalar(step_f[:, :], step_f[:, :], float(NX - 1), None, ALU.min))
            dve.tensor_copy(step_i[:, :], step_f[:, :]).then_inc(s["steps"], 1)
            dve.wait_ge(s["steps"], 1)
            dve.wait_ge(s["b_rows"], 32)
            dve.wait_ge(s["sent"], 16 * TOP * NT)

            for k in ("hb", "yb"):
                dve.sem_inc(s[k], 2)

            def add_b1(st, u, n):
                hold(dve, s["up"], st + 3)
                hold(dve, s["hg"], st + 1)
                dve.tensor_tensor(h_b[:, u], bank[2 + u][:, 0:D], b1_row[:, ds(step_expert(dve, st), 1), :].rearrange("p e n -> p (e n)"),
                                  ALU.add).then_inc(s["hb"], 1)

            def add_b2(st, u, n):
                hold(dve, s["down"], st + 3)
                if not isinstance(st, int) or n:
                    hold(dve, y_left[u], 16 * n)
                dve.tensor_tensor(y_b[:, u], bank[6 + u][:, 0:D], b2_row[:, ds(step_expert(dve, st), 1), :].rearrange("p e n -> p (e n)"),
                                  ALU.add).then_inc(s["yb"], 1)

            expert_steps(dve, [(1, add_b1), (-1, add_b2)])

            def add_back(t, u, count):
                hold(dve, y_arr[u], count)
                row = node_sum[:, ds(t, 1), :].rearrange("p t w -> p (t w)")
                link(dve.scalar_tensor_tensor(out=row, in0=y_in[:, u, 0, :], scalar=share[:, 0, ds(t, 1)], in1=row, op0=ALU.mult, op1=ALU.add))
                link.wait()
                dve.scalar_tensor_tensor(out=row, in0=y_in[:, u, 1, :], scalar=share[:, 1, ds(t, 1)], in1=row,
                                         op0=ALU.mult, op1=ALU.add).then_inc(s["acc"], 1)

            with dve.Fori(0, (NT - 2) // 4) as i:
                link.loop(i, 4)
                for u in range(4):
                    add_back(i * 4 + u, u, 32 * i + 32)
            link.close((NT - 2) // 4)
            for u in range(2):
                add_back(NT - 2 + u, u, 32 * ((NT - 2) // 4) + 32)

        @block.tensor
        def _(pe):
            def product(out_ap, pairs, sem_=None, **kw):
                for n, (w, m) in enumerate(pairs):
                    ins = pe.matmul(out_ap, w, m, start=n == 0, stop=n == len(pairs) - 1, skip_group_check=True)
                return ins

            pe.wait_ge(s["d0"], 1)
            product(bank[5][0:TN, 0:128], [(first_w[:, :], ident[:, :])]).then_inc(s["d0_bc"], 1)
            pe.wait_ge(s["wts"], WTS)
            pe.wait_ge(s["consts"], 1)
            for c in range(KC):
                ins = pe.transpose(bank[7][:, c * NX:(c + 1) * NX], rw_s[:, c * 128:(c + 1) * 128], ident[0:NX, 0:NX])
            ins.then_inc(s["rw_tp"], 1)
            pe.wait_ge(s["path_c"], 1)
            product(bank[6][:, 0:NSTEP], [(ones[0:NG, :], path_cmp[:, 1, :])]).then_inc(s["path_p"], 1)

            pe.wait_ge(s["part"], 1)
            pe.wait_ge(s["wlr"], 1)
            pe.wait_ge(s["rw_ev"], 1)
            pe.wait_ge(s["path_r"], 1)
            pe.sem_inc(s["tp"], 2)
            pe.sem_inc(s["lr"], 2)
            lr_ps = psum[0:TN, 4:8, :].rearrange("p b w -> p (b w)")
            with pe.Fori(0, NT // 2) as i:
                for u in range(2):
                    t = 2 * i + u
                    hold(pe, s["xs"], t + 1)
                    hold(pe, s["lr_x"], t + 1)
                    for c in range(KC):
                        ins = pe.transpose(bank[u][:, c * 128:c * 128 + TN], xs[:, u, c * 128:(c + 1) * 128], ident[0:TN, 0:TN])
                    ins.then_inc(s["tp"], 1)
                    hold(pe, s["xt"], t + 1)
                    product(lr_ps[:, ds(t * 2 * R * H, 2 * R * H)], [(xt[:, u, c, :], w_lr[:, c, :]) for c in range(KC)]).then_inc(s["lr"], 1)
            pe.wait_ge(s["first_up"], 1)
            product(bank[2][0:TN, 0:NT], [(shift[:, 0, :], first_at[:, 0:NT]), (shift[:, 1, :], first_at[:, 1:NT + 1])]).then_inc(s["shifted"], 1)
            pe.wait_ge(s["node_pos"], 1)
            pe.wait_ge(s["lr_ev"], 1)
            pe.wait_ge(s["lr_x"], NT + 2)
            for c in range(KC):
                ins = pe.matmul(bank[6 + c][:, 0:129], zeros[0:TN, 0:128], zeros[0:TN, 0:129], start=True, stop=False, skip_group_check=True)
            ins.then_inc(s["kvm"], 1)
            pe.wait_ge(s["kvm"], 1)
            pe.sem_inc(s["kvm"], 1)
            pe.sem_inc(s["f_pe"], 2)
            with pe.Fori(0, NT // 2) as i:
                for u in range(2):
                    t = 2 * i + u
                    hold(pe, s["f_xt"], t + 1)
                    hold(pe, s["vt"], t + 1)
                    hold(pe, s["kt"], t + 1)
                    product(bank[4 + u][0:TN, :], [(xt[:, u, c, :], wkv[:, c, :]) for c in range(KC)]).then_inc(s["f_kv"], 1)
                    hold(pe, s["f_act"], t + 1)
                    for n in range(2):
                        ins = product(bank[n][0:TN, :], [(xt[:, u, c, :], conv_w[:, c, n * 512:(n + 1) * 512]) for c in range(KC)])
                    ins.then_inc(s["f_pe01"], 1)
                    hold(pe, s["f_dve"], t + 1)
                    for n in range(2, 4):
                        ins = product(bank[n][0:TN, :], [(xt[:, u, c, :], conv_w[:, c, n * 512:(n + 1) * 512]) for c in range(KC)])
                    ins.then_inc(s["f_pe"], 1)
                    hold(pe, s["kt"], t + 3)
                    hold(pe, s["vt"], t + 3)
                    for c in range(KC):
                        ins = pe.matmul(bank[6 + c][:, 0:129], kt[:, u, c * 128:(c + 1) * 128], vt[:, u, c, :],
                                        start=False, stop=False, skip_group_check=True)
                    ins.then_inc(s["kvm"], 1)
            for c in range(KC):
                ins = pe.matmul(bank[6 + c][:, 0:129], zeros[0:TN, 0:128], zeros[0:TN, 0:129], start=False, stop=True, skip_group_check=True)
            ins.then_inc(s["kvm"], 1)
            pe.wait_ge(s["f_act"], NT + 1)
            pe.wait_ge(s["f_dve"], NT + 1)
            pe.wait_ge(s["kv_ready"], 1)

            def span(k):
                return slice(k * SN, (k + 1) * SN) if isinstance(k, int) else ds(k * SN, SN)

            def q_products(k):
                for o in range(KC):
                    ins = product(bank[o][:, 0:SN], [(wqm[:, 0, c, o * 128:(o + 1) * 128], xnT[:, c, span(k)]) for c in range(KC)])
                ins.then_inc(s["q"], 1)

            def sums(k):
                hold(pe, s["q_t"], k + 1)
                for c in range(KC):
                    product(bank[2 + c][:, 0:SN], [(kv_m[:, c, :], qt[:, 2, c, :])])
                    ins = product(bank[c][:, 0:SN], [(ks_m[:, c, :], qt[:, 2, c, :])])
                ins.then_inc(s["nd"], 1)

            def merge(k):
                hold(pe, s["msg"], k + 1)
                for j in range(SJ):
                    ins = product(bank[2 + j // 2][0:TN, (j % 2) * D:(j % 2 + 1) * D],
                                  [(msgT[:, c, j * TN:(j + 1) * TN], wqm[:, 1, c, :]) for c in range(KC)])
                ins.then_inc(s["m"], 1)

            def turn_message(k):
                hold(pe, s["ms"], k + 1)
                for j in range(SJ):
                    for c in range(KC):
                        ins = pe.transpose(bank[4 + c][:, j * TN:(j + 1) * TN], ms[:, j, c * 128:(c + 1) * 128], ident[0:TN, 0:TN])
                ins.then_inc(s["tpm"], 1)

            def hidden(k):
                hold(pe, s["msT"], KC * k + KC)
                hold(pe, s["h2_done"], k + 1)
                for o, b, done in ((0, 6, s["h1a"]), (2, 4, s["h1b"])):
                    for n in range(2):
                        cols = slice((o + n) * 128, (o + n + 1) * 128)
                        ins = product(bank[b + n][:, 0:SN], [(w1_s[:, c, cols], xnT[:, c, span(k)]) for c in range(KC)]
                                      + [(w1_s[:, KC + c, cols], msT[:, c, :]) for c in range(KC)])
                    ins.then_inc(done, 1)

            def output(k):
                hold(pe, s["h_act"], 2 * k + 2)
                for j in range(SJ):
                    ins = product(bank[6 + j // 2][0:TN, (j % 2) * D:(j % 2 + 1) * D],
                                  [(hT[:, c, j * TN:(j + 1) * TN], w2_s[:, c, :]) for c in range(2 * KC)])
                ins.then_inc(s["h2"], 1)

            def q_turn(k):
                q_products(k + 1)
                turn_message(k)
                sums(k + 1)
                hidden(k)
                merge(k + 1)
                output(k)

            q_products(0)
            sums(0)
            merge(0)
            with pe.Fori(0, NS - 2) as k:
                q_turn(k)
            q_turn(NS - 2)
            turn_message(NS - 1)
            hidden(NS - 1)
            output(NS - 1)
            for back in range(2):
                pe.wait_ge(s["a_tail"], back + 1)
                for n in range(2):
                    ins = pe.transpose(bank[0][0:H, n * 128:(n + 1) * 128], tailf[:, n, :], ident[:, :])
                ins.then_inc(s["a_tp"], 1)
                pe.wait_ge(s["a_row"], back + 1)
                row = carry[:, 2:130] if back else carry[:, 0:128]
                pe.transpose(bank[1][:, 0:H], row, ident[0:H, 0:H]).then_inc(s["a_tpb"], 1)
            pe.wait_ge(s["a_sub"], 1)
            pe.wait_ge(s["h2_done"], NS + 1)
            product(bank[U - 1][0:TN, 0:132], [(zeros[:, 0:TN], zeros[:, 0:132])])
            product(bank[U - 1][0:TN, 132:W], [(zeros[:, 0:TN], zeros[:, 0:W - 132])]).then_inc(s["slot"], 1)
            pe.wait_ge(s["slot"], 1)
            pe.sem_inc(s["slot"], U - 1)
            with pe.Fori(0, NSTEP // U) as i:
                for u in range(U):
                    st = U * i + u
                    hold(pe, s["oh"], st + U + 1)
                    hold(pe, s["agg_ev"], st + 1)
                    product(bank[u][0:TN, 0:W], [(onehot[:, u, j, :], ring[:, u, j, :]) for j in range(GJ)]).then_inc(s["slot"], 1)
            pe.wait_ge(s["agg_ev"], NSTEP + 3)
            pe.sem_inc(s["x2tp"], 1)
            pe.sem_inc(s["lg"], 1)
            with pe.Fori(0, NS) as k:
                hold(pe, s["x2n"], k + 1)
                hold(pe, s["x2T"], k + 1)
                for j in range(SJ):
                    for c in range(KC):
                        ins = pe.transpose(bank[c][:, j * TN:(j + 1) * TN], ms[:, j, c * 128:(c + 1) * 128], ident[0:TN, 0:TN])
                ins.then_inc(s["x2tp"], 1)
                hold(pe, s["x2T"], k + 2)
                for j in range(SJ):
                    ins = product(bank[2][0:TN, ds((k * SJ + j) * NX, NX)], [(msT[:, c, j * TN:(j + 1) * TN], rwT[:, c, :]) for c in range(KC)])
                ins.then_inc(s["lg"], 1)
            pe.wait_ge(s["picked"], 1)
            picks = lg_s[:, 4].rearrange("p t e -> p (t e)")
            product(bank[3][0:TN, 0:NT * NX], [(tri[:, :], picks)])
            product(bank[3][0:TN, NT * NX:2 * NT * NX], [(ones[0:TN, 0:TN], picks)]).then_inc(s["ranked"], 1)
            pe.wait_ge(s["steps"], 1)
            pe.wait_ge(s["moe1"], 16)
            for k in ("up", "htp", "down"):
                pe.sem_inc(s[k], 2)

            def turn_x(st, u, n):
                hold(pe, x_arr[u], 16 * n + 16)
                hold(pe, s["xtc"], st + 1)
                for c in range(KC):
                    ins = pe.transpose(bank[u][:, c * 128:(c + 1) * 128], x_in[:, u, c * 128:(c + 1) * 128], ident[:, :])
                ins.then_inc(s["xtp"], 1)

            def up(st, u, n):
                hold(pe, s["xtc"], st + 3)
                hold(pe, s["hb"], st + 1)
                e = step_expert(pe, st)
                product(bank[2 + u][:, 0:D], [(x_T[:, u, c * 128:(c + 1) * 128], mw1_s[:, ds(e, 1), c, :].rearrange("p e n -> p (e n)"))
                                              for c in range(KC)]).then_inc(s["up"], 1)

            def turn_h(st, u, n):
                hold(pe, s["hg"], st + 3)
                hold(pe, s["htc"], st + 1)
                for c in range(KC):
                    ins = pe.transpose(bank[4 + u][:, c * 128:(c + 1) * 128], h_g[:, u, c * 128:(c + 1) * 128], ident[:, :])
                ins.then_inc(s["htp"], 1)

            def down(st, u, n):
                hold(pe, s["htc"], st + 3)
                hold(pe, s["yb"], st + 1)
                e = step_expert(pe, st)
                product(bank[6 + u][:, 0:D], [(h_T[:, u, c * 128:(c + 1) * 128], mw2_s[:, ds(e, 1), c, :].rearrange("p e n -> p (e n)"))
                                              for c in range(KC)]).then_inc(s["down"], 1)

            expert_steps(pe, [(2, turn_x), (1, up), (0, turn_h), (-1, down)])


_INS = {"x": "x", "conv": "L0_gnn_conv_weights", "attn_l": "L0_gnn_attn_l", "attn_r": "L0_gnn_attn_r",
        "h_bias": "L0_gnn_h_bias", "Wq": "L0_mix_Wq", "Wk": "L0_mix_Wk", "Wv": "L0_mix_Wv", "Wm": "L0_mix_Wm",
        "W1": "L0_mix_W1", "W2": "L0_mix_W2", "g1": "L0_mix_g1", "b1": "L0_mix_b1", "g2": "L0_mix_g2",
        "b2": "L0_mix_b2", "router": "L0_ffn_router_w", "mw1": "L0_ffn_w1", "mb1": "L0_ffn_b1",
        "mw2": "L0_ffn_w2", "mb2": "L0_ffn_b2"}


def kernel(**inputs):
    import numpy as _np
    import concourse.bacc as _bacc
    from concourse import mybir as _mybir
    from concourse.bass_utils import run_bass_kernel_spmd as _run

    nc = _bacc.Bacc("TRN2", target_bir_lowering=False, num_devices=1)
    arrays = {name: _np.ascontiguousarray(inputs[key]) for name, key in _INS.items()}
    dst, src, typ = (_np.asarray(inputs[k]) for k in ("dst", "src", "edge_type_8"))
    pad = EP - E
    arrays["dst_ext"] = _np.concatenate([_np.full(1, -1, dst.dtype), dst, _np.full(pad, N, dst.dtype), _np.full(1, N + 1, dst.dtype)])
    arrays["src_pad"] = _np.concatenate([src, _np.zeros(pad, src.dtype)])
    arrays["type_pad"] = _np.concatenate([typ, _np.zeros(pad, typ.dtype)])
    args = {k: nc.dram_tensor(f"in_{k}", a.shape, _mybir.dt.from_np(a.dtype), kind="ExternalInput").ap() for k, a in arrays.items()}
    args["out"] = nc.dram_tensor("out_0", (N, D), F32, kind="ExternalOutput").ap()
    for name, shape in (("feat_t", (N, RF)), ("l_t", (N, R * H)), ("r_t", (N, R * H)), ("rec_t", (EP, 2 + H)),
                        ("dst_t", (EP,)), ("run_t", (EP + N, R * H)),
                        ("xs_t", (NM * 128, D)), ("ys_t", (NM * 128, D))):
        args[name] = nc.dram_tensor(name, shape, F32).ap()
    build(nc, **args)
    r = _run(nc, [{f"in_{k}": a for k, a in arrays.items()}], core_ids=[0])
    return r.results[0]["out_0"]
```

```python
from contextlib import ExitStack

import concourse.bass as bass
from concourse import mybir

ALU = mybir.AluOpType
ACT = mybir.ActivationFunctionType
AX = mybir.AxisListType.X
F32 = mybir.dt.float32
I32 = mybir.dt.int32
ds = bass.ds

N, D, R, H, E = 3750, 256, 8, 4, 60000
HD = D // H
RF = R * D
TN = 125
NT = N // TN
SJ = 3
SN = SJ * TN
NS = N // SN
GE, GJ = 512, 4
NG = -(-E // GE)
EP = NG * GE
EC = EP // 128
NSTEP = NG + NT - 1
NX = 8
TOP = 2
NM = (TOP * N + NX * 127) // 128
assert NM % 2 == 0
KC = D // 128
AH = 32
HW = 128 + 128 // AH
LN_EPS, ATT_EPS = 1e-5, 1e-6
BIG = 1e38
XW = D + 2
W = D + H
U = 3
GR = 4
AD = 2
GC = 8
RQ = NS - 2
EQ = EC // RQ
FS = 3
ZQ = 4
assert N % SN == 0 and EC % (2 * GC) == GC and EC % RQ == 0 and EC % ZQ == 0 and NSTEP % U == 0 and NT % (2 * FS) == 0 and GR * GJ * D <= 2 * RF


class Link:

    def __init__(self, eng, sem):
        self.eng, self.sem, self.base, self.count = eng, sem, 0, 0

    def __call__(self, ins):
        ins.then_inc(self.sem, 1)
        self.count += 1
        return ins

    def wait(self):
        hold(self.eng, self.sem, self.base + self.count)

    def loop(self, trip, per):
        self.per, self.outer = per, self.count
        self.base, self.count = trip * per + self.count, 0

    def close(self, trips):
        assert self.count == self.per, (self.count, self.per)
        self.base, self.count = 0, self.outer + trips * self.per


def hold(eng, sem, value):
    eng.wait_ge(sem, value)
    if not isinstance(value, int):
        eng.nop(nofuse=True)


def build(nc, x, dst_ext, src_pad, type_pad, conv, attn_l, attn_r, h_bias, Wq, Wk, Wv, Wm, W1, W2,
          g1, b1, g2, b2, router, mw1, mb1, mw2, mb2,
          out, feat_t, l_t, r_t, rec_t, dst_t, run_t, xs_t):
    with ExitStack() as ctx:
        def sb(name, shape, dt=F32):
            return ctx.enter_context(nc.sbuf_tensor(name, shape, dt))

        def sem(name):
            return ctx.enter_context(nc.semaphore(name))

        psum = ctx.enter_context(nc.psum_tensor("psum", [128, 8, 512], F32))
        bank = [psum[:, i, :] for i in range(8)]

        node_sum = sb("node_sum", [TN, NT, D])
        arena_n = sb("arena_n", [128, NT * W])
        xnT = arena_n[:, 0:KC * N].rearrange("p (c n) -> p c n", c=KC)
        edge_sum = arena_n[0:TN, :].rearrange("p (t w) -> p t w", w=W)
        arena_h = sb("arena_h", [128, 3 * KC * SN])
        arena_w = sb("arena_w", [128, KC * RF])
        conv_w = arena_w[:, :].rearrange("p (c w) -> p c w", c=KC)
        mw1_s = arena_w[:, :].rearrange("p (e c w) -> p e c w", e=NX, c=KC)
        arena_f = sb("arena_f", [128, 2 * RF])
        attn_b = arena_f[:, 0:RF]
        prod = arena_f[:, RF:2 * RF]
        feat_s = arena_f[0:TN, :].rearrange("p (u w) -> p u w", u=2)
        r_part = arena_f[:, 0:EQ * R * H].rearrange("p (k g) -> p k g", g=R * H)
        is_type = arena_w[:, 0:EQ * R].rearrange("p (k r) -> p k r", r=R)
        attn_rb = arena_h[:, 0:RF]
        ring = arena_f[:, 0:GR * GJ * D].rearrange("p (u w) -> p u w", u=GR)
        weighted = arena_w[:, 0:U * GJ * W].rearrange("p (u j w) -> p u j w", u=U, j=GJ)
        mw2_s = sb("mw2_s", [128, NX, KC, D])
        zero_w = mw2_s[:, :, :, :].rearrange("p e c n -> p (e c n)")[:, 0:EC // ZQ * R * H]
        wqm = sb("wqm", [128, 2, KC, D])
        wkv = sb("wkv", [128, KC, 2 * D])
        w1_s = sb("w1_s", [128, 4, 2 * D])
        w2_s = sb("w2_s", [128, 4, D])
        w_lr = sb("w_lr", [128, KC, 2 * R * H])
        rw_s = sb("rw_s", [NX, D])
        rwT = sb("rwT", [128, KC, NX])
        colv = sb("colv", [128, 2 * KC])
        hb_b2 = sb("hb_b2", [TN, 2, D])
        g2_b = sb("g2_b", [TN, D])
        b1_row = arena_f[:, 0:NX * D].rearrange("p (e n) -> p e n", e=NX)
        b2_row = arena_f[:, NX * D:2 * NX * D].rearrange("p (e n) -> p e n", e=NX)
        ident = sb("ident", [128, 128])
        mask = sb("mask", [128, 128])
        pad_row = sb("pad_row", [128, XW])
        zeros = pad_row[:, 0:132]
        stats = sb("stats", [TN, NT, 6])
        mv = sb("mv", [TN, NT, 2])
        rstd = sb("rstd", [TN, NT, 1])
        xs = sb("xs", [TN, 2, D])
        xt = sb("xt", [128, 2, KC, TN])
        src_a = sb("src_a", [128, EC], I32)
        typ_a = sb("typ_a", [128, EC], I32)
        dst_f = sb("dst_f", [128, EC])
        first_i = sb("first_i", [128, 1], I32)
        first_w = sb("first_w", [128, TN])
        node_id = sb("node_id", [TN, NT])
        part_of = sb("part_of", [TN, NT])
        part_i = sb("part_i", [TN, NT], I32)
        below = sb("below", [TN, NT])
        first_at = sb("first_at", [TN, NT + 1])
        node_at = sb("node_at", [TN, NT])
        node_at_i = sb("node_at_i", [TN, NT], I32)
        shift = sb("shift", [TN, 2, TN])
        keep = sb("keep", [128, EC])
        r_first = sb("r_first", [128, R * H])
        rec = sb("rec", [128, EC, 2 + H])
        rec_idx = rec[:, :, 0].bitcast(I32)
        new_run = sb("new_run", [128, EC])
        end_run = sb("end_run", [128, EC])
        typ_f = src_a[:, :].bitcast(F32)
        run_max = sb("run_max", [128, EC, H])
        dst3 = run_max[:, :, :].rearrange("p k h -> p (k h)")[:, 0:3 * EC].rearrange("p (m k) -> p m k", m=3).bitcast(I32)
        idx_st = sb("idx_st", [128, 2, GC], I32)
        l_ring = sb("l_ring", [128, 2, GC, H])
        tailf = sb("tailf", [128, 2, H])
        rowf = sb("rowf", [H, 2, 128])
        carry = sb("carry", [H, 130])
        cin = sb("cin", [128, H])
        arena_q = sb("arena_q", [128, 2 * KC * SN + SJ * D])
        qt = arena_q[:, 0:2 * KC * SN].rearrange("p (a c n) -> p a c n", a=2, c=KC)
        msg_n = arena_q[0:TN, 2 * KC * SN:]
        found = arena_q[0:TN, 0:FS * EC].rearrange("p (u k) -> p u k", u=FS)
        mk, ek, kt = (arena_q[0:TN, n * 2 * D:(n + 1) * 2 * D].rearrange("p (u d) -> p u d", u=2) for n in range(3))
        vt = arena_q[0:TN, 6 * D:6 * D + 4 * 129].rearrange("p (u c n) -> p u c n", u=2, c=KC)
        onehot = arena_q[:, 0:U * GJ * TN].rearrange("p (u j n) -> p u j n", u=U, j=GJ)
        kv_m = sb("kv_m", [128, KC, HW])
        den_r = sb("den_r", [TN, KC * SJ, 128 // AH])
        msgT = sb("msgT", [128, KC, SN])
        ms = sb("ms", [TN, SJ, D])
        hT = arena_h[:, 0:2 * KC * SN].rearrange("p (c n) -> p c n", c=2 * KC)
        msT = arena_h[:, 2 * KC * SN:].rearrange("p (c n) -> p c n", c=KC)
        lr_s = arena_h[0:TN, 0:NT * 2 * R * H].rearrange("p (t w) -> p t w", t=NT)
        st2 = sb("st2", [TN, SJ, 6])
        mv2 = sb("mv2", [TN, SJ, 2])
        sd2 = sb("sd2", [TN, SJ, 1])
        last_i = sb("last_i", [NG, 1], I32)
        last_f = sb("last_f", [NG, 2])
        thr = sb("thr", [NG, NT - 1])
        path_cmp = sb("path_cmp", [NG, 2, NSTEP])
        ones = sb("ones", [128, 128])
        path_f = sb("path_f", [128, 3, NSTEP])
        path_i = sb("path_i", [1, 2, NSTEP + AD], I32)
        end_i = sb("end_i", [1, NG], I32)
        rec_b = sb("rec_b", [128, GR, GJ, 2 + H])
        dst_rel = sb("dst_rel", [128, U, GJ])
        iota_n = sb("iota_n", [128, 128])
        eps_t = sb("eps_t", [128, 1])
        tmp_t = sb("tmp_t", [TN, 2, NT])
        lg_s = arena_q[0:TN, 0:5 * NT * NX].rearrange("p (a t e) -> p a t e", a=5, t=NT)
        hot = arena_q[0:TN, 5 * NT * NX:7 * NT * NX].rearrange("p (a t e) -> p a t e", a=TOP, t=NT)
        rt = sb("rt", [TN, 6, NT])
        share = sb("share", [TN, TOP, NT])
        row_of = sb("row_of", [TN, TOP, NT], I32)
        tri = sb("tri", [TN, TN])
        ex_t = sb("ex_t", [TN, 4, NX])
        step_x = arena_q[0:1, 7 * NT * NX:7 * NT * NX + NM * NX]
        step_f = path_f[0:1, 1, 0:NM]
        step_i = sb("step_i", [1, NM], I32)
        x_in = arena_n[:, 0:2 * XW].rearrange("p (u d) -> p u d", u=2)
        x_T, h_b, h_g, h_T, y_b = (arena_n[:, 2 * (XW + n * D):2 * (XW + (n + 1) * D)].rearrange("p (u d) -> p u d", u=2)
                                   for n in range(5))
        meta = arena_q[:, 0:2 * NM].rearrange("p (s a) -> p s a", a=2)

        s = {k: sem("s_" + k) for k in (
            "x wts conv attn edges last rw moe consts dve act pool stats std xs tp lr_x xt lr lr_ev lr_out "
            "wlr zeroed run_z dst_out d0 d0_bc part found0 found1 found2 found_ev first_up shifted node_pos scat r_first_in "
            "r_load r_sel f_xt f_kv f_pe01 f_pe f_act f_dve f_out stored kvm mk ek kt vt kv_ready q "
            "q_ex q_t nd msg tmsg msgT m ms_var ms_sd ms tpm msT h1a h1b h_act h2 h2_var h2_sd h2_done idx gath0 gath1 gath_use "
            "a_tail a_tp a_row a_tpb a_sub a_ex rec_out path_c path_p path_r rec_in0 rec_in1 rec_in2 rec_in3 row_in0 "
            "row_in1 row_in2 row_in3 rows_in slot oh agg_ev rw_tp rw_ev x2_var x2_sd x2n x2tp x2T lg lg_x lg_ex picked ranked placed steps "
            "xs_z sent share1 b_rows x_in0 x_in1 xtp xtc up hb hg htp htc down mc ya yb added outd").split()}
        rec_in = [s["rec_in0"], s["rec_in1"], s["rec_in2"], s["rec_in3"]]
        row_in = [s["row_in0"], s["row_in1"], s["row_in2"], s["row_in3"]]
        gath = [s["gath0"], s["gath1"]]

        x_v = x.rearrange("(t p) d -> p t d", p=TN)
        out_v = out[0:N].rearrange("(t p) d -> p t d", p=TN)
        feat_v = feat_t.rearrange("(t p) w -> p t w", p=TN)
        feat_rows = feat_t.rearrange("n (r d) -> (n r) d", r=R)
        l_rows = l_t.rearrange("n (r h) -> (n r) h", h=H)
        run_q = run_t[0:EP, :].rearrange("(p k) w -> p (k w)", p=128)
        found_in = [s["found0"], s["found1"], s["found2"]]
        right = run_max[:, :, :]
        rec_g = rec_t.rearrange("(g q j) w -> g q (j w)", g=NG, j=GJ)
        logits = rec[:, :, 2:2 + H]
        x_rows = xs_t.rearrange("(s p) d -> s p d", p=128)
        x_arr = [s["x_in0"], s["x_in1"]]
        WTS = 16 * 11

        def bcast(v, parts):
            return v.rearrange("(a n) -> a n", a=1).broadcast_to([parts, v.shape[0]])

        def expert_steps(eng, stages):
            first = 3
            last = NM - 3
            assert (last - first) % 2 == 0

            def turn(i):
                for lead, f in stages:
                    if 0 <= i + lead < NM:
                        f(i + lead, (i + lead) % 2, (i + lead) // 2)

            for i in range(-2, first):
                turn(i)
            with eng.Fori(0, (last - first) // 2) as m:
                for v in range(first, first + 2):
                    for lead, f in stages:
                        f(2 * m + (v + lead), (v + lead) % 2, m + (v + lead) // 2)
            for i in range(last, NM + 1):
                turn(i)

        def by_group(eng, first, f):
            base, turns = first // GR, (NG - first) // GR
            with eng.Fori(0, turns) as i:
                for u in range(GR):
                    f(GR * i + (first + u), u, i + base)
            for g in range(first + turns * GR, NG):
                f(g, g % GR, g // GR)

        def step_expert(eng, st):
            at = slice(st, st + 1) if isinstance(st, int) else ds(st, 1)
            return eng.value_load(step_i[0:1, at], min_val=0, max_val=NX - 1)

        block = ctx.enter_context(nc.Block())

        @block.sync
        def _(sp):
            for m in range(3):
                sp.dma_start(dst3[:, m, :], dst_ext[m:m + EP].rearrange("(p k) -> p k", p=128)).then_inc(s["edges"], 16)
            sp.dma_start(src_a[:, :], src_pad.rearrange("(p k) -> p k", p=128)).then_inc(s["edges"], 16)
            sp.dma_start(typ_a[:, :], type_pad.rearrange("(p k) -> p k", p=128)).then_inc(s["edges"], 16)
            with nc.allow_non_contiguous_dma(reason="one destination of each group"):
                sp.dma_start(last_i[:, :], dst_ext[1:1 + EP].rearrange("(g k) -> g k", g=NG)[:, GE - 1:GE]).then_inc(s["last"], 16)
            sp.dma_start(rw_s[:, :], router).then_inc(s["rw"], 16)
            for c in range(KC):
                sp.dma_start(conv_w[:, c, :].rearrange("p (g d) -> p g d", d=HD),
                             conv.rearrange("r h i d -> i (r h) d")[c * 128:(c + 1) * 128]).then_inc(s["conv"], 16)
            sp.dma_start(attn_b, bcast(attn_l.rearrange("r h d -> (r h d)"), 128)).then_inc(s["attn"], 16)
            sp.dma_start(attn_rb, bcast(attn_r.rearrange("r h d -> (r h d)"), 128)).then_inc(s["attn"], 16)
            sp.dma_start(node_sum[:, :, :], x_v).then_inc(s["x"], 16)
            sp.wait_ge(s["d0"], 1)
            sp.dma_start(dst_t.rearrange("(p k) -> p k", p=128), dst_f[:, :]).then_inc(s["dst_out"], 16)
            for n, w in ((0, Wq), (1, Wm)):
                sp.dma_start(wqm[:, n], w.rearrange("(c p) n -> p c n", p=128)).then_inc(s["wts"], 16)
            for n, w in ((0, Wk), (1, Wv)):
                sp.dma_start(wkv[:, :, n * D:(n + 1) * D], w.rearrange("(c p) n -> p c n", p=128)).then_inc(s["wts"], 16)
            sp.dma_start(w1_s[:, :, :], W1.rearrange("(c p) n -> p c n", p=128)).then_inc(s["wts"], 16)
            sp.dma_start(w2_s[:, :, :], W2.rearrange("(c p) n -> p c n", p=128)).then_inc(s["wts"], 16)
            sp.dma_start(hb_b2[:, 0, :], bcast(h_bias, TN)).then_inc(s["wts"], 16)
            sp.dma_start(hb_b2[:, 1, :], bcast(b2, TN)).then_inc(s["wts"], 16)
            sp.dma_start(g2_b[:, :], bcast(g2, TN)).then_inc(s["wts"], 16)
            with nc.allow_non_contiguous_dma(reason="vectors laid out by feature on the partitions"):
                for n, v in ((0, g1), (1, b1)):
                    sp.dma_start(colv[:, n * KC:(n + 1) * KC], v.rearrange("(c p) -> p c", p=128)).then_inc(s["wts"], 16)
            sp.wait_ge(s["zeroed"], 1)
            for q in range(ZQ):
                w = EC // ZQ * R * H
                sp.dma_start(run_q[:, q * w:(q + 1) * w], zero_w).then_inc(s["run_z"], 16)
            sp.wait_ge(s["lr_ev"], 1)
            sp.dma_start(l_t.rearrange("(t p) w -> p t w", p=TN), lr_s[:, :, 0:R * H]).then_inc(s["lr_out"], 16)
            sp.dma_start(r_t.rearrange("(t p) w -> p t w", p=TN), lr_s[:, :, R * H:2 * R * H]).then_inc(s["lr_out"], 16)
            sp.wait_ge(s["run_z"], 16 * ZQ)
            sp.dma_start(mw2_s[:, :, :, :].rearrange("p e c n -> p (e c) n"),
                         mw2.rearrange("e (c p) n -> p (e c) n", p=128)).then_inc(s["moe"], 16)
            sp.sem_inc(s["stored"], 2)
            with sp.Fori(0, NT // 2) as i:
                for u in range(2):
                    t = 2 * i + u
                    hold(sp, s["f_act"], t + 2)
                    hold(sp, s["f_dve"], t + 2)
                    sp.dma_start(feat_v[:, ds(t, 1), :].rearrange("p t w -> p (t w)"), feat_s[:, u, :]).then_inc(s["f_out"], 16)
                    hold(sp, s["f_out"], 16 * (t + 1))
                    sp.sem_inc(s["stored"], 1)
            for n in range(2):
                half = slice(n * NM // 2, (n + 1) * NM // 2)
                sp.dma_start(xs_t.rearrange("(s p) w -> p s w", p=128)[:, half, :],
                             pad_row[:, :].unsqueeze(1).broadcast_to([128, NM // 2, XW])).then_inc(s["xs_z"], 16)
            sp.wait_ge(s["f_pe"], NT + 2)
            sp.wait_ge(s["scat"], 16 * NT)
            with sp.Fori(0, RQ) as q:
                hold(sp, s["r_sel"], q + 1)
                sp.dma_start(r_part.rearrange("p k g -> p (k g)"), run_q[:, ds(q * EQ * R * H, EQ * R * H)]).then_inc(s["r_load"], 16)
            sp.wait_ge(s["r_sel"], RQ + 1)
            sp.wait_ge(s["a_ex"], 1)
            sp.dma_start(rec_t.rearrange("(p k) w -> p (k w)", p=128), rec[:, :, :].rearrange("p k w -> p (k w)")).then_inc(s["rec_out"], 16)
            sp.wait_ge(s["rec_out"], 16)
            sp.wait_ge(s["path_r"], 1)

            def load_record(g, u, n):
                at = slice(g, g + 1) if isinstance(g, int) else ds(g, 1)
                sp.dma_start(rec_b[:, u].rearrange("p j w -> p (j w)"), rec_g[at].rearrange("g q w -> (g q) w")).then_inc(rec_in[u], 16)

            def next_record(g, u, n):
                before = slice(g - GR, g - GR + 1) if isinstance(g, int) else ds(g - GR, 1)
                end = sp.value_load(end_i[0:1, before], min_val=1, max_val=NSTEP)
                hold(sp, s["oh"], 2 * end + 2 * U)
                load_record(g, u, n)

            for g in range(GR):
                load_record(g, g, 0)
            by_group(sp, GR, next_record)
            sp.wait_ge(s["slot"], NSTEP + U)
            sp.dma_start(b1_row.rearrange("p e n -> p (e n)"), bcast(mb1.rearrange("e n -> (e n)"), 128)).then_inc(s["b_rows"], 16)
            sp.dma_start(b2_row.rearrange("p e n -> p (e n)"), bcast(mb2.rearrange("e n -> (e n)"), 128)).then_inc(s["b_rows"], 16)
            sp.dma_start(mw1_s.rearrange("p e c n -> p (e c) n"), mw1.rearrange("e (c p) n -> p (e c) n", p=128)).then_inc(s["moe"], 16)
            sp.wait_ge(s["picked"], 1)
            sp.dma_start(out_v, node_sum[:, :, :]).then_inc(s["outd"], 16)
            sp.dma_start(out[N:N + 128], pad_row[:, 0:D]).then_inc(s["outd"], 16)
            sp.wait_ge(s["sent"], 16 * TOP * NT)
            for st in range(2):
                sp.dma_start(x_in[:, st], x_rows[st]).then_inc(x_arr[st], 16)
            with sp.Fori(0, NM // 2 - 1) as i:
                for u in range(2):
                    hold(sp, s["xtp"], 2 * i + u + 1)
                    hold(sp, s["mc"], 2 * i + u + 1)
                    sp.dma_start(x_in[:, u], x_rows[ds(2 * i + u + 2, 1)].rearrange("s p d -> (s p) d")).then_inc(x_arr[u], 16)

        @block.gpsimd
        def _(pool):
            link = Link(pool, s["pool"])
            link(pool.memset(ident[:, :], 0.0))
            link(pool.memset(ones[:, :], 1.0))
            link(pool.memset(pad_row[:, :], 0.0))
            link(pool.memset(eps_t[:, :], LN_EPS))
            link(pool.memset(vt[:, :, :, 128:129], 1.0))
            for tile, step, base, mul in ((iota_n[:, :], 1, 0, 0), (thr[:, :], TN, TN, 0), (path_cmp[:, 0, :], 1, 0, 0),
                                          (path_f[:, 0, :], 1, 0, 0), (last_f[:, 0:1], 0, 1, 1), (node_id[:, :], TN, 0, 1)):
                link(pool.iota(tile, pattern=[[step, tile.shape[1]]], base=base, channel_multiplier=mul,
                               allow_small_or_imprecise_dtypes=True))
            link.wait()
            link(pool.iota(pad_row[:, D + 1:D + 2], pattern=[[0, 1]], base=N, channel_multiplier=1,
                           allow_small_or_imprecise_dtypes=True))
            link(pool.affine_select(out=ident[:, :], in_=ident[:, :], compare_op=ALU.not_equal, fill=1.0,
                                    base=0, pattern=[[-1, 128]], channel_multiplier=1))
            link(pool.affine_select(out=shift[:, 0, :], in_=zeros[0:TN, 0:TN], compare_op=ALU.not_equal, fill=1.0,
                                    base=-1, pattern=[[-1, TN]], channel_multiplier=1))
            link(pool.affine_select(out=shift[:, 1, :], in_=zeros[0:TN, 0:TN], compare_op=ALU.not_equal, fill=1.0,
                                    base=TN - 1, pattern=[[-1, TN]], channel_multiplier=TN))
            link(pool.affine_select(out=tri[:, :], in_=ones[0:TN, 0:TN], compare_op=ALU.is_gt, fill=0.0,
                                    base=0, pattern=[[1, TN]], channel_multiplier=-1))
            link(pool.affine_select(out=mask[:, :], in_=ones[:, :], compare_op=ALU.is_ge, fill=0.0,
                                    base=0, pattern=[[-AH, 128 // AH], [0, AH]], channel_multiplier=1))
            link.wait()
            pool.affine_select(out=mask[:, :], in_=mask[:, :], compare_op=ALU.is_ge, fill=0.0,
                               base=AH - 1, pattern=[[AH, 128 // AH], [0, AH]], channel_multiplier=-1).then_inc(s["consts"], 1)

            pool.wait_ge(s["part"], 1)
            pool.wait_ge(s["dst_out"], 16)
            for t in range(NT):
                if t >= FS:
                    pool.wait_ge(s["found_ev"], t - FS + 1)
                pool.indirect_dma_start(out=found[:, t % FS, :], out_offset=None, in_=dst_t.rearrange("(p k) -> p k", p=128),
                                        in_offset=bass.IndirectOffsetOnAxis(ap=part_i[:, t:t + 1], axis=0)).then_inc(found_in[t % FS], 16)
            pool.wait_ge(s["idx"], 1)
            pool.wait_ge(s["lr_out"], 32)

            def keep_rows(u, col, times):
                hold(pool, gath[u], times * (GC * 16))
                link(pool.tensor_copy(logits[:, ds(col, GC), :], l_ring[:, u]))

            def ask(u, col):
                link(pool.tensor_copy(idx_st[:, u, :], rec_idx[:, ds(col, GC)]))
                link.wait()
                for c in range(GC):
                    pool.indirect_dma_start(out=l_ring[:, u, c, :], out_offset=None, in_=l_rows,
                                            in_offset=bass.IndirectOffsetOnAxis(ap=idx_st[:, u, c:c + 1], axis=0),
                                            ).then_inc(gath[u], 16)

            turns = EC // (2 * GC) - 1
            for u in range(2):
                ask(u, u * GC)
            pool.wait_ge(s["node_pos"], 1)
            pool.wait_ge(s["run_z"], 16 * ZQ)
            for t in range(NT):
                pool.indirect_dma_start(out=run_t, out_offset=bass.IndirectOffsetOnAxis(ap=node_at_i[:, t:t + 1], axis=0),
                                        in_=lr_s[:, t, R * H:2 * R * H], in_offset=None).then_inc(s["scat"], 16)
            pool.indirect_dma_start(out=r_first[:, :], out_offset=None, in_=r_t,
                                    in_offset=bass.IndirectOffsetOnAxis(ap=first_i[:, 0:1], axis=0)).then_inc(s["r_first_in"], 16)
            with pool.Fori(0, turns) as i:
                link.loop(i, 4)
                for u in range(2):
                    keep_rows(u, 2 * GC * i + u * GC, i + 1)
                    ask(u, 2 * GC * i + (u + 2) * GC)
            link.close(turns)
            keep_rows(0, 2 * GC * turns, turns + 1)
            ask(0, 2 * GC * turns + 2 * GC)
            keep_rows(1, 2 * GC * turns + GC, turns + 1)
            keep_rows(0, 2 * GC * turns + 2 * GC, turns + 2)
            link.wait()
            pool.sem_inc(s["gath_use"], 1)

            pool.wait_ge(s["f_out"], 16 * NT)

            def gather_rows(g, u, n):
                hold(pool, rec_in[u], 16 * n + 16)
                for j in range(GJ):
                    pool.indirect_dma_start(out=ring[:, u, j * D:(j + 1) * D], out_offset=None, in_=feat_rows,
                                            in_offset=bass.IndirectOffsetOnAxis(ap=rec_b[:, u, j, 0:1].bitcast(I32), axis=0),
                                            ).then_inc(row_in[u], 16)

            by_group(pool, 0, gather_rows)

            pool.wait_ge(s["placed"], 1)
            pool.wait_ge(s["xs_z"], 32)
            for a in range(TOP):
                if a:
                    pool.wait_ge(s["share1"], 1)
                for t in range(NT):
                    pool.indirect_dma_start(out=xs_t, out_offset=bass.IndirectOffsetOnAxis(ap=row_of[:, a, t:t + 1], axis=0),
                                            in_=edge_sum[:, t, 0:XW], in_offset=None).then_inc(s["sent"], 16)
            pool.wait_ge(s["outd"], 32)

            def add_rows(st, u):
                hold(pool, s["yb"], st + 3)
                at = slice(st, st + 1) if isinstance(st, int) else ds(st, 1)
                link(pool.tensor_copy(idx_st[:, u, 0:1], meta[:, at, 1]))
                link.wait()
                if not isinstance(st, int) or st:
                    hold(pool, s["added"], 16 * st)
                pool.indirect_dma_start(out=out, out_offset=bass.IndirectOffsetOnAxis(ap=idx_st[:, u, 0:1], axis=0),
                                        in_=y_b[:, u], in_offset=None, compute_op=ALU.add).then_inc(s["added"], 16)

            for u in range(2):
                add_rows(u, u)
            with pool.Fori(0, NM // 2 - 1) as i:
                link.loop(i, 2)
                for u in range(2):
                    add_rows(2 * i + (u + 2), u)
            link.close(NM // 2 - 1)
            pool.wait_ge(s["added"], 16 * NM)

        @block.scalar
        def _(act):
            act.wait_ge(s["stats"], 1)
            act.wait_ge(s["consts"], 1)
            act.activation(rstd[:, :, 0], mv[:, :, 1], ACT.Sqrt, bias=eps_t[0:TN, :]).then_inc(s["std"], 1)
            act.sem_inc(s["lr_x"], 2)
            with act.Fori(0, NT // 2) as i:
                for u in range(2):
                    t = 2 * i + u
                    hold(act, s["tp"], t + 3)
                    hold(act, s["lr"], t + 1)
                    v = bank[u][:, 0:256].rearrange("p (c n) -> p c n", c=KC)[:, :, 0:TN]
                    act.activation(xt[:, u], v, ACT.Copy).then_inc(s["xt"], 1)
                    act.activation(xnT[:, :, ds(t * TN, TN)], v, ACT.Copy).then_inc(s["lr_x"], 1)
            act.wait_ge(s["lr_x"], NT + 2)
            act.wait_ge(s["lr"], NT + 2)
            act.sem_inc(s["vt"], 2)
            act.sem_inc(s["f_act"], 1)
            with act.Fori(0, NT // 2) as i:
                for u in range(2):
                    t = 2 * i + u
                    hold(act, s["f_pe"], t + 1)
                    act.activation(xt[:, u], xnT[:, :, ds(t * TN, TN)], ACT.Copy).then_inc(s["f_xt"], 1)
                    hold(act, s["mk"], t + 1)
                    act.activation(ek[:, u, :], mk[:, u, :], ACT.Exp).then_inc(s["ek"], 1)
                    hold(act, s["kt"], t + 3)
                    hold(act, s["kvm"], t + 1)
                    act.activation(vt[:, u, :, 0:128], bank[4 + u][0:TN, D:2 * D].rearrange("p (c n) -> p c n", c=KC),
                                   ACT.Copy).then_inc(s["vt"], 1)
                    hold(act, s["f_pe01"], t + 1)
                    hold(act, s["stored"], t + 1)
                    act.activation(feat_s[:, u, 0:1024].rearrange("p (n w) -> p n w", n=2), psum[0:TN, 0:2, :],
                                   ACT.Copy).then_inc(s["f_act"], 1)
            act.wait_ge(s["lr_out"], 32)
            act.wait_ge(s["scat"], 16 * NT)

            def q_exp(k):
                hold(act, s["q"], k + 1)
                act.activation(qt[:, 0], psum[:, 0:2, 0:SN], ACT.Exp).then_inc(s["q_ex"], 1)
                act.activation(qt[:, 1], psum[:, 0:2, 0:SN], ACT.Relu).then_inc(s["q_ex"], 1)

            def message_turned(k):
                hold(act, s["tmsg"], k + 1)
                act.activation(msgT[:, :, :], psum[:, 0:2, 0:SN], ACT.Copy).then_inc(s["msgT"], 1)

            def ms_turned(k):
                hold(act, s["tpm"], k + 1)
                for c in range(KC):
                    act.activation(msT[:, c, :], bank[4 + c][:, 0:SN], ACT.Identity, scale=colv[:, c:c + 1],
                                   bias=colv[:, KC + c:KC + c + 1]).then_inc(s["msT"], 1)

            def hidden_relu(k, o, b, done):
                hold(act, done, k + 1)
                act.activation(hT[:, o:o + KC, :], psum[:, b:b + KC, 0:SN], ACT.Relu).then_inc(s["h_act"], 1)

            def root(k, var, sd):
                hold(act, s[var], k + 1)
                act.activation(sd2[:, :, 0], mv2[:, :, 1], ACT.Sqrt, bias=eps_t[0:TN, :]).then_inc(s[sd], 1)

            def q_turn(k, ahead):
                hidden_relu(k, KC, 4, s["h1a"])
                message_turned(k + 1)
                hidden_relu(k, 0, 6, s["h1b"])
                root(k + 1, "ms_var", "ms_sd")
                if ahead:
                    q_exp(k + 2)
                root(k, "h2_var", "h2_sd")
                ms_turned(k + 1)

            q_exp(0)
            message_turned(0)
            root(0, "ms_var", "ms_sd")
            q_exp(1)
            ms_turned(0)
            with act.Fori(0, NS - 2) as k:
                q_turn(k, True)
            q_turn(NS - 2, False)
            hidden_relu(NS - 1, KC, 4, s["h1a"])
            hidden_relu(NS - 1, 0, 6, s["h1b"])
            root(NS - 1, "h2_var", "h2_sd")
            act.wait_ge(s["a_sub"], 1)
            act.activation(logits, run_max[:, :, :], ACT.Exp).then_inc(s["a_ex"], 1)

            def landed(g, u, n):
                hold(act, row_in[u], 16 * GJ * n + 16 * GJ)
                act.sem_inc(s["rows_in"], 1)

            by_group(act, 0, landed)
            act.sem_inc(s["x2T"], 1)
            with act.Fori(0, NS) as k:
                hold(act, s["x2_var"], k + 1)
                act.activation(sd2[:, :, 0], mv2[:, :, 1], ACT.Sqrt, bias=eps_t[0:TN, :]).then_inc(s["x2_sd"], 1)
                hold(act, s["x2tp"], k + 2)
                hold(act, s["lg"], k + 1)
                act.activation(msT[:, :, :], psum[:, 0:2, 0:SN], ACT.Copy).then_inc(s["x2T"], 1)
            act.wait_ge(s["lg_x"], 1)
            act.activation(lg_s[:, 1], lg_s[:, 0], ACT.Exp).then_inc(s["lg_ex"], 1)

            for k in ("xtc", "hg", "htc"):
                act.sem_inc(s[k], 2)

            def x_turned(st, u, n):
                hold(act, s["xtp"], st + 1)
                hold(act, s["up"], st + 1)
                act.activation(x_T[:, u], bank[u][:, 0:D], ACT.Copy).then_inc(s["xtc"], 1)

            def gelu(st, u, n):
                hold(act, s["hb"], st + 3)
                hold(act, s["htp"], st + 1)
                act.activation(h_g[:, u], h_b[:, u], ACT.Gelu).then_inc(s["hg"], 1)

            def h_turned(st, u, n):
                hold(act, s["htp"], st + 3)
                hold(act, s["down"], st + 1)
                act.activation(h_T[:, u], bank[4 + u][:, 0:D], ACT.Copy).then_inc(s["htc"], 1)

            expert_steps(act, [(2, x_turned), (1, gelu), (0, h_turned)])

        @block.vector
        def _(dve):
            link = Link(dve, s["dve"])

            def layer_stats():
                link.wait()
                for j in range(SJ):
                    ins = dve.bn_aggr(mv2[:, j, :], st2[:, j, :])
                return ins

            dve.memset(zero_w, 0.0).then_inc(s["zeroed"], 1)
            dve.wait_ge(s["edges"], 16 * 5)
            link(dve.tensor_copy(dst_f[:, :], dst3[:, 1, :]))
            dve.wait_ge(s["consts"], 1)
            link.wait()
            link(dve.tensor_scalar(first_w[:, :], ones[:, 0:TN], dst_f[:, 0:1], None, ALU.mult))
            link(dve.tensor_scalar(first_i[:, :], dst3[:, 1, 0:1], float(N - 1), None, ALU.min))
            link.wait()
            dve.sem_inc(s["d0"], 1)
            link(dve.scalar_tensor_tensor(out=rec_idx, in0=src_a[:, :], scalar=float(R), in1=typ_a[:, :], op0=ALU.mult, op1=ALU.add))
            link(dve.tensor_copy(rec[:, :, 1], dst3[:, 1, :]))
            link(dve.tensor_tensor(new_run[:, :], dst3[:, 0, :], dst3[:, 1, :], ALU.not_equal))
            link(dve.tensor_tensor(end_run[:, :], dst3[:, 1, :], dst3[:, 2, :], ALU.not_equal))
            link.wait()
            link(dve.tensor_copy(typ_f, typ_a[:, :]))
            link(dve.tensor_scalar(keep[:, :], new_run[:, :], -1.0, 1.0, ALU.mult, ALU.add))
            link.wait()
            link(dve.tensor_scalar(new_run[:, :], new_run[:, :], -BIG, None, ALU.mult))
            dve.tensor_scalar(end_run[:, :], end_run[:, :], -BIG, None, ALU.mult).then_inc(s["idx"], 1)
            dve.wait_ge(s["d0_bc"], 1)
            cmp = arena_q[0:TN, 0:5 * 128].rearrange("p (t n) -> p t n", t=5)
            for t in range(0, NT, 5):
                link(dve.tensor_tensor(cmp, bank[5][0:TN, 0:128].unsqueeze(1).broadcast_to([TN, 5, 128]),
                                       node_id[:, t:t + 5].unsqueeze(2).broadcast_to([TN, 5, 128]), ALU.is_lt))
                link.wait()
                link(dve.tensor_reduce(part_of[:, t:t + 5], cmp, AX, ALU.add))
                link.wait()
            link(dve.tensor_scalar(part_of[:, :], part_of[:, :], -1.0, 0.0, ALU.add, ALU.max))
            link.wait()
            dve.tensor_copy(part_i[:, :], part_of[:, :]).then_inc(s["part"], 1)
            dve.wait_ge(s["last"], 16)
            dve.wait_ge(s["consts"], 1)
            link(dve.tensor_copy(last_f[:, 1:2], last_i[:, :]))
            link.wait()
            link(dve.tensor_scalar(thr[:, :], thr[:, :], last_f[:, 1:2], None, ALU.is_le))
            link.wait()
            link(dve.tensor_reduce(last_f[:, 1:2], thr[:, :], AX, ALU.add))
            link.wait()
            link(dve.tensor_tensor(last_f[:, 1:2], last_f[:, 1:2], last_f[:, 0:1], ALU.add))
            link.wait()
            dve.tensor_scalar(path_cmp[:, 1, :], path_cmp[:, 0, :], last_f[:, 1:2], None, ALU.is_ge).then_inc(s["path_c"], 1)
            dve.wait_ge(s["rw_tp"], 1)
            dve.tensor_copy(rwT[:, :, :], bank[7][:, 0:KC * NX].rearrange("p (c n) -> p c n", c=KC)).then_inc(s["rw_ev"], 1)
            dve.wait_ge(s["path_p"], 1)
            link(dve.tensor_copy(path_f[:, 1, :], bank[6][:, 0:NSTEP]))
            link(dve.tensor_copy(end_i[:, :], bank[6][0:1, NSTEP:NSTEP + NG]))
            link.wait()
            link(dve.tensor_tensor(path_f[:, 2, :], path_f[:, 0, :], path_f[:, 1, :], ALU.subtract))
            link(dve.tensor_copy(path_i[0:1, 0, 0:NSTEP], path_f[0:1, 1, :]))
            link(dve.memset(path_i[0:1, 1, :], 0))
            link.wait()
            link(dve.tensor_copy(path_i[0:1, 1, AD:NSTEP + AD], path_f[0:1, 2, :]))
            link.wait()
            dve.tensor_scalar(path_f[:, 2, :], path_f[:, 2, :], float(TN), None, ALU.mult).then_inc(s["path_r"], 1)

            for side in range(2):
                dve.wait_ge(s["conv"], 16 * KC)
                dve.wait_ge(s["attn"], 32)
                for c in range(KC):
                    link(dve.tensor_tensor(prod, conv_w[:, c, :], attn_rb if side else attn_b, ALU.mult))
                    link.wait()
                    link(dve.tensor_reduce(w_lr[:, c, side * R * H:(side + 1) * R * H],
                                           prod.rearrange("p (g d) -> p g d", d=HD), AX, ALU.add))
                    link.wait()
            dve.sem_inc(s["wlr"], 1)

            dve.wait_ge(s["x"], 16)
            with dve.Fori(0, NT // (2 * FS)) as i:
                link.loop(i, 2 * FS)
                for v in range(2 * FS):
                    t = 2 * FS * i + v
                    link(dve.bn_stats(stats[:, ds(t, 1), :].rearrange("p t w -> p (t w)"),
                                      node_sum[:, ds(t, 1), :].rearrange("p t w -> p (t w)")))
            link.close(NT // (2 * FS))
            link.wait()
            link(dve.tensor_tensor(mv[:, :, 0], stats[:, :, 1], stats[:, :, 4], ALU.add))
            link(dve.tensor_tensor(tmp_t[:, 0, :], stats[:, :, 1], stats[:, :, 4], ALU.subtract))
            link(dve.tensor_tensor(tmp_t[:, 1, :], stats[:, :, 2], stats[:, :, 5], ALU.add))
            link.wait()
            link(dve.tensor_scalar(mv[:, :, 0], mv[:, :, 0], 0.5, None, ALU.mult))
            link(dve.tensor_tensor(tmp_t[:, 0, :], tmp_t[:, 0, :], tmp_t[:, 0, :], ALU.mult))
            link(dve.tensor_scalar(tmp_t[:, 1, :], tmp_t[:, 1, :], 1.0 / D, None, ALU.mult))
            link.wait()
            dve.scalar_tensor_tensor(out=mv[:, :, 1], in0=tmp_t[:, 0, :], scalar=0.25, in1=tmp_t[:, 1, :],
                                     op0=ALU.mult, op1=ALU.add).then_inc(s["stats"], 1)
            dve.wait_ge(s["std"], 1)
            link(dve.reciprocal(rstd[:, :, 0], rstd[:, :, 0]))
            link.wait()
            with dve.Fori(0, NT // (2 * FS)) as i:
                link.loop(i, 4 * FS)
                for v in range(2 * FS):
                    t, n = 2 * FS * i + v, v % FS
                    row = node_sum[:, ds(t, 1), :].rearrange("p t w -> p (t w)")
                    hold(dve, s["tp"], t + 1)
                    dve.tensor_scalar(xs[:, v % 2, :], row, mv[:, ds(t, 1), 0], rstd[:, ds(t, 1), 0],
                                      ALU.subtract, ALU.mult).then_inc(s["xs"], 1)
                    hold(dve, found_in[n], 16 * (2 * i) + 16 * (v // FS + 1))
                    link(dve.tensor_scalar(found[:, n, :], found[:, n, :], node_id[:, ds(t, 1)], None, ALU.is_lt))
                    link.wait()
                    link(dve.tensor_reduce(below[:, ds(t, 1)], found[:, n, :], AX, ALU.add))
                    link.wait()
                    dve.sem_inc(s["found_ev"], 1)
            link.close(NT // (2 * FS))
            link(dve.scalar_tensor_tensor(out=first_at[:, 0:NT], in0=part_of[:, :], scalar=float(EC), in1=below[:, :],
                                          op0=ALU.mult, op1=ALU.add))
            link(dve.memset(first_at[:, NT:NT + 1], float(E)))
            link.wait()
            dve.sem_inc(s["first_up"], 1)
            link(dve.tensor_scalar(node_id[:, :], node_id[:, :], float(EP), None, ALU.add))
            dve.wait_ge(s["shifted"], 1)
            link(dve.tensor_tensor(node_at[:, :], bank[2][0:TN, 0:NT], first_at[:, 0:NT], ALU.is_gt))
            link.wait()
            link(dve.tensor_tensor(first_at[:, 0:NT], first_at[:, 0:NT], node_id[:, :], ALU.subtract))
            link.wait()
            link(dve.tensor_tensor(node_at[:, :], node_at[:, :], first_at[:, 0:NT], ALU.mult))
            link.wait()
            link(dve.tensor_tensor(node_at[:, :], node_at[:, :], node_id[:, :], ALU.add))
            link.wait()
            dve.tensor_copy(node_at_i[:, :], node_at[:, :]).then_inc(s["node_pos"], 1)
            dve.wait_ge(s["lr"], NT + 2)
            dve.tensor_copy(lr_s[:, :, :].rearrange("p t w -> p (t w)"),
                            psum[0:TN, 4:8, :].rearrange("p b w -> p (b w)")[:, 0:NT * 2 * R * H]).then_inc(s["lr_ev"], 1)

            dve.wait_ge(s["wts"], WTS)
            link(dve.tensor_tensor(hb_b2[:, 0, :], hb_b2[:, 0, :], hb_b2[:, 1, :], ALU.add))
            link.wait()
            dve.sem_inc(s["kt"], 2)
            dve.sem_inc(s["f_dve"], 1)
            with dve.Fori(0, NT // 2) as i:
                link.loop(i, 6)
                for u in range(2):
                    t = 2 * i + u
                    k_ps = bank[4 + u][0:TN, 0:D]
                    row = node_sum[:, ds(t, 1), :].rearrange("p t w -> p (t w)")
                    hold(dve, s["f_kv"], t + 1)
                    dve.tensor_scalar(mk[:, u, :], k_ps, 0.0, None, ALU.min).then_inc(s["mk"], 1)
                    hold(dve, s["ek"], t + 1)
                    hold(dve, s["kvm"], t + 1)
                    dve.scalar_tensor_tensor(out=kt[:, u, :], in0=k_ps, scalar=0.0, in1=ek[:, u, :],
                                             op0=ALU.max, op1=ALU.add).then_inc(s["kt"], 1)
                    hold(dve, s["f_pe"], t + 3)
                    hold(dve, s["stored"], t + 1)
                    dve.tensor_copy(feat_s[:, u, 1024:2048].rearrange("p (n w) -> p n w", n=2),
                                    psum[0:TN, 2:4, :]).then_inc(s["f_dve"], 1)
                    link(dve.tensor_scalar(xs[:, u, :], row, mv[:, ds(t, 1), 0], rstd[:, ds(t, 1), 0], ALU.subtract, ALU.mult))
                    link.wait()
                    link(dve.tensor_tensor(row, row, xs[:, u, :], ALU.add))
                    link.wait()
                    link(dve.tensor_tensor(row, row, hb_b2[:, 0, :], ALU.add))
            link.close(NT // 2)
            dve.wait_ge(s["kvm"], NT + 3)
            for c in range(KC):
                link(dve.scalar_tensor_tensor(out=kv_m[:, c, 0:128], in0=bank[6 + c][:, 0:128], scalar=1.0 / N,
                                              in1=mask[:, :], op0=ALU.mult, op1=ALU.mult))
                link(dve.tensor_scalar(kv_m[:, c, 128:HW], mask[:, :].rearrange("p (h d) -> p h d", d=AH)[:, :, 0],
                                       bank[6 + c][:, 128:129], None, ALU.mult))
            link.wait()
            dve.sem_inc(s["kv_ready"], 1)

            dve.wait_ge(s["r_first_in"], 16)
            dve.sem_inc(s["h2_done"], 1)
            dve.sem_inc(s["r_sel"], 1)
            m_at = [bank[2][0:TN, 0:D], bank[2][0:TN, D:2 * D], bank[3][0:TN, 0:D]]
            o_at = [bank[6][0:TN, 0:D], bank[6][0:TN, D:2 * D], bank[7][0:TN, 0:D]]
            norm = msg_n.rearrange("p (j d) -> p j d", j=SJ)

            def normalise(to, at):
                link(dve.reciprocal(sd2[:, :, 0], sd2[:, :, 0]))
                link.wait()
                for j in range(SJ):
                    link(dve.tensor_scalar(to[:, j, :], at[j], mv2[:, j, 0:1], sd2[:, j, :], ALU.subtract, ALU.mult))
                link.wait()

            def q_feature(k):
                hold(dve, s["q_ex"], 2 * k + 2)
                dve.scalar_tensor_tensor(out=qt[:, 1], in0=qt[:, 0], scalar=1.0, in1=qt[:, 1],
                                         op0=ALU.min, op1=ALU.add).then_inc(s["q_t"], 1)

            def message(k):
                hold(dve, s["nd"], k + 1)
                nd = psum[0:TN, 2:4, 0:SJ * HW].rearrange("p a (b w) -> p a b w", w=HW)
                for a in range(KC):
                    link(dve.tensor_scalar(den_r[:, a * SJ:(a + 1) * SJ, :], nd[:, a, :, 128:HW], ATT_EPS, None, ALU.add))
                link.wait()
                link(dve.reciprocal(den_r[:, :, :], den_r[:, :, :]))
                link.wait()
                for a in range(KC):
                    dve.scalar_tensor_tensor(out=msg_n[:, a * SJ * 128:(a + 1) * SJ * 128].rearrange("p (b h d) -> p b h d", b=SJ, d=AH),
                                             in0=nd[:, a, :, 0:128].rearrange("p b (h d) -> p b h d", d=AH), scalar=float(N),
                                             in1=den_r[:, a * SJ:(a + 1) * SJ, :].unsqueeze(3).broadcast_to([TN, SJ, 128 // AH, AH]),
                                             op0=ALU.mult, op1=ALU.mult).then_inc(s["msg"], 1)

            def norm_1(k):
                hold(dve, s["m"], k + 1)
                for j in range(SJ):
                    link(dve.bn_stats(st2[:, j, :], m_at[j]))
                layer_stats().then_inc(s["ms_var"], 1)
                hold(dve, s["ms_sd"], k + 1)
                normalise(ms, m_at)
                dve.sem_inc(s["ms"], 1)

            def norm_2(k):
                hold(dve, s["h2"], k + 1)
                for j in range(SJ):
                    link(dve.bn_stats(st2[:, j, :], o_at[j]))
                layer_stats().then_inc(s["h2_var"], 1)
                hold(dve, s["h2_sd"], k + 1)
                normalise(norm, o_at)
                link(dve.tensor_tensor(norm, norm, g2_b[:, :].unsqueeze(1).broadcast_to([TN, SJ, D]), ALU.mult))
                link.wait()
                rows = node_sum[:, ds(k * SJ, SJ), :] if not isinstance(k, int) else node_sum[:, k * SJ:(k + 1) * SJ, :]
                link(dve.tensor_tensor(rows, rows, norm, ALU.add))
                link.wait()
                dve.sem_inc(s["h2_done"], 1)

            def right_part(q):
                hold(dve, s["r_load"], 16 * q + 16)
                for g in range(R * H):
                    link(dve.tensor_tensor_scan(r_part[:, :, g], keep[:, ds(q * EQ, EQ)], r_part[:, :, g],
                                                r_first[:, g:g + 1], ALU.mult, ALU.add))
                link(dve.tensor_tensor(is_type, typ_f[:, ds(q * EQ, EQ)].unsqueeze(2).broadcast_to([128, EQ, R]),
                                       iota_n[:, 0:R].unsqueeze(1).broadcast_to([128, EQ, R]), ALU.is_equal))
                link.wait()
                link(dve.tensor_copy(r_first[:, :], r_part[:, EQ - 1, :]))
                link.wait()
                part4 = r_part.rearrange("p k (r h) -> p k r h", h=H)
                link(dve.tensor_tensor(part4, part4, is_type.unsqueeze(3).broadcast_to([128, EQ, R, H]), ALU.mult))
                link.wait()
                link(dve.tensor_reduce(right[:, ds(q * EQ, EQ), :], r_part.rearrange("p k (r h) -> p k h r", h=H), AX, ALU.add))
                link.wait()
                dve.sem_inc(s["r_sel"], 1)

            q_feature(0)
            message(0)
            norm_1(0)
            q_feature(1)
            with dve.Fori(0, NS - 2) as k:
                link.loop(k, 3 + 7 + 9 + R * H + 4)
                message(k + 1)
                right_part(k)
                norm_1(k + 1)
                q_feature(k + 2)
                norm_2(k)
            link.close(NS - 2)
            message(NS - 1)
            norm_1(NS - 1)
            norm_2(NS - 2)
            norm_2(NS - 1)

            dve.wait_ge(s["gath_use"], 1)
            link(dve.tensor_tensor(logits, logits, right, ALU.add))
            link.wait()
            link(dve.scalar_tensor_tensor(out=logits, in0=logits, scalar=0.2, in1=logits, op0=ALU.mult, op1=ALU.max))
            link.wait()

            def flip(ap, back):
                return ap[:, ::-1] if back else ap

            for back in range(2):
                marks = end_run if back else new_run
                for again in range(2):
                    for h in range(H):
                        src = run_max[:, :, h] if back or again else logits[:, :, h]
                        link(dve.tensor_tensor_scan(flip(run_max[:, :, h], back), flip(marks[:, :], back), flip(src, back),
                                                    cin[:, h:h + 1] if again else -BIG, ALU.add, ALU.max))
                    link.wait()
                    if again:
                        continue
                    edge = 0 if back else EC - 1
                    link(dve.tensor_copy(tailf[:, 0, :], run_max[:, edge, :]))
                    link(dve.tensor_reduce(tailf[:, 1, 0:1], marks[:, :], AX, ALU.min))
                    link.wait()
                    link(dve.tensor_copy(tailf[:, 1, 1:H], tailf[:, 1, 0:1].broadcast_to([128, H - 1])))
                    link(dve.memset(carry[:, :], -BIG))
                    link.wait()
                    dve.sem_inc(s["a_tail"], 1)
                    dve.wait_ge(s["a_tp"], back + 1)
                    link(dve.tensor_copy(rowf[:, :, :], bank[0][0:H, 0:256].rearrange("p (a n) -> p a n", a=2)))
                    link.wait()
                    link(dve.tensor_tensor_scan(flip(carry[:, 1:129], back), flip(rowf[:, 1, :], back), flip(rowf[:, 0, :], back),
                                                -BIG, ALU.add, ALU.max))
                    link.wait()
                    dve.sem_inc(s["a_row"], 1)
                    dve.wait_ge(s["a_tpb"], back + 1)
                    link(dve.tensor_copy(cin[:, :], bank[1][:, 0:H]))
                    link.wait()
            dve.tensor_tensor(run_max[:, :, :], logits, run_max[:, :, :], ALU.subtract).then_inc(s["a_sub"], 1)

            dve.wait_ge(s["h1b"], NS)
            dve.memset(arena_n[:, :], 0.0).then_inc(s["dve"], 1)
            link.count += 1
            link.wait()
            dve.sem_inc(s["oh"], 2 * U)
            dve.sem_inc(s["agg_ev"], 2)

            def add_step(at, psum_row):
                b = dve.value_load(path_i[0:1, 1, at], min_val=0, max_val=NT - 1)
                row = edge_sum[:, ds(b, 1), :].rearrange("p t w -> p (t w)")
                dve.tensor_tensor(row, row, psum_row[0:TN, 0:W], ALU.add).then_inc(s["agg_ev"], 1)

            def group_of(st):
                return dve.value_load(path_i[0:1, 0, ds(st, 1)], min_val=0, max_val=NG - 1)

            with dve.Fori(0, NSTEP // U) as i:
                link.loop(i, 2 * U)
                for u in range(U):
                    st = U * i + u
                    if u == 0:
                        g = group_of(st)
                    g_slot = g % GR
                    hold(dve, s["rows_in"], g + 1)
                    rows = ring[:, ds(g_slot, 1), :].rearrange("p s (j h d) -> p (s j) h d", j=GJ, h=H)
                    ex = rec_b[:, ds(g_slot, 1), :, 2:2 + H].rearrange("p s j h -> p (s j) h")
                    link(dve.tensor_scalar(dst_rel[:, u, :], rec_b[:, ds(g_slot, 1), :, 1].rearrange("p s j -> p (s j)"),
                                           path_f[:, 2, ds(st, 1)], None, ALU.subtract))
                    link(dve.tensor_copy(weighted[:, u, :, D:W], ex))
                    dve.tensor_tensor(weighted[:, u, :, 0:D].rearrange("p j (h d) -> p j h d", h=H), rows,
                                      ex.unsqueeze(3).broadcast_to([128, GJ, H, HD]), ALU.mult).then_inc(s["oh"], 1)
                    if u < U - 1:
                        g = group_of(st + 1)
                    link.wait()
                    dve.tensor_tensor(onehot[:, u], iota_n[:, 0:TN].unsqueeze(1).broadcast_to([128, GJ, TN]),
                                      dst_rel[:, u, :].unsqueeze(2).broadcast_to([128, GJ, TN]), ALU.is_equal).then_inc(s["oh"], 1)
                    hold(dve, s["slot"], st + U + 1 - AD)
                    hold(dve, s["agg_ev"], st + 2)
                    add_step(ds(st, 1), bank[(u - AD) % U])
            link.close(NSTEP // U)
            dve.wait_ge(s["slot"], NSTEP + U)
            for a in range(AD):
                dve.wait_ge(s["agg_ev"], NSTEP + a + 2)
                add_step(slice(NSTEP + a, NSTEP + a + 1), bank[U - AD + a])
            dve.wait_ge(s["agg_ev"], NSTEP + AD + 2)

            den = edge_sum[:, :, D:W]
            link(dve.tensor_scalar(den, den, 1e-30, None, ALU.max))
            link.wait()
            link(dve.reciprocal(den, den))
            link.wait()
            with dve.Fori(0, NS) as k:
                link.loop(k, 13)
                rows = node_sum[:, ds(k * SJ, SJ), :]
                for j in range(SJ):
                    t = k * SJ + j
                    v = edge_sum[:, ds(t, 1), 0:D].rearrange("p t (h d) -> p (t h) d", h=H)
                    link(dve.tensor_tensor(v, v, edge_sum[:, ds(t, 1), D:W].rearrange("p t h -> p (t h)").unsqueeze(2)
                                           .broadcast_to([TN, H, HD]), ALU.mult))
                link.wait()
                link(dve.tensor_tensor(rows, rows, edge_sum[:, ds(k * SJ, SJ), 0:D], ALU.add))
                link.wait()
                for j in range(SJ):
                    link(dve.bn_stats(st2[:, j, :], node_sum[:, ds(k * SJ + j, 1), :].rearrange("p t w -> p (t w)")))
                layer_stats().then_inc(s["x2_var"], 1)
                hold(dve, s["x2_sd"], k + 1)
                link(dve.reciprocal(sd2[:, :, 0], sd2[:, :, 0]))
                link.wait()
                hold(dve, s["x2tp"], k + 1)
                for j in range(SJ):
                    link(dve.tensor_scalar(ms[:, j, :], node_sum[:, ds(k * SJ + j, 1), :].rearrange("p t w -> p (t w)"),
                                           mv2[:, j, 0:1], sd2[:, j, :], ALU.subtract, ALU.mult))
                link.wait()
                dve.sem_inc(s["x2n"], 1)
                link(dve.tensor_tensor(rows, rows, ms[:, :, :], ALU.add))
                link(dve.tensor_copy(edge_sum[:, ds(k * SJ, SJ), 0:D], ms[:, :, :]))
            link.close(NS)
            dve.wait_ge(s["lg"], NS + 1)
            lg, pr, scr = bank[2][0:TN, 0:NT * NX].rearrange("p (t e) -> p t e", e=NX), lg_s[:, 2], lg_s[:, 3]
            experts = iota_n[0:TN, 0:NX].unsqueeze(1).broadcast_to([TN, NT, NX])

            def wide(ap):
                return ap.unsqueeze(2).broadcast_to([TN, NT, NX])

            def then(ins):
                link(ins)
                link.wait()

            then(dve.tensor_reduce(rt[:, 0, :], lg, AX, ALU.max))
            dve.tensor_tensor(lg_s[:, 0], lg, wide(rt[:, 0, :]), ALU.subtract).then_inc(s["lg_x"], 1)
            dve.wait_ge(s["lg_ex"], 1)
            then(dve.tensor_reduce(rt[:, 1, :], lg_s[:, 1], AX, ALU.add))
            then(dve.reciprocal(rt[:, 1, :], rt[:, 1, :]))
            then(dve.tensor_tensor(pr, lg_s[:, 1], wide(rt[:, 1, :]), ALU.mult))
            for a in range(TOP):
                then(dve.tensor_reduce(rt[:, 2 + a, :], pr, AX, ALU.max))
                then(dve.tensor_tensor(scr, pr, wide(rt[:, 2 + a, :]), ALU.is_lt))
                then(dve.scalar_tensor_tensor(out=scr, in0=scr, scalar=float(NX), in1=experts, op0=ALU.mult, op1=ALU.add))
                then(dve.tensor_reduce(rt[:, 4, :], scr, AX, ALU.min))
                then(dve.tensor_tensor(hot[:, a], experts, wide(rt[:, 4, :]), ALU.is_equal))
                if a == 0:
                    then(dve.scalar_tensor_tensor(out=pr, in0=hot[:, a], scalar=-4.0, in1=pr, op0=ALU.mult, op1=ALU.add))
            dve.tensor_tensor(lg_s[:, 4], hot[:, 0], hot[:, 1], ALU.add).then_inc(s["picked"], 1)
            then(dve.tensor_tensor(rt[:, 4, :], rt[:, 2, :], rt[:, 3, :], ALU.add))
            then(dve.tensor_scalar(rt[:, 4, :], rt[:, 4, :], 1e-12, None, ALU.max))
            then(dve.reciprocal(rt[:, 4, :], rt[:, 4, :]))
            for a in range(TOP):
                link(dve.tensor_tensor(share[:, a, :], rt[:, 2 + a, :], rt[:, 4, :], ALU.mult))
            dve.wait_ge(s["ranked"], 1)
            total, upto = bank[3][0:TN, NT * NX:2 * NT * NX].rearrange("p (t e) -> p t e", e=NX), lg_s[:, 0]
            then(dve.tensor_copy(lg_s[:, 1], total))
            for e in range(NX):
                link(dve.tensor_tensor_scan(upto[:, :, e], ones[0:TN, 0:NT], lg_s[:, 1, :, e], 0.0, ALU.mult, ALU.add))
            link.wait()
            then(dve.tensor_copy(ex_t[:, 0, :], upto[:, NT - 1, :]))
            tens = lg_s[:, 3].rearrange("p t e -> p (t e)").rearrange("p (e t) -> p e t", e=NX)
            then(dve.tensor_scalar(rt[:, 5, :], iota_n[0:TN, 0:NT], 128.0, None, ALU.mult))
            then(dve.tensor_tensor(tens, ex_t[:, 0, :].unsqueeze(2).broadcast_to([TN, NX, NT]),
                                   rt[:, 5, :].unsqueeze(1).broadcast_to([TN, NX, NT]), ALU.is_gt))
            then(dve.tensor_reduce(ex_t[:, 1, :], tens, AX, ALU.add))
            then(dve.tensor_tensor_scan(ex_t[:, 2, :], ones[0:TN, 0:NX], ex_t[:, 1, :], 0.0, ALU.mult, ALU.add))
            then(dve.tensor_tensor(ex_t[:, 3, :], ex_t[:, 2, :], ex_t[:, 1, :], ALU.subtract))
            then(dve.tensor_tensor(upto, upto, lg_s[:, 1], ALU.subtract))
            then(dve.tensor_tensor(upto, upto, bank[3][0:TN, 0:NT * NX].rearrange("p (t e) -> p t e", e=NX), ALU.add))
            then(dve.scalar_tensor_tensor(out=upto, in0=ex_t[:, 3, :].unsqueeze(1).broadcast_to([TN, NT, NX]), scalar=128.0,
                                          in1=upto, op0=ALU.mult, op1=ALU.add))
            for a in range(TOP):
                then(dve.tensor_tensor(hot[:, a], hot[:, a], upto, ALU.mult))
                then(dve.tensor_reduce(rt[:, a, :], hot[:, a], AX, ALU.add))
                link(dve.tensor_copy(row_of[:, a, :], rt[:, a, :]))
            link(dve.tensor_copy(edge_sum[:, :, D], share[:, 0, :]))
            link(dve.tensor_scalar(edge_sum[:, :, D + 1], node_id[:, :], -float(EP), None, ALU.add))
            link.wait()
            dve.sem_inc(s["placed"], 1)
            then(dve.tensor_tensor(step_x.rearrange("p (n e) -> p n e", e=NX), path_f[0:1, 0, 0:NM].unsqueeze(2).broadcast_to([1, NM, NX]),
                                   ex_t[0:1, 2, :].unsqueeze(1).broadcast_to([1, NM, NX]), ALU.is_ge))
            then(dve.tensor_reduce(step_f, step_x.rearrange("p (n e) -> p n e", e=NX), AX, ALU.add))
            then(dve.tensor_scalar(step_f, step_f, float(NX - 1), None, ALU.min))
            dve.tensor_copy(step_i[:, :], step_f).then_inc(s["steps"], 1)
            dve.wait_ge(s["steps"], 1)
            dve.wait_ge(s["sent"], 16 * NT)
            dve.tensor_copy(edge_sum[:, :, D], share[:, 1, :]).then_inc(s["share1"], 1)
            dve.wait_ge(s["b_rows"], 32)
            dve.wait_ge(s["sent"], 16 * TOP * NT)

            for k in ("hb", "yb"):
                dve.sem_inc(s[k], 2)

            def take_meta(st, u, n):
                hold(dve, x_arr[u], 16 * n + 16)
                at = slice(st, st + 1) if isinstance(st, int) else ds(st, 1)
                dve.tensor_copy(meta[:, at, :].rearrange("p s a -> p (s a)"), x_in[:, u, D:XW]).then_inc(s["mc"], 1)

            def add_b1(st, u, n):
                hold(dve, s["up"], st + 3)
                hold(dve, s["hg"], st + 1)
                dve.tensor_tensor(h_b[:, u], bank[2 + u][:, 0:D], b1_row[:, ds(step_expert(dve, st), 1), :].rearrange("p e n -> p (e n)"),
                                  ALU.add).then_inc(s["hb"], 1)

            def add_b2(st, u, n):
                hold(dve, s["down"], st + 3)
                if not isinstance(st, int) or st >= 2:
                    hold(dve, s["added"], 16 * (st - 1))
                dve.tensor_tensor(y_b[:, u], bank[6 + u][:, 0:D], b2_row[:, ds(step_expert(dve, st), 1), :].rearrange("p e n -> p (e n)"),
                                  ALU.add).then_inc(s["ya"], 1)
                at = slice(st, st + 1) if isinstance(st, int) else ds(st, 1)
                hold(dve, s["ya"], st + 1)
                dve.tensor_scalar(y_b[:, u], y_b[:, u], meta[:, at, 0], None, ALU.mult).then_inc(s["yb"], 1)

            expert_steps(dve, [(2, take_meta), (1, add_b1), (-1, add_b2)])

        @block.tensor
        def _(pe):
            def product(out_ap, pairs, sem_=None, **kw):
                for n, (w, m) in enumerate(pairs):
                    ins = pe.matmul(out_ap, w, m, start=n == 0, stop=n == len(pairs) - 1, skip_group_check=True)
                return ins

            pe.wait_ge(s["d0"], 1)
            product(bank[5][0:TN, 0:128], [(first_w[:, :], ident[:, :])]).then_inc(s["d0_bc"], 1)
            pe.wait_ge(s["rw"], 16)
            pe.wait_ge(s["consts"], 1)
            for c in range(KC):
                ins = pe.transpose(bank[7][:, c * NX:(c + 1) * NX], rw_s[:, c * 128:(c + 1) * 128], ident[0:NX, 0:NX])
            ins.then_inc(s["rw_tp"], 1)
            pe.wait_ge(s["path_c"], 1)
            product(bank[6][:, 0:NSTEP], [(ones[0:NG, :], path_cmp[:, 1, :])])
            product(bank[6][0:1, NSTEP:NSTEP + NG], [(last_f[:, 1:2], ident[0:NG, 0:NG])]).then_inc(s["path_p"], 1)

            pe.wait_ge(s["part"], 1)
            pe.wait_ge(s["wlr"], 1)
            pe.wait_ge(s["rw_ev"], 1)
            pe.wait_ge(s["path_r"], 1)
            pe.sem_inc(s["tp"], 2)
            pe.sem_inc(s["lr"], 2)
            lr_ps = psum[0:TN, 4:8, :].rearrange("p b w -> p (b w)")

            def turn_xn(t, u):
                hold(pe, s["xs"], t + 1)
                hold(pe, s["lr_x"], t + 1)
                for c in range(KC):
                    ins = pe.transpose(bank[u][:, c * 128:c * 128 + TN], xs[:, u, c * 128:(c + 1) * 128], ident[0:TN, 0:TN])
                ins.then_inc(s["tp"], 1)

            def logit_columns(t, u):
                w = 2 * R * H
                hold(pe, s["xt"], t + 1)
                at = slice(t * w, (t + 1) * w) if isinstance(t, int) else ds(t * w, w)
                product(lr_ps[:, at], [(xt[:, u, c, :], w_lr[:, c, :]) for c in range(KC)]).then_inc(s["lr"], 1)

            turn_xn(0, 0)
            with pe.Fori(0, NT // 2 - 1) as i:
                turn_xn(2 * i + 1, 1)
                logit_columns(2 * i, 0)
                turn_xn(2 * i + 2, 0)
                logit_columns(2 * i + 1, 1)
            turn_xn(NT - 1, 1)
            logit_columns(NT - 2, 0)
            logit_columns(NT - 1, 1)
            pe.wait_ge(s["first_up"], 1)
            product(bank[2][0:TN, 0:NT], [(shift[:, 0, :], first_at[:, 0:NT]), (shift[:, 1, :], first_at[:, 1:NT + 1])]).then_inc(s["shifted"], 1)
            pe.wait_ge(s["wts"], WTS)
            pe.wait_ge(s["node_pos"], 1)
            pe.wait_ge(s["lr_ev"], 1)
            pe.wait_ge(s["lr_x"], NT + 2)
            for c in range(KC):
                ins = pe.matmul(bank[6 + c][:, 0:129], zeros[0:TN, 0:128], zeros[0:TN, 0:129], start=True, stop=False, skip_group_check=True)
            ins.then_inc(s["kvm"], 1)
            pe.wait_ge(s["kvm"], 1)
            pe.sem_inc(s["kvm"], 1)
            pe.sem_inc(s["f_pe"], 2)
            with pe.Fori(0, NT // 2) as i:
                for u in range(2):
                    t = 2 * i + u
                    hold(pe, s["f_xt"], t + 1)
                    hold(pe, s["vt"], t + 1)
                    hold(pe, s["kt"], t + 1)
                    product(bank[4 + u][0:TN, :], [(xt[:, u, c, :], wkv[:, c, :]) for c in range(KC)]).then_inc(s["f_kv"], 1)
                    hold(pe, s["f_act"], t + 1)
                    for n in range(2):
                        ins = product(bank[n][0:TN, :], [(xt[:, u, c, :], conv_w[:, c, n * 512:(n + 1) * 512]) for c in range(KC)])
                    ins.then_inc(s["f_pe01"], 1)
                    hold(pe, s["f_dve"], t + 1)
                    for n in range(2, 4):
                        ins = product(bank[n][0:TN, :], [(xt[:, u, c, :], conv_w[:, c, n * 512:(n + 1) * 512]) for c in range(KC)])
                    ins.then_inc(s["f_pe"], 1)
                    hold(pe, s["kt"], t + 3)
                    hold(pe, s["vt"], t + 3)
                    for c in range(KC):
                        ins = pe.matmul(bank[6 + c][:, 0:129], kt[:, u, c * 128:(c + 1) * 128], vt[:, u, c, :],
                                        start=False, stop=False, skip_group_check=True)
                    ins.then_inc(s["kvm"], 1)
            for c in range(KC):
                ins = pe.matmul(bank[6 + c][:, 0:129], zeros[0:TN, 0:128], zeros[0:TN, 0:129], start=False, stop=True, skip_group_check=True)
            ins.then_inc(s["kvm"], 1)
            pe.wait_ge(s["f_act"], NT + 1)
            pe.wait_ge(s["f_dve"], NT + 1)
            pe.wait_ge(s["kv_ready"], 1)

            def span(k):
                return slice(k * SN, (k + 1) * SN) if isinstance(k, int) else ds(k * SN, SN)

            def q_products(k):
                for o in range(KC):
                    ins = product(bank[o][:, 0:SN], [(wqm[:, 0, c, o * 128:(o + 1) * 128], xnT[:, c, span(k)]) for c in range(KC)])
                ins.then_inc(s["q"], 1)

            def sums(k):
                hold(pe, s["q_t"], k + 1)
                for b in range(SJ * KC):
                    j, c = b // KC, b % KC
                    ins = product(bank[2 + b // SJ][0:TN, (b % SJ) * HW:(b % SJ + 1) * HW],
                                  [(qt[:, 1, c, j * TN:(j + 1) * TN], kv_m[:, c, :])])
                ins.then_inc(s["nd"], 1)

            def turn_message(k):
                hold(pe, s["msg"], KC * k + KC)
                for j in range(SJ):
                    for c in range(KC):
                        ins = pe.transpose(bank[c][:, j * TN:(j + 1) * TN], msg_n[:, j * D + c * 128:j * D + (c + 1) * 128],
                                           ident[0:TN, 0:TN])
                ins.then_inc(s["tmsg"], 1)

            def merge(k):
                hold(pe, s["msgT"], k + 1)
                for j in range(SJ):
                    ins = product(bank[2 + j // 2][0:TN, (j % 2) * D:(j % 2 + 1) * D],
                                  [(msgT[:, c, j * TN:(j + 1) * TN], wqm[:, 1, c, :]) for c in range(KC)])
                ins.then_inc(s["m"], 1)

            def turn_ms(k):
                hold(pe, s["ms"], k + 1)
                for j in range(SJ):
                    for c in range(KC):
                        ins = pe.transpose(bank[4 + c][:, j * TN:(j + 1) * TN], ms[:, j, c * 128:(c + 1) * 128], ident[0:TN, 0:TN])
                ins.then_inc(s["tpm"], 1)

            def hidden(k, o, b, done):
                for n in range(2):
                    cols = slice((o + n) * 128, (o + n + 1) * 128)
                    ins = product(bank[b + n][:, 0:SN], [(w1_s[:, c, cols], xnT[:, c, span(k)]) for c in range(KC)]
                                  + [(w1_s[:, KC + c, cols], msT[:, c, :]) for c in range(KC)])
                ins.then_inc(done, 1)

            def hidden_a(k):
                hold(pe, s["msT"], KC * k + KC)
                hidden(k, KC, 4, s["h1a"])

            def hidden_b(k):
                hold(pe, s["h2_done"], k + 1)
                hidden(k, 0, 6, s["h1b"])

            def output(k):
                hold(pe, s["h_act"], 2 * k + 2)
                for j in range(SJ):
                    ins = product(bank[6 + j // 2][0:TN, (j % 2) * D:(j % 2 + 1) * D],
                                  [(hT[:, c, j * TN:(j + 1) * TN], w2_s[:, c, :]) for c in range(2 * KC)])
                ins.then_inc(s["h2"], 1)

            def q_turn(k, ahead):
                sums(k + 1)
                hidden_a(k)
                turn_message(k + 1)
                hidden_b(k)
                merge(k + 1)
                if ahead:
                    q_products(k + 2)
                output(k)
                turn_ms(k + 1)

            q_products(0)
            sums(0)
            turn_message(0)
            merge(0)
            q_products(1)
            turn_ms(0)
            with pe.Fori(0, NS - 2) as k:
                q_turn(k, True)
            q_turn(NS - 2, False)
            hidden_a(NS - 1)
            hidden_b(NS - 1)
            output(NS - 1)
            for back in range(2):
                pe.wait_ge(s["a_tail"], back + 1)
                for n in range(2):
                    ins = pe.transpose(bank[0][0:H, n * 128:(n + 1) * 128], tailf[:, n, :], ident[:, :])
                ins.then_inc(s["a_tp"], 1)
                pe.wait_ge(s["a_row"], back + 1)
                row = carry[:, 2:130] if back else carry[:, 0:128]
                pe.transpose(bank[1][:, 0:H], row, ident[0:H, 0:H]).then_inc(s["a_tpb"], 1)
            pe.wait_ge(s["a_sub"], 1)
            pe.wait_ge(s["h2_done"], NS + 1)
            for a in range(AD):
                product(bank[U - AD + a][0:TN, 0:132], [(zeros[:, 0:TN], zeros[:, 0:132])])
                ins = product(bank[U - AD + a][0:TN, 132:W], [(zeros[:, 0:TN], zeros[:, 0:W - 132])])
            ins.then_inc(s["slot"], 1)
            pe.wait_ge(s["slot"], 1)
            pe.sem_inc(s["slot"], U - 1)
            with pe.Fori(0, NSTEP // U) as i:
                for u in range(U):
                    st = U * i + u
                    hold(pe, s["oh"], 2 * st + 2 * (U + 1))
                    hold(pe, s["agg_ev"], st + AD)
                    product(bank[u][0:TN, 0:W], [(onehot[:, u, j, :], weighted[:, u, j, :]) for j in range(GJ)]).then_inc(s["slot"], 1)
            pe.wait_ge(s["agg_ev"], NSTEP + AD + 2)
            pe.sem_inc(s["x2tp"], 1)
            pe.sem_inc(s["lg"], 1)
            with pe.Fori(0, NS) as k:
                hold(pe, s["x2n"], k + 1)
                hold(pe, s["x2T"], k + 1)
                for j in range(SJ):
                    for c in range(KC):
                        ins = pe.transpose(bank[c][:, j * TN:(j + 1) * TN], ms[:, j, c * 128:(c + 1) * 128], ident[0:TN, 0:TN])
                ins.then_inc(s["x2tp"], 1)
                hold(pe, s["x2T"], k + 2)
                for j in range(SJ):
                    ins = product(bank[2][0:TN, ds((k * SJ + j) * NX, NX)], [(msT[:, c, j * TN:(j + 1) * TN], rwT[:, c, :]) for c in range(KC)])
                ins.then_inc(s["lg"], 1)
            pe.wait_ge(s["picked"], 1)
            picks = lg_s[:, 4].rearrange("p t e -> p (t e)")
            product(bank[3][0:TN, 0:NT * NX], [(tri[:, :], picks)])
            product(bank[3][0:TN, NT * NX:2 * NT * NX], [(ones[0:TN, 0:TN], picks)]).then_inc(s["ranked"], 1)
            pe.wait_ge(s["steps"], 1)
            pe.wait_ge(s["moe"], 32)
            for k in ("up", "htp", "down"):
                pe.sem_inc(s[k], 2)

            def turn_x(st, u, n):
                hold(pe, x_arr[u], 16 * n + 16)
                hold(pe, s["xtc"], st + 1)
                for c in range(KC):
                    ins = pe.transpose(bank[u][:, c * 128:(c + 1) * 128], x_in[:, u, c * 128:(c + 1) * 128], ident[:, :])
                ins.then_inc(s["xtp"], 1)

            def up(st, u, n):
                hold(pe, s["xtc"], st + 3)
                hold(pe, s["hb"], st + 1)
                e = step_expert(pe, st)
                product(bank[2 + u][:, 0:D], [(x_T[:, u, c * 128:(c + 1) * 128], mw1_s[:, ds(e, 1), c, :].rearrange("p e n -> p (e n)"))
                                              for c in range(KC)]).then_inc(s["up"], 1)

            def turn_h(st, u, n):
                hold(pe, s["hg"], st + 3)
                hold(pe, s["htc"], st + 1)
                for c in range(KC):
                    ins = pe.transpose(bank[4 + u][:, c * 128:(c + 1) * 128], h_g[:, u, c * 128:(c + 1) * 128], ident[:, :])
                ins.then_inc(s["htp"], 1)

            def down(st, u, n):
                hold(pe, s["htc"], st + 3)
                hold(pe, s["yb"], st + 1)
                e = step_expert(pe, st)
                product(bank[6 + u][:, 0:D], [(h_T[:, u, c * 128:(c + 1) * 128], mw2_s[:, ds(e, 1), c, :].rearrange("p e n -> p (e n)"))
                                              for c in range(KC)]).then_inc(s["down"], 1)

            expert_steps(pe, [(2, turn_x), (1, up), (0, turn_h), (-1, down)])


_INS = {"x": "x", "conv": "L0_gnn_conv_weights", "attn_l": "L0_gnn_attn_l", "attn_r": "L0_gnn_attn_r",
        "h_bias": "L0_gnn_h_bias", "Wq": "L0_mix_Wq", "Wk": "L0_mix_Wk", "Wv": "L0_mix_Wv", "Wm": "L0_mix_Wm",
        "W1": "L0_mix_W1", "W2": "L0_mix_W2", "g1": "L0_mix_g1", "b1": "L0_mix_b1", "g2": "L0_mix_g2",
        "b2": "L0_mix_b2", "router": "L0_ffn_router_w", "mw1": "L0_ffn_w1", "mb1": "L0_ffn_b1",
        "mw2": "L0_ffn_w2", "mb2": "L0_ffn_b2"}


def kernel(**inputs):
    import numpy as _np
    import concourse.bacc as _bacc
    from concourse import mybir as _mybir
    from concourse.bass_utils import run_bass_kernel_spmd as _run

    nc = _bacc.Bacc("TRN2", target_bir_lowering=False, num_devices=1)
    arrays = {name: _np.ascontiguousarray(inputs[key]) for name, key in _INS.items()}
    dst, src, typ = (_np.asarray(inputs[k]) for k in ("dst", "src", "edge_type_8"))
    pad = EP - E
    arrays["dst_ext"] = _np.concatenate([_np.full(1, -1, dst.dtype), dst, _np.full(pad, N, dst.dtype), _np.full(1, N + 1, dst.dtype)])
    arrays["src_pad"] = _np.concatenate([src, _np.zeros(pad, src.dtype)])
    arrays["type_pad"] = _np.concatenate([typ, _np.zeros(pad, typ.dtype)])
    args = {k: nc.dram_tensor(f"in_{k}", a.shape, _mybir.dt.from_np(a.dtype), kind="ExternalInput").ap() for k, a in arrays.items()}
    args["out"] = nc.dram_tensor("out_0", (N + 128, D), F32, kind="ExternalOutput").ap()
    for name, shape in (("feat_t", (N, RF)), ("l_t", (N, R * H)), ("r_t", (N, R * H)), ("rec_t", (EP, 2 + H)),
                        ("dst_t", (EP,)), ("run_t", (EP + N, R * H)),
                        ("xs_t", (NM * 128, XW))):
        args[name] = nc.dram_tensor(name, shape, F32).ap()
    build(nc, **args)
    r = _run(nc, [{f"in_{k}": a for k, a in arrays.items()}], core_ids=[0])
    return r.results[0]["out_0"][:N]
```
